# Optimizing a Trainium2 kernel written in Bass

```python
import numpy as np
import jax
import jax.numpy as jnp

def _softmax(x, axis=-1):
    return jax.nn.softmax(x, axis=axis)

def _gelu(x):
    return jax.nn.gelu(x, approximate=True)

def _silu(x):
    return jax.nn.silu(x)

def _sigmoid(x):
    return jax.nn.sigmoid(x)

def _layernorm(x, axis=-1, eps=1e-05):
    m = jnp.mean(x, axis=axis, keepdims=True)
    v = jnp.var(x, axis=axis, keepdims=True)
    return (x - m) / jnp.sqrt(v + eps)

def _scatter_add(tgt, idx, src, axis=0):
    return tgt.at[idx].add(src)

def _segment_sum(src, seg, n):
    return jax.ops.segment_sum(src, seg, n)
kernel_name = 'mk_gnn_preln_d4_gnn_r32_7d69ca'

def setup_inputs(seed: int=0):
    np.random.seed(seed)
    _w = jnp.asarray

    def _rec_inputs():
        import jax
        import jax.numpy as jnp
        _gk = jax.random.key(seed)
        x = -0.0003713 + 1 * jax.random.normal(jax.random.fold_in(_gk, 1), (3125, 128), jnp.float32)
        src = jax.random.randint(jax.random.fold_in(_gk, 2), (100000,), 0, 3125, jnp.int32)
        dst = jax.random.randint(jax.random.fold_in(_gk, 3), (100000,), 0, 3125, jnp.int32)
        _o = jnp.argsort(dst, stable=True)
        src = src[_o]
        dst = dst[_o]
        edge_attr_16 = 0.000254156 + 0.999948 * jax.random.normal(jax.random.fold_in(_gk, 12), (100000, 16), jnp.float32)
        return (x, src, dst, edge_attr_16)
    x, src, dst, edge_attr_16 = _rec_inputs()

    def _L0_gnn_setup():
        import jax, jax.numpy as jnp
        import numpy as np
        N = 3125
        E = 50000
        IN_DIM = 128
        OUT_DIM = 128
        NEG_SLOPE = 0.01
        key = jax.random.key(seed)
        k1, k2, k3, k4, k5, k6 = jax.random.split(key, 6)
        feat = jax.random.normal(k1, (N, IN_DIM), dtype=jnp.float32)
        biclique_mask = jax.random.uniform(k2, (IN_DIM,), dtype=jnp.float32)
        W = jax.random.normal(k3, (OUT_DIM, IN_DIM), dtype=jnp.float32) * 0.05
        attn = jax.random.normal(k4, (OUT_DIM,), dtype=jnp.float32) * 0.1
        src = jax.random.randint(k5, (E,), 0, N, dtype=jnp.int32)
        dst = jax.random.randint(k6, (E,), 0, N, dtype=jnp.int32)
        return {'feat': feat, 'biclique_mask': biclique_mask, 'W': W, 'attn': attn, 'src': src, 'dst': dst}
    _L0_gnn_all = _L0_gnn_setup()
    _L0_gnn_in = {k: v for k, v in _L0_gnn_all.items() if k in ('biclique_mask', 'W', 'attn')}
    del _L0_gnn_all

    def _L1_gnn_setup():
        import jax, jax.numpy as jnp
        import numpy as np
        N, IN, OUT, H, ED, E = (50000, 128, 128, 3, 16, 25000)
        NEG_SLOPE = 0.2
        LN_EPS = 1e-05

        def gat_block(x, edge_index, edge_attr, W, W_edge, att_src, att_dst, att_edge, gat_bias, lin_W, lin_b, ln_g, ln_b):
            row, col = (edge_index[0], edge_index[1])
            n = x.shape[0]
            deg = jax.ops.segment_sum(jnp.ones((edge_attr.shape[0],), x.dtype), col, num_segments=n)
            loop_attr = jax.ops.segment_sum(edge_attr, col, num_segments=n) / jnp.maximum(deg, 1.0)[:, None]
            loop = jnp.arange(n, dtype=row.dtype)
            row2 = jnp.concatenate([row, loop])
            col2 = jnp.concatenate([col, loop])
            ea2 = jnp.concatenate([edge_attr, loop_attr], axis=0)
            xp = (x @ W).reshape(n, H, OUT)
            a_src = jnp.einsum('nhc,hc->nh', xp, att_src)
            a_dst = jnp.einsum('nhc,hc->nh', xp, att_dst)
            ep = (ea2 @ W_edge).reshape(-1, H, OUT)
            a_edge = jnp.einsum('ehc,hc->eh', ep, att_edge)
            alpha = a_src[row2] + a_dst[col2] + a_edge
            alpha = jnp.where(alpha >= 0, alpha, NEG_SLOPE * alpha)
            m = jax.ops.segment_max(alpha, col2, num_segments=n)
            ex = jnp.exp(alpha - m[col2])
            denom = jax.ops.segment_sum(ex, col2, num_segments=n)
            attn = ex / denom[col2]
            msg = attn[:, :, None] * xp[row2]
            agg = jax.ops.segment_sum(msg, col2, num_segments=n)
            x_gat = agg.reshape(n, H * OUT) + gat_bias
            y = x_gat @ lin_W + lin_b
            h = x + y
            mu = h.mean(-1, keepdims=True)
            var = ((h - mu) ** 2).mean(-1, keepdims=True)
            return (h - mu) * jax.lax.rsqrt(var + LN_EPS) * ln_g + ln_b
        key = jax.random.key(seed)
        ks = jax.random.split(key, 12)
        s = lambda k, shape, fan: jax.random.normal(k, shape, jnp.float32) / np.sqrt(fan)
        return {'x': jax.random.normal(ks[0], (N, IN), jnp.float32), 'edge_index': jax.random.randint(ks[1], (2, E), 0, N, jnp.int64), 'edge_attr': jax.random.normal(ks[2], (E, ED), jnp.float32), 'W': s(ks[3], (IN, H * OUT), IN), 'W_edge': s(ks[4], (ED, H * OUT), ED), 'att_src': s(ks[5], (H, OUT), OUT), 'att_dst': s(ks[6], (H, OUT), OUT), 'att_edge': s(ks[7], (H, OUT), OUT), 'gat_bias': jnp.zeros((H * OUT,), jnp.float32), 'lin_W': s(ks[8], (H * OUT, OUT), H * OUT), 'lin_b': jnp.zeros((OUT,), jnp.float32), 'ln_g': jnp.ones((OUT,), jnp.float32), 'ln_b': jnp.zeros((OUT,), jnp.float32)}
    _L1_gnn_all = _L1_gnn_setup()
    _L1_gnn_in = {k: v for k, v in _L1_gnn_all.items() if k in ('W', 'W_edge', 'att_src', 'att_dst', 'att_edge', 'gat_bias', 'lin_W', 'lin_b', 'ln_g', 'ln_b')}
    del _L1_gnn_all

    def _L2_gnn_setup():
        import jax, jax.numpy as jnp
        import numpy as np
        N_NODES = 50000
        key = jax.random.key(seed)
        ks = jax.random.split(key, 4)
        x = jax.random.normal(ks[0], (N_NODES, 128), dtype=jnp.float32)
        edge_index = jax.random.randint(ks[1], (2, 25000), 0, N_NODES, dtype=jnp.int64)
        W = jax.random.normal(ks[2], (8, 128, 128), dtype=jnp.float32) * (1.0 / np.sqrt(128))
        b = jnp.zeros((8, 128), dtype=jnp.float32)
        W_dict = jax.random.normal(ks[3], (128, 8), dtype=jnp.float32) * (1.0 / np.sqrt(128))
        b_dict = jnp.zeros((8,), dtype=jnp.float32)
        return {'x': x, 'edge_index': edge_index, 'W': W, 'b': b, 'W_dict': W_dict, 'b_dict': b_dict}
    _L2_gnn_all = _L2_gnn_setup()
    _L2_gnn_in = {k: v for k, v in _L2_gnn_all.items() if k in ('W', 'b', 'W_dict', 'b_dict')}
    del _L2_gnn_all

    def _L3_gnn_setup():
        import jax, jax.numpy as jnp
        import numpy as np
        N_NODES = 3125
        N_EDGES = 50000
        IN_F = 128
        H = 8
        F = 16
        NEG_SLOPE = 0.2
        EPS = 1e-16
        key = jax.random.key(seed)
        k1, k2, k3, k4, k5, k6 = jax.random.split(key, 6)
        x = jax.random.normal(k1, (N_NODES, IN_F), dtype=jnp.float32)
        edge_index = jax.random.randint(k2, (2, N_EDGES), 0, N_NODES, dtype=jnp.int64)
        W_proj = jax.random.normal(k3, (IN_F, H * F), dtype=jnp.float32) * (1.0 / np.sqrt(IN_F))
        W_skip = jax.random.normal(k4, (IN_F, H * F), dtype=jnp.float32) * (1.0 / np.sqrt(IN_F))
        a_src = jax.random.normal(k5, (1, H, F), dtype=jnp.float32) * 0.1
        a_tgt = jax.random.normal(k6, (1, H, F), dtype=jnp.float32) * 0.1
        return {'x': x, 'edge_index': edge_index, 'W_proj': W_proj, 'W_skip': W_skip, 'a_src': a_src, 'a_tgt': a_tgt}
    _L3_gnn_all = _L3_gnn_setup()
    _L3_gnn_in = {k: v for k, v in _L3_gnn_all.items() if k in ('W_proj', 'W_skip', 'a_src', 'a_tgt')}
    del _L3_gnn_all
    return {'x': x, 'src': src, 'dst': dst, 'edge_attr_16': edge_attr_16, 'L0_gnn_biclique_mask': _L0_gnn_in['biclique_mask'], 'L0_gnn_W': _L0_gnn_in['W'], 'L0_gnn_attn': _L0_gnn_in['attn'], 'L1_gnn_W': _L1_gnn_in['W'], 'L1_gnn_W_edge': _L1_gnn_in['W_edge'], 'L1_gnn_att_src': _L1_gnn_in['att_src'], 'L1_gnn_att_dst': _L1_gnn_in['att_dst'], 'L1_gnn_att_edge': _L1_gnn_in['att_edge'], 'L1_gnn_gat_bias': _L1_gnn_in['gat_bias'], 'L1_gnn_lin_W': _L1_gnn_in['lin_W'], 'L1_gnn_lin_b': _L1_gnn_in['lin_b'], 'L1_gnn_ln_g': _L1_gnn_in['ln_g'], 'L1_gnn_ln_b': _L1_gnn_in['ln_b'], 'L2_gnn_W': _L2_gnn_in['W'], 'L2_gnn_b': _L2_gnn_in['b'], 'L2_gnn_W_dict': _L2_gnn_in['W_dict'], 'L2_gnn_b_dict': _L2_gnn_in['b_dict'], 'L3_gnn_W_proj': _L3_gnn_in['W_proj'], 'L3_gnn_W_skip': _L3_gnn_in['W_skip'], 'L3_gnn_a_src': _L3_gnn_in['a_src'], 'L3_gnn_a_tgt': _L3_gnn_in['a_tgt']}

def reference(x, src, dst, edge_attr_16, L0_gnn_biclique_mask, L0_gnn_W, L0_gnn_attn, L1_gnn_W, L1_gnn_W_edge, L1_gnn_att_src, L1_gnn_att_dst, L1_gnn_att_edge, L1_gnn_gat_bias, L1_gnn_lin_W, L1_gnn_lin_b, L1_gnn_ln_g, L1_gnn_ln_b, L2_gnn_W, L2_gnn_b, L2_gnn_W_dict, L2_gnn_b_dict, L3_gnn_W_proj, L3_gnn_W_skip, L3_gnn_a_src, L3_gnn_a_tgt):
    import jax
    import jax.numpy as jnp

    def _L0_gnn_ref(feat, biclique_mask, W, attn, src, dst):
        import jax, jax.numpy as jnp
        import numpy as np
        N = 3125
        E = 50000
        IN_DIM = 128
        OUT_DIM = 128
        NEG_SLOPE = 0.01
        h = feat * biclique_mask[None, :] @ W.T
        s = jax.nn.leaky_relu(h @ attn, negative_slope=NEG_SLOPE)
        score = s[src]
        seg_max = jax.ops.segment_max(score, dst, num_segments=N)
        seg_max = jnp.where(jnp.isfinite(seg_max), seg_max, 0.0)
        ex = jnp.exp(score - seg_max[dst])
        denom = jax.ops.segment_sum(ex, dst, num_segments=N)
        a = ex / denom[dst]
        m = h[src] * a[:, None]
        h_new = jax.ops.segment_sum(m, dst, num_segments=N)
        return jax.nn.relu(h_new)

    def _L1_gnn_ref(x, edge_index, edge_attr, W, W_edge, att_src, att_dst, att_edge, gat_bias, lin_W, lin_b, ln_g, ln_b):
        import jax, jax.numpy as jnp
        import numpy as np
        N, IN, OUT, H, ED, E = (50000, 128, 128, 3, 16, 25000)
        NEG_SLOPE = 0.2
        LN_EPS = 1e-05

        def gat_block(x, edge_index, edge_attr, W, W_edge, att_src, att_dst, att_edge, gat_bias, lin_W, lin_b, ln_g, ln_b):
            row, col = (edge_index[0], edge_index[1])
            n = x.shape[0]
            deg = jax.ops.segment_sum(jnp.ones((edge_attr.shape[0],), x.dtype), col, num_segments=n)
            loop_attr = jax.ops.segment_sum(edge_attr, col, num_segments=n) / jnp.maximum(deg, 1.0)[:, None]
            loop = jnp.arange(n, dtype=row.dtype)
            row2 = jnp.concatenate([row, loop])
            col2 = jnp.concatenate([col, loop])
            ea2 = jnp.concatenate([edge_attr, loop_attr], axis=0)
            xp = (x @ W).reshape(n, H, OUT)
            a_src = jnp.einsum('nhc,hc->nh', xp, att_src)
            a_dst = jnp.einsum('nhc,hc->nh', xp, att_dst)
            ep = (ea2 @ W_edge).reshape(-1, H, OUT)
            a_edge = jnp.einsum('ehc,hc->eh', ep, att_edge)
            alpha = a_src[row2] + a_dst[col2] + a_edge
            alpha = jnp.where(alpha >= 0, alpha, NEG_SLOPE * alpha)
            m = jax.ops.segment_max(alpha, col2, num_segments=n)
            ex = jnp.exp(alpha - m[col2])
            denom = jax.ops.segment_sum(ex, col2, num_segments=n)
            attn = ex / denom[col2]
            msg = attn[:, :, None] * xp[row2]
            agg = jax.ops.segment_sum(msg, col2, num_segments=n)
            x_gat = agg.reshape(n, H * OUT) + gat_bias
            y = x_gat @ lin_W + lin_b
            h = x + y
            mu = h.mean(-1, keepdims=True)
            var = ((h - mu) ** 2).mean(-1, keepdims=True)
            return (h - mu) * jax.lax.rsqrt(var + LN_EPS) * ln_g + ln_b
        return gat_block(x, edge_index, edge_attr, W, W_edge, att_src, att_dst, att_edge, gat_bias, lin_W, lin_b, ln_g, ln_b)

    def _L2_gnn_ref(x, edge_index, W, b, W_dict, b_dict):
        import jax, jax.numpy as jnp
        import numpy as np
        N_NODES = 50000
        N = x.shape[0]
        K = W.shape[0]
        num_atoms = W_dict.shape[1]
        loop = jnp.arange(N, dtype=edge_index.dtype)
        src = jnp.concatenate([edge_index[0], loop])
        dst = jnp.concatenate([edge_index[1], loop])
        deg = jax.ops.segment_sum(jnp.ones_like(dst, dtype=x.dtype), dst, num_segments=N)
        dis = jnp.where(deg > 0, jax.lax.rsqrt(jnp.maximum(deg, 1.0)), 0.0)
        norm = (dis[src] * dis[dst])[:, None]
        coeff = jax.nn.softmax(x @ W_dict + b_dict, axis=-1)
        total = jnp.zeros((N, W.shape[2]), dtype=x.dtype)
        for k in range(K):
            h = x @ W[k]
            agg = jax.ops.segment_sum(h[src] * norm, dst, num_segments=N) + b[k]
            feat = jax.nn.relu(agg)
            total = total + feat * coeff[:, k % num_atoms, None]
        return total

    def _L3_gnn_ref(x, edge_index, W_proj, W_skip, a_src, a_tgt):
        import jax, jax.numpy as jnp
        import numpy as np
        N_NODES = 3125
        N_EDGES = 50000
        IN_F = 128
        H = 8
        F = 16
        NEG_SLOPE = 0.2
        EPS = 1e-16
        N = x.shape[0]
        p = (x @ W_proj).reshape(N, H, F)
        scores_src = jnp.sum(p * a_src, axis=-1)
        scores_tgt = jnp.sum(p * a_tgt, axis=-1)
        src = edge_index[0]
        tgt = edge_index[1]
        s = jax.nn.leaky_relu(scores_src[src] + scores_tgt[tgt], negative_slope=NEG_SLOPE)
        e = jnp.exp(s - jnp.max(s))
        denom = jax.ops.segment_sum(e, tgt, num_segments=N)[tgt]
        att = e / (denom + EPS)
        msg = p[src] * att[:, :, None]
        out = jax.ops.segment_sum(msg, tgt, num_segments=N)
        out = out + (x @ W_skip).reshape(N, H, F)
        out = out.reshape(N, H * F)
        return jax.nn.elu(out)
    edge_index = jnp.stack([src, dst])
    h = jnp.maximum(_layernorm(x, axis=-1), 0.0)
    x = x + _L0_gnn_ref(h, L0_gnn_biclique_mask, L0_gnn_W, L0_gnn_attn, src, dst)
    h = jnp.maximum(_layernorm(x, axis=-1), 0.0)
    x = x + _L1_gnn_ref(h, edge_index, edge_attr_16, L1_gnn_W, L1_gnn_W_edge, L1_gnn_att_src, L1_gnn_att_dst, L1_gnn_att_edge, L1_gnn_gat_bias, L1_gnn_lin_W, L1_gnn_lin_b, L1_gnn_ln_g, L1_gnn_ln_b)
    h = jnp.maximum(_layernorm(x, axis=-1), 0.0)
    x = x + _L2_gnn_ref(h, edge_index, L2_gnn_W, L2_gnn_b, L2_gnn_W_dict, L2_gnn_b_dict)
    h = jnp.maximum(_layernorm(x, axis=-1), 0.0)
    x = x + _L3_gnn_ref(h, edge_index, L3_gnn_W_proj, L3_gnn_W_skip, L3_gnn_a_src, L3_gnn_a_tgt)
    return x

_drawn_inputs = setup_inputs


def setup_inputs(seed=0):
    import zlib

    import numpy as np

    out = dict(_drawn_inputs(seed))
    spreads = {'L1_gnn_gat_bias': (0.0, 0.1),
     'L1_gnn_lin_b': (0.0, 0.1),
     'L1_gnn_ln_g': (1.0, 0.2),
     'L1_gnn_ln_b': (0.0, 0.1),
     'L2_gnn_b': (0.0, 0.558),
     'L2_gnn_b_dict': (0.0, 0.8)}
    factors = {'L0_gnn_attn': 8.0, 'L1_gnn_att_dst': 3.134, 'L3_gnn_a_src': 3.554, 'L3_gnn_a_tgt': 8.0}
    for name, (base, spread) in spreads.items():
        noise = np.random.default_rng([zlib.crc32(name.encode()), seed]).standard_normal(out[name].shape)
        drawn = base * np.exp(spread * noise) if base else spread * noise
        out[name] = jnp.asarray(drawn.astype(out[name].dtype))
    for name, factor in factors.items():
        out[name] = (out[name] * factor).astype(out[name].dtype)
    return out
```

```python
from contextlib import ExitStack

import concourse.bass as bass
from concourse import mybir

F32 = mybir.dt.float32
BF16 = mybir.dt.bfloat16
I32 = mybir.dt.int32
ALU = mybir.AluOpType
ACT = mybir.ActivationFunctionType
AX = mybir.AxisListType

P = 128
N = 3125
E = 100000
D = 128
NB = -(-N // P)
NP = NB * P
TAIL = N - (NB - 1) * P
EC = -(-E // P) + 2
EC = 16 * (-(-E // (16 * P)))
EP = EC * P
PAD = EP - E
PAD_DST = NP
KW = 8
EA = 16
H1 = 3
H3 = 8
C3 = D // H3
K2 = 8
GROUP = 2
BODY = 32
HAND = 4
DEPTH = 2
TILES = -(-E // P)
GROUPS_NEEDED = (TILES + NB - 1 + NB * (GROUP - 1)) // GROUP
STEPS = BODY * (-(-GROUPS_NEEDED * GROUP // BODY))
GROUPS = STEPS // GROUP
NCH = 8
CH = STEPS // NCH
ACCW = H1 * D + 2 * H1
GC = 16
BIG = 1.0e37
LN_EPS = 1e-5
assert EC % GC == 0 and CH <= P and STEPS == NCH * CH and BODY % (HAND * DEPTH) == 0


def build_gnn(nc, x, src, dst, edge_attr, L0_mask, L0_W, L0_attn, L1_W, L1_We, L1_as, L1_ad, L1_ae,
              L1_gb, L1_lW, L1_lb, L1_g, L1_b, L2_W, L2_b, L2_Wd, L2_bd, L3_Wp, L3_Ws, L3_as, L3_at, out):
    ctx = ExitStack()
    with ctx:
        def sb(name, shape, dt=F32):
            return ctx.enter_context(nc.sbuf_tensor(name, shape, dt))

        layer_sems = []

        def sem(name):
            layer_sems.append(nc.alloc_semaphore(name))
            return layer_sems[-1]

        def end_layer():
            nc.clear_and_free_semaphores(layer_sems)
            nc.all_engine_barrier()
            layer_sems.clear()

        def dram(name, shape, dt=F32):
            return nc.dram_tensor(name, shape, dt).ap()

        src_flat = dram("src_flat", (EP // P, P), I32)
        dst_flat = dram("dst_flat", (EP // P, P), I32)
        dst_ext = dram("dst_ext", (EP + 2,), I32)
        lo_flat = dram("lo_flat", (EC * P,), BF16)
        row_table = dram("row_table", (NP, D))
        edge_rows = dram("edge_rows", (EP // P, P * KW))
        seeds = dram("seeds", (EP + NP, KW))
        seeds_edges = seeds[0:EP, :]

        xs = sb("xs", [P, NB, D])
        hs = sb("hs", [P, NB, D])
        A1 = sb("A1", [P, NB * ACCW])
        A2 = sb("A2", [P, EC * KW])
        A3 = sb("A3", [P, STEPS * KW])
        a_edge = sb("a_edge", [P, EC, H1])
        gath = sb("gath", [P, BODY, D])
        onehot = sb("onehot", [P, HAND * DEPTH, P])
        weighted = sb("weighted", [P, HAND * DEPTH, ACCW])
        idx_step = sb("idx_step", [P, STEPS + BODY], I32)
        idx_ring = sb("idx_ring", [P, 2, BODY // 2], I32)
        dst_step = sb("dst_step", [P, STEPS + HAND])
        hi_b = sb("hi_b", [P, EC])
        keep_f = sb("keep_f", [P, EC])
        pen_f = sb("pen_f", [P, EC])
        pen_b = sb("pen_b", [P, EC])
        scan_tmp = sb("scan_tmp", [P, EC])
        iota_row = sb("iota_row", [P, P])
        iota_p = sb("iota_p", [P, 1])
        iota_hi = sb("iota_hi", [P, NB])
        ident = sb("ident", [P, P])
        tri = sb("tri", [P, P])
        ones = sb("ones", [P, P])
        carry_row = sb("carry_row", [KW, 6, P + 1])
        carry_col = sb("carry_col", [P, 4, KW])
        blk_reg = sb("blk_reg", [1, GROUPS], I32)
        deg = sb("deg", [P, NB])
        seed_idx = sb("seed_idx", [P, NB], I32)
        small = sb("small", [P, 16, NB])
        scal = sb("scal", [P, 2 * KW, NB])
        split = sb("split", [P, 3, KW, NB], BF16)
        wbuf = sb("wbuf", [P, 3 * 384])
        wnat = sb("wnat", [P, 384])
        bias_row = sb("bias_row", [P, D])
        ps = ctx.enter_context(nc.psum_tensor("ps", [P, 8, 512], F32))

        seed_vals = A2[:, 0:NB * KW].rearrange("p (b k) -> p b k", k=KW)
        SE = A2[:, :].rearrange("p (c k) -> p c k", k=KW)
        DB = A3[:, 0:EC * KW].rearrange("p (c k) -> p c k", k=KW)
        WS = A3[:, :].rearrange("p (s k) -> p s k", k=KW)
        tmp = A1[:, 0:NP].rearrange("p (b f) -> p b f", f=D)
        hT = A1[:, NP:2 * NP].rearrange("p (b f) -> p b f", f=D)
        hW = A1[:, 2 * NP:3 * NP].rearrange("p (b f) -> p b f", f=D)
        table_view = row_table.rearrange("(b p) f -> p b f", p=P)

        dve_chain = ctx.enter_context(nc.semaphore("dve_chain"))
        dve_count = [0]

        def link(dve, ins):
            dve_count[0] += 1
            ins.then_inc(dve_chain, 1)
            dve.wait_ge(dve_chain, dve_count[0])

        loaded = sem("loaded")
        pads_set = sem("pads_set")
        iota_set = sem("iota_set")
        pad_i = sb("pad_i", [1, 3 * PAD + 4], I32)
        with nc.Block() as block:
            @block.sync
            def _(sp):
                sp.dma_start(src_flat.rearrange("a b -> (a b)")[0:E].unsqueeze(0), src.unsqueeze(0)).then_inc(loaded, 16)
                sp.dma_start(dst_flat.rearrange("a b -> (a b)")[0:E].unsqueeze(0), dst.unsqueeze(0)).then_inc(loaded, 16)
                sp.dma_start(dst_ext[1:E + 1].unsqueeze(0), dst.unsqueeze(0)).then_inc(loaded, 16)
                sp.dma_start(xs[:, 0:NB - 1, :], x[0:(NB - 1) * P, :].rearrange("(b p) f -> p b f", p=P)).then_inc(loaded, 16)
                sp.wait_ge(pads_set, 5)
                sp.dma_start(xs[0:TAIL, NB - 1, :], x[(NB - 1) * P:N, :]).then_inc(loaded, 16)
                sp.dma_start(src_flat.rearrange("a b -> (a b)")[E:EP].unsqueeze(0), pad_i[:, 0:PAD]).then_inc(loaded, 16)
                sp.dma_start(dst_flat.rearrange("a b -> (a b)")[E:EP].unsqueeze(0), pad_i[:, PAD:2 * PAD]).then_inc(loaded, 16)
                sp.dma_start(dst_ext[E + 1:EP + 2].unsqueeze(0), pad_i[:, PAD:2 * PAD + 1]).then_inc(loaded, 16)
                sp.dma_start(dst_ext[0:1].unsqueeze(0), pad_i[:, 2 * PAD + 2:2 * PAD + 3]).then_inc(loaded, 16)
                sp.dma_start(seeds.rearrange("(p a) k -> p (a k)", p=P), A3[:, 0:(EP + NP) * KW // P]).then_inc(loaded, 16)
                sp.wait_ge(loaded, 10 * 16)

            @block.vector
            def _(dve):
                dve.memset(pad_i[:, 0:PAD], 0).then_inc(pads_set, 1)
                dve.memset(pad_i[:, PAD:2 * PAD + 2], PAD_DST).then_inc(pads_set, 1)
                dve.memset(pad_i[:, 2 * PAD + 2:2 * PAD + 4], -1).then_inc(pads_set, 1)
                dve.memset(xs[:, NB - 1, :], 0.0).then_inc(pads_set, 1)
                dve.memset(A3[:], 0.0).then_inc(pads_set, 1)
                dve.memset(ones[:], 1.0)
                dve.memset(idx_step[:, STEPS:STEPS + BODY], 0)
                dve.memset(dst_step[:, STEPS:STEPS + HAND], -1.0)
                dve.wait_ge(iota_set, 3)
                dve.tensor_scalar(ident[:], iota_row[:], iota_p[:, 0:1], None, ALU.is_equal)
                dve.tensor_scalar(tri[:], iota_row[:], iota_p[:, 0:1], None, ALU.is_gt)

            @block.gpsimd
            def _(pool):
                pool.iota(iota_row[:], [[1, P]], base=0, channel_multiplier=0,
                          allow_small_or_imprecise_dtypes=True).then_inc(iota_set, 1)
                pool.iota(iota_p[:], [[1, 1]], base=0, channel_multiplier=1,
                          allow_small_or_imprecise_dtypes=True).then_inc(iota_set, 1)
                pool.iota(iota_hi[:], [[1, NB]], base=0, channel_multiplier=0,
                          allow_small_or_imprecise_dtypes=True).then_inc(iota_set, 1)

        src_i = A1[:, 0:EC].bitcast(I32)
        prev_i = A1[:, EC:2 * EC].bitcast(I32)
        cur_i = A1[:, 2 * EC:3 * EC].bitcast(I32)
        next_i = A1[:, 3 * EC:4 * EC].bitcast(I32)
        lo_i = A1[:, 4 * EC:5 * EC].bitcast(I32)
        hi_i = A1[:, 5 * EC:6 * EC].bitcast(I32)
        lo_f = A1[:, 6 * EC:7 * EC]
        last_i = A2[0:1, 0:EC].bitcast(I32)
        last_f = A2[0:1, EC:2 * EC]
        before = A2[0:NB, 2 * EC:3 * EC]
        in_or_after = A2[0:NB, 3 * EC:3 * EC + GROUPS]
        by_step = A2[0:NB, 4 * EC:4 * EC + STEPS].rearrange("p (g i) -> p g i", i=GROUP)
        group_no = A2[:, 6 * EC:6 * EC + GROUPS]
        loT = A2[:, 7 * EC:7 * EC + 7 * P // 2].bitcast(BF16)
        plan = A3[:, 0:64]
        plan_i = A3[:, 64:128].bitcast(I32)
        step_no = A3[:, 128:128 + NCH]
        diff = A3[:, 160:160 + P]
        coef = A3[:, 320:322]
        tile_i = sb("tile_i", [P, NCH], I32)
        block_lo = sb("block_lo", [P, NCH])
        TQ = EC // 7

        plan_in = sem("plan_in")
        plan_iota = sem("plan_iota")
        plan_ready = sem("plan_ready")
        plan_done = sem("plan_done")
        lo_out = sem("lo_out")
        with nc.Block() as block:
            @block.sync
            def _(sp):
                sp.dma_start(src_i, src_flat.rearrange("a b -> (a b)").rearrange("(p c) -> p c", p=P)).then_inc(plan_in, 16)
                sp.dma_start(prev_i, dst_ext[0:EP].rearrange("(p c) -> p c", p=P)).then_inc(plan_in, 16)
                sp.dma_start(cur_i, dst_ext[1:EP + 1].rearrange("(p c) -> p c", p=P)).then_inc(plan_in, 16)
                sp.dma_start(next_i, dst_ext[2:EP + 2].rearrange("(p c) -> p c", p=P)).then_inc(plan_in, 16)
                with nc.allow_non_contiguous_dma("one element per tile"):
                    sp.dma_start(last_i.unsqueeze(2), dst_flat[:, P - 1:P].unsqueeze(0)).then_inc(plan_in, 16)
                sp.wait_ge(plan_ready, 6)
                for q in range(7):
                    sp.dma_start(lo_flat[q * TQ * P:(q + 1) * TQ * P].rearrange("(c p) -> c p", p=P),
                                 loT[0:TQ, q * P:(q + 1) * P]).then_inc(lo_out, 16)
                sp.wait_ge(lo_out, 7 * 16)

            @block.gpsimd
            def _(pool):
                pool.iota(group_no, [[1, GROUPS]], base=0, channel_multiplier=0,
                          allow_small_or_imprecise_dtypes=True).then_inc(plan_iota, 1)
                pool.iota(step_no, [[CH, NCH]], base=0, channel_multiplier=1,
                          allow_small_or_imprecise_dtypes=True).then_inc(plan_iota, 1)

            @block.tensor
            def _(pe):
                pe.wait_ge(plan_ready, 1)
                for q in range(2):
                    mm = pe.matmul(ps[0:NB, q, 0:EC // 2], ones[0:1, 0:NB], last_f[:, q * EC // 2:(q + 1) * EC // 2],
                                   start=True, stop=True)
                mm.then_inc(plan_done, 1)
                pe.wait_ge(plan_ready, 2)
                pe.matmul(ps[0:NB, 2, 0:1], tri[0:NB, 0:NB], plan[0:NB, 4:5], start=True, stop=True).then_inc(plan_done, 1)
                pe.wait_ge(plan_ready, 3)
                pe.matmul(ps[0:NB, 3, 0:1], diff[0:NB, 0:NB], plan[0:NB, 6:7], start=True, stop=True).then_inc(plan_done, 1)
                pe.wait_ge(plan_ready, 4)
                pe.matmul(ps[0:1, 4, 0:GROUPS], ones[0:NB, 0:1], in_or_after, start=True, stop=True)
                for c in range(NCH):
                    mm = pe.matmul(ps[0:CH, 5, 2 * c:2 * c + 2], by_step.rearrange("p g i -> p (g i)")[:, c * CH:(c + 1) * CH],
                                   coef[0:NB, :], start=True, stop=True)
                mm.then_inc(plan_done, 1)
                pe.wait_ge(plan_ready, 5)
                for q in range(7):
                    mm = pe.transpose(ps[0:TQ, 6 + q // 4, (q % 4) * P:(q % 4 + 1) * P], lo_f[:, q * TQ:(q + 1) * TQ], ident[:])
                mm.then_inc(plan_done, 1)

            @block.vector
            def _(dve):
                dve.wait_ge(plan_in, 5 * 16)
                dve.tensor_copy(last_f, last_i).then_inc(plan_ready, 1)
                dve.wait_ge(plan_done, 1)
                link(dve, dve.tensor_scalar(plan[:, 0:1], iota_p[:], float(P), None, ALU.mult))
                link(dve, dve.tensor_scalar(plan[:, 1:2], plan[:, 0:1], float(P), None, ALU.add))
                for k in range(2):
                    link(dve, dve.tensor_scalar(before.rearrange("p (q c) -> p q c", q=2), ps[0:NB, 0:2, 0:EC // 2],
                                                plan[0:NB, k:k + 1], None, ALU.is_lt))
                    link(dve, dve.tensor_reduce(plan[0:NB, 2 + k:3 + k], before, AX.X, ALU.add))
                link(dve, dve.tensor_tensor(plan[0:NB, 5:6], plan[0:NB, 3:4], plan[0:NB, 2:3], ALU.subtract))
                link(dve, dve.tensor_scalar(plan_i[0:NB, 0:1], plan[0:NB, 5:6], 2.0, None, ALU.add))
                link(dve, dve.tensor_scalar(plan_i[0:NB, 1:2], plan_i[0:NB, 0:1], 1, None, ALU.arith_shift_right))
                dve.tensor_copy(plan[0:NB, 4:5], plan_i[0:NB, 1:2]).then_inc(plan_ready, 1)
                dve.wait_ge(plan_done, 2)
                link(dve, dve.tensor_copy(plan[0:NB, 7:8], ps[0:NB, 2, 0:1]))
                link(dve, dve.scalar_tensor_tensor(out=plan[0:NB, 6:7], in0=plan[0:NB, 7:8], scalar=-float(GROUP),
                                                   in1=plan[0:NB, 2:3], op0=ALU.mult, op1=ALU.add))
                link(dve, dve.tensor_scalar(plan[:, 8:9], iota_p[:], 1.0, None, ALU.add))
                link(dve, dve.tensor_scalar(diff, iota_row[:], plan[:, 8:9], None, ALU.is_equal))
                dve.tensor_tensor(diff, ident[:], diff, ALU.subtract).then_inc(plan_ready, 1)
                dve.wait_ge(plan_done, 3)
                dve.wait_ge(plan_iota, 2)
                link(dve, dve.memset(coef[:, 0:1], 1.0))
                link(dve, dve.tensor_copy(coef[0:NB, 1:2], ps[0:NB, 3, 0:1]))
                link(dve, dve.tensor_scalar(in_or_after, group_no[0:NB, :], plan[0:NB, 7:8], None, ALU.is_ge))
                dve.tensor_copy(by_step, in_or_after.unsqueeze(2).broadcast_to([NB, GROUPS, GROUP])).then_inc(plan_ready, 1)
                link(dve, dve.tensor_scalar(hi_i, src_i, 7, None, ALU.arith_shift_right))
                link(dve, dve.tensor_scalar(lo_i, src_i, P - 1, None, ALU.bitwise_and))
                link(dve, dve.tensor_copy(hi_b[:], hi_i))
                dve.tensor_copy(lo_f, lo_i).then_inc(plan_ready, 1)
                dve.wait_ge(plan_done, 4)
                dve.tensor_scalar(blk_reg[:], ps[0:1, 4, 0:GROUPS], -1.0, None, ALU.add)
                counts = ps[0:CH, 5, 0:2 * NCH].rearrange("p (c two) -> p c two", two=2)
                dve.tensor_scalar(block_lo[0:CH, :], counts[:, :, 0], float(P), -float(P), ALU.mult, ALU.add)
                link(dve, dve.tensor_tensor(plan[0:CH, 16:16 + NCH], counts[:, :, 1], step_no[0:CH, :], ALU.add))
                dve.tensor_scalar(tile_i[0:CH, :], plan[0:CH, 16:16 + NCH], float(EP // P - 1), None, ALU.min)
                dve.wait_ge(plan_done, 5)
                for q in range(7):
                    last = dve.tensor_copy(loT[0:TQ, q * P:(q + 1) * P], ps[0:TQ, 6 + q // 4, (q % 4) * P:(q % 4 + 1) * P])
                last.then_inc(plan_ready, 1)
                dve.tensor_tensor(keep_f[:], cur_i, prev_i, ALU.is_equal)
                link(dve, dve.tensor_tensor(pen_b[:], cur_i, next_i, ALU.is_equal))
                dve.tensor_scalar(pen_f[:], keep_f[:], BIG, -BIG, ALU.mult, ALU.add)
                link(dve, dve.tensor_scalar(pen_b[:], pen_b[:], BIG, -BIG, ALU.mult, ALU.add))
                for k, v in enumerate((keep_f, pen_f, pen_b)):
                    link(dve, dve.tensor_reduce(scan_tmp[:, k:k + 1], v[:], AX.X, ALU.min))
                    link(dve, dve.tensor_copy(carry_col[:, k, :], scan_tmp[:, k:k + 1].broadcast_to([P, KW])))

        src_rows = A1[:, 0:NCH * P].bitcast(I32)
        dst_rows = A1[:, NCH * P:2 * NCH * P].bitcast(I32)
        src_rf = A1[:, 2 * NCH * P:3 * NCH * P]
        dst_rf = A1[:, 3 * NCH * P:4 * NCH * P]
        EQ = 14
        NQ = (EC * EA // P) // EQ
        ea_in = A2[:, 0:EQ * P]
        ea_T = A2[:, EQ * P:2 * EQ * P]
        we_prod = A2[:, 2 * EQ * P:2 * EQ * P + 3 * 384]
        step_rows_in = sem("step_rows_in")
        ea_loaded = sem("ea_loaded")
        rows_f = sem("rows_f")
        rows_turned = sem("rows_turned")
        rows_kept = sem("rows_kept")
        carry_turned = sem("carry_turned")
        ve_col = sb("ve_col", [P, 4])
        ve_diag = sb("ve_diag", [P, 8 * H1])
        ve_ready = sem("ve_ready")
        ve_placed = sem("ve_placed")
        ea_turned = sem("ea_turned")
        ea_kept = sem("ea_kept")
        ae_done = sem("ae_done")
        ae_kept = sem("ae_kept")
        ea_zero = sem("ea_zero")
        w_in = sem("w_in")
        EA_ROWS = E * EA // P
        PER = EC * EA // P
        FULL = EA_ROWS // PER
        REST = EA_ROWS - FULL * PER
        ea_view = edge_attr.rearrange("(r j) c -> r (j c)", j=8)
        ve_dram = dram("ve_dram", (EA, H1))
        with nc.Block() as block:
            @block.gpsimd
            def _(pool):
                for c in range(NCH):
                    pool.indirect_dma_start(src_rows[0:CH, c * P:(c + 1) * P], None, src_flat,
                                            bass.IndirectOffsetOnAxis(ap=tile_i[0:CH, c:c + 1], axis=0)).then_inc(step_rows_in, 16)
                    pool.indirect_dma_start(dst_rows[0:CH, c * P:(c + 1) * P], None, dst_flat,
                                            bass.IndirectOffsetOnAxis(ap=tile_i[0:CH, c:c + 1], axis=0)).then_inc(step_rows_in, 16)

            @block.sync
            def _(sp):
                sp.dma_start(wnat[0:EA, :], L1_We).then_inc(w_in, 16)
                sp.dma_start(wbuf[0:EA, 0:384], L1_ae.rearrange("h c -> (h c)").unsqueeze(0).broadcast_to([EA, 384])).then_inc(w_in, 16)
                sp.wait_ge(ve_ready, 2)
                sp.dma_start(ve_dram, ve_col[0:EA, 0:H1]).then_inc(ve_placed, 16)
                sp.wait_ge(ve_placed, 16)
                with nc.allow_non_contiguous_dma("eight small squares"):
                    for j in range(8):
                        sp.dma_start(ve_diag[j * EA:(j + 1) * EA, j * H1:(j + 1) * H1], ve_dram).then_inc(ve_placed, 16)
                sp.wait_ge(ea_zero, 1)
                for q in range(NQ):
                    if q:
                        sp.wait_ge(ea_turned, q)
                    sp.dma_start(ea_in[0:FULL, :], ea_view[0:FULL * PER, :].rearrange("(p t) w -> p (t w)", t=PER)[:, q * EQ * P:(q + 1) * EQ * P]).then_inc(ea_loaded, 16)
                    here = min(max(REST - q * EQ, 0), EQ)
                    if here:
                        sp.dma_start(ea_in[FULL:FULL + 1, 0:here * P],
                                     ea_view[FULL * PER + q * EQ:FULL * PER + q * EQ + here, :].rearrange("t w -> (t w)").unsqueeze(0)).then_inc(ea_loaded, 16)
                sp.wait_ge(ea_loaded, 16 * (NQ + -(-REST // EQ)))
                sp.wait_ge(ve_placed, 16 * 9)

            @block.tensor
            def _(pe):
                for k in range(3):
                    mm = pe.transpose(ps[0:KW, 0, k * P:(k + 1) * P], carry_col[:, k, :], ident[:])
                mm.then_inc(carry_turned, 1)
                for c in range(NCH):
                    pe.wait_ge(rows_f, c + 1)
                    if c >= 2:
                        pe.wait_ge(rows_kept, c - 1)
                    pe.transpose(ps[:, 1 + c % 2, 0:CH], src_rf[0:CH, c * P:(c + 1) * P], ident[0:CH, 0:CH])
                    pe.transpose(ps[:, 1 + c % 2, P:P + CH], dst_rf[0:CH, c * P:(c + 1) * P], ident[0:CH, 0:CH]).then_inc(rows_turned, 1)
                pe.wait_ge(ve_placed, 16 * 9)
                for q in range(NQ):
                    pe.wait_ge(ea_loaded, 16 * (q + 1 + min(q + 1, -(-REST // EQ))))
                    if q:
                        pe.wait_ge(ea_kept, q)
                    for t in range(EQ):
                        mm = pe.transpose(ps[:, 3 + t // 4, (t % 4) * P:(t % 4 + 1) * P], ea_in[:, t * P:(t + 1) * P], ident[:])
                    mm.then_inc(ea_turned, 1)
                    pe.wait_ge(ea_kept, q + 1)
                    if q:
                        pe.wait_ge(ae_kept, q)
                    for t in range(EQ):
                        mm = pe.matmul(ps[:, 7, t * 24:(t + 1) * 24], ea_T[:, t * P:(t + 1) * P], ve_diag[:], start=True, stop=True)
                    mm.then_inc(ae_done, 1)

            @block.scalar
            def _(act):
                for q in range(NQ):
                    act.wait_ge(ea_turned, q + 1)
                    if q:
                        act.wait_ge(ae_done, q)
                    act.copy(ea_T[:, 0:12 * P].rearrange("p (b c) -> p b c", c=512), ps[:, 3:6, :])
                    act.copy(ea_T[:, 12 * P:EQ * P], ps[:, 6, 0:2 * P]).then_inc(ea_kept, 1)
                    act.wait_ge(ae_done, q + 1)
                    act.copy(a_edge[:, q * EQ * 8:(q + 1) * EQ * 8, :].rearrange("p c h -> p (c h)"), ps[:, 7, 0:EQ * 24]).then_inc(ae_kept, 1)

            @block.vector
            def _(dve):
                dve.memset(ea_in, 0.0).then_inc(ea_zero, 1)
                dve.memset(ve_diag[:], 0.0).then_inc(ve_ready, 1)
                dve.wait_ge(w_in, 32)
                link(dve, dve.tensor_tensor(we_prod[0:EA, 0:384], wnat[0:EA, :], wbuf[0:EA, 0:384], ALU.mult))
                dve.tensor_reduce(ve_col[0:EA, 0:H1], we_prod[0:EA, 0:384].rearrange("p (h c) -> p h c", c=P), AX.X, ALU.add).then_inc(ve_ready, 1)
                dve.wait_ge(step_rows_in, 2 * NCH * 16)
                for c in range(NCH):
                    dve.tensor_copy(src_rf[0:CH, c * P:(c + 1) * P], src_rows[0:CH, c * P:(c + 1) * P])
                    dve.tensor_scalar(dst_rf[0:CH, c * P:(c + 1) * P], dst_rows[0:CH, c * P:(c + 1) * P],
                                      block_lo[0:CH, c:c + 1], None, ALU.subtract).then_inc(rows_f, 1)
                dve.wait_ge(carry_turned, 1)
                dve.tensor_copy(carry_row[:, 0:3, 0:P], ps[0:KW, 0, 0:3 * P].rearrange("k (a p) -> k a p", p=P))
                for c in range(NCH):
                    dve.wait_ge(rows_turned, c + 1)
                    dve.tensor_copy(idx_step[:, c * CH:(c + 1) * CH], ps[:, 1 + c % 2, 0:CH])
                    dve.tensor_copy(dst_step[:, c * CH:(c + 1) * CH], ps[:, 1 + c % 2, P:P + CH]).then_inc(rows_kept, 1)

        end_layer()
        def per_node(v):
            return v.unsqueeze(2).broadcast_to([P, NB, D])

        def per_feature(v):
            return v.unsqueeze(1).broadcast_to([P, NB, D])

        def standardise(dve, act_sync, of):
            to_act, from_act = act_sync
            mean, var, rec = small[:, 0, :], small[:, 1, :], small[:, 2, :]
            link(dve, dve.tensor_reduce(mean, of, AX.X, ALU.add))
            link(dve, dve.tensor_scalar(mean, mean, 1.0 / D, None, ALU.mult))
            link(dve, dve.tensor_tensor(hs[:], of, per_node(mean), ALU.subtract))
            link(dve, dve.tensor_tensor(tmp, hs[:], hs[:], ALU.mult))
            link(dve, dve.tensor_reduce(var, tmp, AX.X, ALU.add))
            dve.tensor_scalar(var, var, 1.0 / D, LN_EPS, ALU.mult, ALU.add).then_inc(to_act, 1)
            dve.wait_ge(from_act, 1)
            link(dve, dve.reciprocal(rec, var))
            link(dve, dve.tensor_tensor(hs[:], hs[:], per_node(rec), ALU.mult))

        def std_root(act, to_act, from_act):
            act.wait_ge(to_act, 1)
            act.activation(small[:, 1, :], small[:, 1, :], ACT.Sqrt).then_inc(from_act, 1)

        def turn_blocks(pe, source, ready, turned, kept, first=0):
            for b in range(NB):
                g = b // 4
                if b % 4 == 0:
                    pe.wait_ge(ready, first + 1)
                    if g >= 2:
                        pe.wait_ge(kept, g - 1)
                mm = pe.transpose(ps[:, g % 2, (b % 4) * P:(b % 4 + 1) * P], source[:, b, :], ident[:])
                if b % 4 == 3 or b == NB - 1:
                    mm.then_inc(turned, 1)

        def keep_blocks(act, target, turned, kept, scale=None):
            for g in range(-(-NB // 4)):
                n = min(4, NB - 4 * g)
                act.wait_ge(turned, g + 1)
                got = ps[:, g % 2, 0:n * P].rearrange("p (b f) -> p b f", f=P)
                act.activation(target[:, 4 * g:4 * g + n, :], got, ACT.Copy if scale is None else ACT.Identity,
                               scale=1.0 if scale is None else scale).then_inc(kept, 1)

        def gather_scalars(L, K):
            lo_in = [sem(f"L{L}_lo_in{i}") for i in range(2)]
            lo_hot_ready = sem(f"L{L}_lo_hot_ready")
            picked_ready = sem(f"L{L}_picked_ready")
            picked_used = sem(f"L{L}_picked_used")
            turn_summed = sem(f"L{L}_turn_summed")
            split_ready = sem(f"L{L}_split_ready")
            turn_started = sem(f"L{L}_turn_started")
            lo_bc = A1[:, 0:2 * GC * P // 2].bitcast(BF16).rearrange("p (i e) -> p i e", i=2)
            lo_hot = A1[:, 2048:2048 + 2 * GC * P // 2].bitcast(BF16).rearrange("p (i e) -> p i e", i=2)
            mask = A1[:, 4096:4096 + GC * NB].rearrange("p (c h) -> p c h", h=NB)
            prod = A1[:, 4608:4608 + GC * KW * NB].rearrange("p (c k h) -> p c k h", k=KW, h=NB)
            CPB = 2
            QC = 4
            NQ = GC // QC
            TURNS = EC // GC
            with nc.Block() as block:
                @block.sync
                def _(sp):
                    for i in range(2):
                        sp.dma_start(lo_bc[:, i, :], lo_flat[i * GC * P:(i + 1) * GC * P].unsqueeze(0).broadcast_to([P, GC * P])).then_inc(lo_in[i], 16)
                    with sp.Fori(0, (TURNS - 3) // 2) as t:
                        for i in range(2):
                            sp.wait_ge(lo_hot_ready, t * 2 + i + 1)
                            sp.dma_start(lo_bc[:, i, :], lo_flat[bass.ds((t * 2 + i + 2) * GC * P, GC * P)].unsqueeze(0).broadcast_to([P, GC * P])).then_inc(lo_in[i], 16)
                    sp.wait_ge(lo_hot_ready, TURNS - 2)
                    sp.dma_start(lo_bc[:, 0, :], lo_flat[(TURNS - 1) * GC * P:TURNS * GC * P].unsqueeze(0).broadcast_to([P, GC * P])).then_inc(lo_in[0], 16)
                    sp.wait_ge(lo_in[0], 16 * (TURNS // 2 + 1))
                    sp.wait_ge(lo_in[1], 16 * (TURNS // 2))

                @block.vector
                def _(dve):
                    rest = prod.rearrange("p c k h -> p (c k h)")[:, 0:K * NB].rearrange("p (k h) -> p k h", h=NB)
                    link(dve, dve.tensor_copy(split[:, 0, 0:K, :], scal[:, 0:K, :]))
                    link(dve, dve.tensor_tensor(rest, scal[:, 0:K, :], split[:, 0, 0:K, :], ALU.subtract))
                    link(dve, dve.tensor_copy(split[:, 1, 0:K, :], rest))
                    link(dve, dve.tensor_tensor(rest, rest, split[:, 1, 0:K, :], ALU.subtract))
                    dve.tensor_copy(split[:, 2, 0:K, :], rest).then_inc(split_ready, 1)

                    def hot(n, i):
                        dve.wait_ge(lo_in[i], n * 16 + 16)
                        dve.tensor_scalar(lo_hot[:, i, :], lo_bc[:, i, :], iota_p[:, 0:1], None, ALU.is_equal).then_inc(lo_hot_ready, 1)

                    def pick(t):
                        dve.tensor_tensor(mask, hi_b[:, bass.ds(t * GC, GC)].unsqueeze(2).broadcast_to([P, GC, NB]),
                                          iota_hi[:].unsqueeze(1).broadcast_to([P, GC, NB]), ALU.is_equal).then_inc(turn_started, 1)
                        dve.wait_ge(turn_started, t * 2 + 1)
                        for q in range(NQ):
                            dve.wait_ge(picked_ready, t * NQ + q + 1)
                            for b in range(QC // CPB):
                                c0 = q * QC + b * CPB
                                got = ps[:, (q % 2) * 2 + b, 0:CPB * K * NB].rearrange("p (c k h) -> p c k h", k=K, h=NB)
                                last = dve.tensor_tensor(prod[:, c0:c0 + CPB, 0:K, :], got,
                                                         mask[:, c0:c0 + CPB, :].unsqueeze(2).broadcast_to([P, CPB, K, NB]), ALU.mult)
                            last.then_inc(picked_used, 1)
                        dve.wait_ge(picked_used, t * NQ + NQ + 2)
                        dve.tensor_reduce(SE[:, bass.ds(t * GC, GC), 0:K], prod[:, :, 0:K, :], AX.X, ALU.add).then_inc(turn_started, 1)
                        dve.wait_ge(turn_started, t * 2 + 2)

                    dve.sem_inc(picked_used, 2)
                    hot(0, 0)
                    with dve.Fori(0, (TURNS - 1) // 2) as u:
                        for i in range(2):
                            hot(u + i, 1 - i)
                            pick(u * 2 + i)
                    pick(TURNS - 1)

                @block.tensor
                def _(pe):
                    pe.wait_ge(split_ready, 1)

                    def turn(t, i):
                        for q in range(NQ):
                            pe.wait_ge(picked_used, t * NQ + q + 1)
                            if q == 0:
                                pe.wait_ge(lo_hot_ready, t + 1)
                            for c in range(QC):
                                for s in range(3):
                                    mm = pe.matmul(ps[:, (q % 2) * 2 + c // CPB, (c % CPB) * K * NB:(c % CPB + 1) * K * NB],
                                                   lo_hot[:, i, (q * QC + c) * P:(q * QC + c + 1) * P],
                                                   split[:, s, 0:K, :].rearrange("p k h -> p (k h)"),
                                                   start=(s == 0), stop=(s == 2))
                            mm.then_inc(picked_ready, 1)

                    with pe.Fori(0, (TURNS - 1) // 2) as u:
                        for i in range(2):
                            turn(u * 2 + i, i)
                    turn(TURNS - 1, 0)

        def scans(L, jobs):
            ends_ready = sem(f"L{L}_ends_ready")
            ends_turned = sem(f"L{L}_ends_turned")
            starts_ready = sem(f"L{L}_starts_ready")
            starts_turned = sem(f"L{L}_starts_turned")

            def run(dve, k, job, out, initial):
                K, source, draft, target, factor, frow, op0, op1, neutral, rev = job
                way = slice(None, None, -1) if rev else slice(None)
                return dve.tensor_tensor_scan(out[:, way], factor[:][:, way], source(k)[:, way], initial, op0, op1)

            with nc.Block() as block:
                @block.vector
                def _(dve):
                    for n, job in enumerate(jobs):
                        K, source, draft, target, factor, frow, op0, op1, neutral, rev = job
                        for k in range(K):
                            link(dve, run(dve, k, job, draft(k), neutral))
                            end = draft(k)[:, 0:1] if rev else draft(k)[:, EC - 1:EC]
                            last = dve.tensor_copy(carry_col[:, n, k:k + 1], end)
                        last.then_inc(ends_ready, 1)
                    for n, job in enumerate(jobs):
                        K, source, draft, target, factor, frow, op0, op1, neutral, rev = job
                        dve.wait_ge(ends_turned, n + 1)
                        ends = carry_row[0:K, 3, 0:P]
                        link(dve, dve.tensor_copy(ends, ps[0:K, n, 0:P]))
                        if rev:
                            dve.memset(carry_row[0:K, 4 + n, P:P + 1], neutral)
                            link(dve, dve.tensor_tensor_scan(carry_row[0:K, 4 + n, 0:P][:, ::-1], carry_row[0:K, frow, 0:P][:, ::-1],
                                                             ends[:, ::-1], neutral, op0, op1))
                        else:
                            dve.memset(carry_row[0:K, 4 + n, 0:1], neutral)
                            link(dve, dve.tensor_tensor_scan(carry_row[0:K, 4 + n, 1:P + 1], carry_row[0:K, frow, 0:P],
                                                             ends, neutral, op0, op1))
                        dve.sem_inc(starts_ready, 1)
                    for n, job in enumerate(jobs):
                        K, source, draft, target, factor, frow, op0, op1, neutral, rev = job
                        dve.wait_ge(starts_turned, n + 1)
                        link(dve, dve.tensor_copy(carry_col[:, 2 + n, 0:K], ps[:, 2 + n, 0:K]))
                        for k in range(K):
                            link(dve, run(dve, k, job, target(k), carry_col[:, 2 + n, k:k + 1]))

                @block.tensor
                def _(pe):
                    for n, job in enumerate(jobs):
                        K = job[0]
                        pe.wait_ge(ends_ready, n + 1)
                        pe.transpose(ps[0:K, n, 0:P], carry_col[:, n, 0:K], ident[:]).then_inc(ends_turned, 1)
                    for n, job in enumerate(jobs):
                        K, rev = job[0], job[-1]
                        pe.wait_ge(starts_ready, n + 1)
                        starts = carry_row[0:K, 4 + n, 1:P + 1] if rev else carry_row[0:K, 4 + n, 0:P]
                        pe.transpose(ps[:, 2 + n, 0:K], starts, ident[0:K, 0:K]).then_inc(starts_turned, 1)

        def copy_down(L, K):
            scans(f"{L}c", [(K, lambda k: DB[:, :, k], lambda k: A1[:, k * EC:(k + 1) * EC], lambda k: DB[:, :, k],
                             keep_f, 0, ALU.mult, ALU.add, 0.0, False)])

        def segment_max(L, K):
            fw = lambda k: A1[:, k * EC:(k + 1) * EC]
            bw = lambda k: A1[:, (K + k) * EC:(K + k + 1) * EC]
            scans(f"{L}m", [(K, lambda k: SE[:, :, k], fw, fw, pen_f, 1, ALU.add, ALU.max, -BIG, False),
                            (K, lambda k: SE[:, :, k], bw, bw, pen_b, 2, ALU.add, ALU.max, -BIG, True)])
            forward = A1[:, 0:K * EC].rearrange("p (k c) -> p c k", k=K)
            backward = A1[:, K * EC:2 * K * EC].rearrange("p (k c) -> p c k", k=K)
            return forward, backward

        def to_steps(L, K):
            out_done = sem(f"L{L}_edge_rows_out")
            chunk_in = [sem(f"L{L}_chunk_in{c}") for c in range(NCH)]
            chunk_turned = sem(f"L{L}_chunk_turned")
            chunk_kept = sem(f"L{L}_chunk_kept")
            rows = A1[:, 0:NCH * P * KW].rearrange("p (c e k) -> p c e k", c=NCH, k=KW)
            with nc.Block() as block:
                @block.sync
                def _(sp):
                    sp.dma_start(edge_rows.rearrange("a b -> (a b)").rearrange("(p c) -> p c", p=P),
                                 SE.rearrange("p c k -> p (c k)")).then_inc(out_done, 16)
                    sp.wait_ge(out_done, 16)

                @block.gpsimd
                def _(pool):
                    pool.wait_ge(out_done, 16)
                    for c in range(NCH):
                        pool.indirect_dma_start(rows[0:CH, c, :, :].rearrange("p e k -> p (e k)"), None, edge_rows,
                                                bass.IndirectOffsetOnAxis(ap=tile_i[0:CH, c:c + 1], axis=0)).then_inc(chunk_in[c], 16)

                @block.tensor
                def _(pe):
                    for c in range(NCH):
                        pe.wait_ge(chunk_in[c], 16)
                        if c >= 2:
                            pe.wait_ge(chunk_kept, c - 1)
                        for k in range(K):
                            mm = pe.transpose(ps[:, (c % 2) * 2 + k // 4, (k % 4) * CH:(k % 4 + 1) * CH], rows[0:CH, c, :, k],
                                              ident[0:CH, 0:CH])
                        mm.then_inc(chunk_turned, 1)

                @block.vector
                def _(dve):
                    for c in range(NCH):
                        dve.wait_ge(chunk_turned, c + 1)
                        for g in range(-(-K // 4)):
                            n = min(4, K - 4 * g)
                            last = dve.tensor_copy(WS[:, c * CH:(c + 1) * CH, 4 * g:4 * g + n],
                                                   ps[:, (c % 2) * 2 + g, 0:n * CH].rearrange("p (k s) -> p s k", k=n))
                        last.then_inc(chunk_kept, 1)

        def row_pass(L, K, W, weight, ex0, ex1):
            rows_in = [sem(f"L{L}_rows_in{h}") for h in range(BODY // HAND)]
            idx_copied = sem(f"L{L}_idx_copied")
            rows_used = sem(f"L{L}_rows_used")
            hot_ready = sem(f"L{L}_hot_ready")
            multiplied = sem(f"L{L}_multiplied")
            flushed = sem(f"L{L}_flushed")
            pool_turns = sem(f"L{L}_pool_turns")
            act_turns = sem(f"L{L}_act_turns")
            acc = A1[:, 0:NB * W].rearrange("p (b w) -> p b w", w=W)
            HANDS = BODY // HAND
            HALF = BODY // 2
            GPH = HAND // GROUP
            nmul = {"none": 0, "act1": D, "act3": H1 * D, "dve8": D}[weight]
            with nc.Block() as block:
                @block.gpsimd
                def _(pool):
                    with pool.Fori(0, STEPS // BODY) as it:
                        for h in range(HANDS):
                            if h % (HANDS // 2) == 0:
                                pool.wait_ge(idx_copied, it * 2 + h // (HANDS // 2) + 1)
                                pool.sem_inc(pool_turns, 1)
                            if weight == "none":
                                pool.wait_ge(flushed, (it * HANDS + h + 1) * GPH)
                            else:
                                pool.wait_ge(rows_used, it * HANDS + h + 1)
                            pool.sem_inc(pool_turns, 1)
                            for j in range(HAND):
                                s = h * HAND + j
                                g = pool.indirect_dma_start(gath[:, s, :], None, row_table,
                                                            bass.IndirectOffsetOnAxis(ap=idx_ring[:, s // HALF, s % HALF:s % HALF + 1], axis=0))
                                g.then_inc(rows_in[h], 16)

                @block.scalar
                def _(act):
                    act.copy(idx_ring[:].rearrange("p a b -> p (a b)"), idx_step[:, 0:BODY]).then_inc(idx_copied, 2)
                    if weight in ("act1", "act3"):
                        act.sem_inc(rows_used, HANDS)
                    with act.Fori(0, STEPS // BODY) as it:
                        for h in range(HANDS):
                            if weight in ("act1", "act3"):
                                act.wait_ge(rows_in[h], it * (16 * HAND) + 16 * HAND)
                                act.sem_inc(act_turns, 1)
                                act.wait_ge(multiplied, it * HANDS + h + 1)
                                act.sem_inc(act_turns, 1)
                                slot = (h % DEPTH) * HAND
                                if ex1 > ex0:
                                    act.copy(weighted[:, slot:slot + HAND, nmul:nmul + ex1 - ex0],
                                             WS[:, bass.ds(it * BODY + h * HAND, HAND), ex0:ex1])
                                for j in range(HAND):
                                    for k in range(1 if weight == "act1" else H1):
                                        last = act.activation(weighted[:, slot + j, k * D:(k + 1) * D], gath[:, h * HAND + j, :],
                                                              ACT.Copy, scale=WS[:, bass.ds(it * BODY + h * HAND + j, 1), k])
                                last.then_inc(rows_used, 1)
                            if h % (HANDS // 2) == HANDS // 2 - 1:
                                half = h // (HANDS // 2)
                                for g in range(half * HANDS // 2, (half + 1) * HANDS // 2):
                                    act.wait_ge(rows_in[g], it * (16 * HAND) + 16 * HAND)
                                    act.sem_inc(act_turns, 1)
                                act.copy(idx_ring[:, half, :], idx_step[:, bass.ds(it * BODY + BODY + half * HALF, HALF)]).then_inc(idx_copied, 1)

                @block.vector
                def _(dve):
                    link(dve, dve.memset(A1[:, 0:NB * W], 0.0))
                    if weight == "dve8":
                        dve.sem_inc(rows_used, HANDS)

                    def hot(it, h):
                        for j in range(HAND):
                            s = (h % DEPTH) * HAND + j
                            if j == 0:
                                dve.wait_ge(multiplied, it * HANDS + h + 1)
                            last = dve.tensor_scalar(onehot[:, s, :], iota_row[:], dst_step[:, bass.ds(it * BODY + h * HAND + j, 1)],
                                                     None, ALU.is_equal)
                        last.then_inc(hot_ready, 1)

                    dve.wait_ge(multiplied, 1)
                    for j in range(HAND):
                        last = dve.tensor_scalar(onehot[:, j, :], iota_row[:], dst_step[:, j:j + 1], None, ALU.is_equal)
                    last.then_inc(hot_ready, 1)
                    with dve.Fori(0, STEPS // BODY) as it:
                        for h in range(HANDS):
                            if weight == "dve8":
                                dve.wait_ge(rows_in[h], it * (16 * HAND) + 16 * HAND)
                                slot = (h % DEPTH) * HAND
                                wk = WS[:, bass.ds(it * BODY + h * HAND, HAND), :]
                                dve.tensor_copy(weighted[:, slot:slot + HAND, D:D + H3], wk)
                                for j in range(HAND):
                                    last = dve.tensor_tensor(weighted[:, slot + j, 0:D].rearrange("p (k c) -> p k c", c=C3),
                                                             gath[:, h * HAND + j, :].rearrange("p (k c) -> p k c", c=C3),
                                                             WS[:, bass.ds(it * BODY + h * HAND + j, 1), :].rearrange("p o k -> p (o k)").unsqueeze(2).broadcast_to([P, H3, C3]), ALU.mult)
                                last.then_inc(rows_used, 1)
                            hot(it, h + 1)
                            for g in range(GPH):
                                gg = it * (BODY // GROUP) + h * GPH + g
                                b = dve.value_load(blk_reg[0:1, bass.ds(gg, 1)], min_val=0, max_val=NB - 1)
                                if g == 0:
                                    dve.wait_ge(multiplied, it * HANDS + h + 1 + DEPTH)
                                a = acc[:, bass.ds(b, 1), :].rearrange("p o w -> p (o w)")
                                dve.wait_ge(flushed, gg + HANDS * GPH)
                                dve.tensor_tensor(a, a, ps[:, (h % DEPTH) * GPH + g, 0:W], ALU.add).then_inc(flushed, 1)

                @block.tensor
                def _(pe):
                    pe.sem_inc(multiplied, DEPTH)
                    pe.sem_inc(flushed, HANDS * GPH)
                    with pe.Fori(0, STEPS // BODY) as it:
                        for h in range(HANDS):
                            pe.wait_ge(hot_ready, it * HANDS + h + 1)
                            if weight == "none":
                                pe.wait_ge(rows_in[h], it * (16 * HAND) + 16 * HAND)
                            else:
                                pe.wait_ge(rows_used, it * HANDS + h + 1 + HANDS)
                            for j in range(HAND):
                                s = (h % DEPTH) * HAND + j
                                g = (h % DEPTH) * GPH + j // GROUP
                                rhs = gath[:, h * HAND + j, :] if weight == "none" else weighted[:, s, 0:W]
                                mm = pe.matmul(ps[:, g, 0:W], onehot[:, s, :], rhs, start=(j % GROUP == 0), stop=(j % GROUP == GROUP - 1))
                            mm.then_inc(multiplied, 1)
            return acc

        def node_products(pe, lhs, rhs, width, ready, done, per_bank=4):
            pe.wait_ge(*ready)
            for b in range(NB):
                mm = pe.matmul(ps[:, 2 + b // per_bank, (b % per_bank) * width:(b % per_bank + 1) * width], lhs[:, b, :], rhs, start=True, stop=True)
            mm.then_inc(done, 1)

        TG = -(-NB // 4)

        def wide_products(pe, lhs, rhs, kept, done, used):
            for b in range(NB):
                g = b // 4
                if b % 4 == 0:
                    pe.wait_ge(kept, TG)
                    if g >= 2:
                        pe.wait_ge(used, g - 1)
                mm = pe.matmul(ps[:, 2 + g % 2, (b % 4) * P:(b % 4 + 1) * P], lhs[:, b, :], rhs, start=True, stop=True)
                if b % 4 == 3 or b == NB - 1:
                    mm.then_inc(done, 1)

        def bank_squares(g):
            n = min(4, NB - 4 * g)
            return slice(4 * g, 4 * g + n), ps[:, 2 + g % 2, 0:n * P].rearrange("p (b f) -> p b f", f=P)

        def write_table(sp, source, ready, out_done):
            sp.wait_ge(*ready)
            sp.dma_start(table_view, source).then_inc(out_done, 16)
            sp.wait_ge(out_done, 16)

        wT = wbuf[:, 0:P]
        mask_col = ve_col[:, 3:4]
        attn_bc = bias_row
        a0_in, a0_root, a0_rooted, a0_norm = sem("a0_in"), sem("a0_root"), sem("a0_rooted"), sem("a0_norm")
        a0_turned, a0_kept, a0_done, a0_used = sem("a0_turned"), sem("a0_kept"), sem("a0_done"), sem("a0_used")
        a0_wt, a0_wk, a0_table = sem("a0_wt"), sem("a0_wk"), sem("a0_table")
        with nc.Block() as block:
            @block.sync
            def _(sp):
                sp.dma_start(wnat[:, 0:P], L0_W).then_inc(a0_in, 16)
                with nc.allow_non_contiguous_dma("one column"):
                    sp.dma_start(mask_col, L0_mask.unsqueeze(1)).then_inc(a0_in, 16)
                sp.dma_start(attn_bc[:], L0_attn.unsqueeze(0).broadcast_to([P, D])).then_inc(a0_in, 16)
                write_table(sp, hW, (a0_used, TG), a0_table)

            @block.vector
            def _(dve):
                standardise(dve, (a0_root, a0_rooted), xs[:])
                dve.tensor_scalar(hs[:], hs[:], 0.0, None, ALU.max).then_inc(a0_norm, 1)
                dve.wait_ge(a0_wt, 1)
                dve.tensor_copy(wT, ps[:, 4, 0:P]).then_inc(a0_wk, 1)
                for g in range(TG):
                    bs, got = bank_squares(g)
                    dve.wait_ge(a0_done, g + 1)
                    dve.tensor_copy(hW[:, bs, :], got).then_inc(a0_used, 1)
                dve.wait_ge(a0_used, TG)
                dve.wait_ge(a0_in, 48)
                link(dve, dve.tensor_tensor(tmp, hW, per_feature(attn_bc[:]), ALU.mult))
                link(dve, dve.tensor_reduce(scal[:, 0, :], tmp, AX.X, ALU.add))
                link(dve, dve.scalar_tensor_tensor(out=scal[:, 0, :], in0=scal[:, 0, :], scalar=0.01, in1=scal[:, 0, :],
                                                   op0=ALU.mult, op1=ALU.max))

            @block.scalar
            def _(act):
                std_root(act, a0_root, a0_rooted)
                act.wait_ge(a0_in, 48)
                keep_blocks(act, hT, a0_turned, a0_kept, scale=mask_col)

            @block.tensor
            def _(pe):
                pe.wait_ge(a0_in, 48)
                pe.transpose(ps[:, 4, 0:P], wnat[:, 0:P], ident[:]).then_inc(a0_wt, 1)
                turn_blocks(pe, hs, a0_norm, a0_turned, a0_kept)
                pe.wait_ge(a0_wk, 1)
                wide_products(pe, hT, wT, a0_kept, a0_done, a0_used)

        gather_scalars(0, 1)
        forward, backward = segment_max(0, 1)
        w0_shift, w0_exp = sem("w0_shift"), sem("w0_exp")
        with nc.Block() as block:
            @block.vector
            def _(dve):
                link(dve, dve.tensor_tensor(forward, forward, backward, ALU.max))
                dve.tensor_tensor(SE[:, :, 0:1], SE[:, :, 0:1], forward, ALU.subtract).then_inc(w0_shift, 1)
                dve.tensor_copy(SE[:, :, 1:1 + H1], a_edge[:])
                dve.memset(SE[:, :, 4:5], 1.0)
                dve.memset(SE[:, :, 5:KW], 0.0)

            @block.scalar
            def _(act):
                act.wait_ge(w0_shift, 1)
                act.activation(SE[:, :, 0], SE[:, :, 0], ACT.Exp).then_inc(w0_exp, 1)

        to_steps(0, 5)
        acc = row_pass(0, 5, D + 5, "act1", 0, 5)

        loop_score = sb("loop_score", [P, H1, NB])
        f0_ready, f0_done, f0_blocks = sem("f0_ready"), sem("f0_done"), sem("f0_blocks")
        with nc.Block() as block:
            @block.vector
            def _(dve):
                den, rec = small[:, 0, :], small[:, 1, :]
                dve.tensor_copy(deg[:], acc[:, :, D + 4])
                link(dve, dve.tensor_scalar(den, acc[:, :, D], 0.5, None, ALU.max))
                link(dve, dve.reciprocal(rec, den))
                link(dve, dve.tensor_tensor(hs[:], acc[:, :, 0:D], per_node(rec), ALU.mult))
                link(dve, dve.scalar_tensor_tensor(out=xs[:], in0=hs[:], scalar=0.0, in1=xs[:], op0=ALU.max, op1=ALU.add))
                link(dve, dve.tensor_scalar(den, deg[:], 1.0, None, ALU.max))
                link(dve, dve.reciprocal(rec, den))
                for k in range(H1):
                    dve.tensor_tensor(loop_score[:, k, :], acc[:, :, D + 1 + k], rec, ALU.mult)
                dve.wait_ge(f0_done, 1)
                totals, upto, node_no, first = small[:, 2, :], small[:, 3, :], small[:, 4, :], small[:, 5, :]
                link(dve, dve.tensor_copy(totals, ps[:, 1, 0:NB]))
                link(dve, dve.tensor_tensor_scan(upto, ones[:, 0:NB], totals, 0.0, ALU.mult, ALU.add))
                link(dve, dve.tensor_tensor(upto, upto, totals, ALU.subtract))
                link(dve, dve.tensor_tensor(first, upto, ps[:, 0, 0:NB], ALU.add))
                link(dve, dve.tensor_scalar(node_no, iota_hi[:], float(P), iota_p[:, 0:1], ALU.mult, ALU.add))
                link(dve, dve.tensor_scalar(node_no, node_no, float(EP), None, ALU.add))
                link(dve, dve.tensor_tensor(node_no, node_no, first, ALU.subtract))
                link(dve, dve.tensor_scalar(den, deg[:], 0.0, None, ALU.is_equal))
                link(dve, dve.tensor_tensor(node_no, node_no, den, ALU.mult))
                link(dve, dve.tensor_tensor(seed_idx[:], node_no, first, ALU.add))

            @block.tensor
            def _(pe):
                pe.matmul(ps[:, 0, 0:NB], tri[:], acc[:, :, D + 4], start=True, stop=True)
                pe.matmul(ps[:, 1, 0:NB], ones[:], acc[:, :, D + 4], start=True, stop=True).then_inc(f0_done, 1)

        def scatter_seeds(pool, done):
            for b in range(NB):
                pool.indirect_dma_start(seeds, bass.IndirectOffsetOnAxis(ap=seed_idx[:, b:b + 1], axis=0),
                                        seed_vals[:, b, :], None).then_inc(done, 16)
            pool.wait_ge(done, 16 * NB)

        end_layer()

        U = wbuf[:, 1152 - 2 * H1:1152]
        att_bc = A2[:, 1024:1024 + 2 * 384]
        u_prods = A2[:, 2048:2048 + 768]
        a1_in, a1_root, a1_rooted, a1_norm = sem("a1_in"), sem("a1_root"), sem("a1_rooted"), sem("a1_norm")
        a1_turned, a1_kept, a1_done = sem("a1_turned"), sem("a1_kept"), sem("a1_done")
        a1_u, a1_seed, a1_seeded, a1_table = sem("a1_u"), sem("a1_seed"), sem("a1_seeded"), sem("a1_table")
        with nc.Block() as block:
            @block.sync
            def _(sp):
                sp.dma_start(wnat[:], L1_W).then_inc(a1_in, 16)
                sp.dma_start(att_bc[:, 0:384], L1_as.rearrange("h c -> (h c)").unsqueeze(0).broadcast_to([P, 384])).then_inc(a1_in, 16)
                sp.dma_start(att_bc[:, 384:768], L1_ad.rearrange("h c -> (h c)").unsqueeze(0).broadcast_to([P, 384])).then_inc(a1_in, 16)
                write_table(sp, hs[:], (a1_norm, 1), a1_table)

            @block.gpsimd
            def _(pool):
                pool.wait_ge(a1_seed, 1)
                scatter_seeds(pool, a1_seeded)

            @block.vector
            def _(dve):
                dve.memset(A2[:, 0:NB * KW], 0.0)
                standardise(dve, (a1_root, a1_rooted), xs[:])
                dve.tensor_scalar(hs[:], hs[:], 0.0, None, ALU.max).then_inc(a1_norm, 1)
                dve.wait_ge(a1_in, 48)
                for k in range(2):
                    u_prod = u_prods[:, k * 384:(k + 1) * 384]
                    link(dve, dve.tensor_tensor(u_prod, wnat[:], att_bc[:, k * 384:(k + 1) * 384], ALU.mult))
                    last = dve.tensor_reduce(U[:, k * H1:(k + 1) * H1], u_prod.rearrange("p (h c) -> p h c", c=D), AX.X, ALU.add)
                last.then_inc(a1_u, 1)
                dve.wait_ge(a1_done, 1)
                got = ps[:, 2, 0:NB * 2 * H1].rearrange("p (b k) -> p k b", k=2 * H1)
                link(dve, dve.tensor_copy(scal[:, 0:2 * H1, :], got))
                dve.tensor_copy(seed_vals[:, :, 0:H1].rearrange("p b k -> p k b"), scal[:, H1:2 * H1, :])
                link(dve, dve.tensor_tensor(loop_score[:], loop_score[:], scal[:, 0:H1, :], ALU.add))
                link(dve, dve.tensor_tensor(loop_score[:], loop_score[:], scal[:, H1:2 * H1, :], ALU.add))
                dve.scalar_tensor_tensor(out=seed_vals[:, :, H1:2 * H1].rearrange("p b k -> p k b"), in0=loop_score[:], scalar=0.2,
                                         in1=loop_score[:], op0=ALU.mult, op1=ALU.max).then_inc(a1_seed, 1)

            @block.scalar
            def _(act):
                std_root(act, a1_root, a1_rooted)
                keep_blocks(act, hT, a1_turned, a1_kept)

            @block.tensor
            def _(pe):
                turn_blocks(pe, hs, a1_norm, a1_turned, a1_kept)
                pe.wait_ge(a1_kept, TG)
                node_products(pe, hT, U, 2 * H1, (a1_u, 1), a1_done, per_bank=NB)

        gather_scalars(1, H1)
        db1_in = sem("db1_in")
        with nc.Block() as block:
            @block.sync
            def _(sp):
                sp.dma_start(A3[:, 0:EC * KW], seeds_edges.rearrange("(p c) k -> p (c k)", p=P)).then_inc(db1_in, 16)
                sp.wait_ge(db1_in, 16)
        copy_down(1, 2 * H1)
        with nc.Block() as block:
            @block.vector
            def _(dve):
                link(dve, dve.tensor_tensor(SE[:, :, 0:H1], SE[:, :, 0:H1], DB[:, :, 0:H1], ALU.add))
                link(dve, dve.tensor_tensor(SE[:, :, 0:H1], SE[:, :, 0:H1], a_edge[:], ALU.add))
                link(dve, dve.scalar_tensor_tensor(out=SE[:, :, 0:H1], in0=SE[:, :, 0:H1], scalar=0.2, in1=SE[:, :, 0:H1],
                                                   op0=ALU.mult, op1=ALU.max))
        forward, backward = segment_max(1, H1)
        w1_shift, w1_exp = sem("w1_shift"), sem("w1_exp")
        with nc.Block() as block:
            @block.vector
            def _(dve):
                link(dve, dve.tensor_tensor(forward, forward, backward, ALU.max))
                link(dve, dve.tensor_tensor(forward, forward, DB[:, :, H1:2 * H1], ALU.max))
                dve.tensor_tensor(SE[:, :, 0:H1], SE[:, :, 0:H1], forward, ALU.subtract)
                dve.tensor_tensor(SE[:, :, H1:2 * H1], DB[:, :, H1:2 * H1], forward, ALU.subtract).then_inc(w1_shift, 1)
                dve.memset(SE[:, :, 2 * H1:KW], 0.0)
                link(dve, dve.tensor_scalar(scan_tmp[:], keep_f[:], -1.0, 1.0, ALU.mult, ALU.add))
                dve.wait_ge(w1_exp, 1)
                dve.tensor_tensor(SE[:, :, H1:2 * H1], SE[:, :, H1:2 * H1], scan_tmp[:].unsqueeze(2).broadcast_to([P, EC, H1]), ALU.mult)

            @block.scalar
            def _(act):
                act.wait_ge(w1_shift, 1)
                act.activation(SE[:, :, 0:2 * H1], SE[:, :, 0:2 * H1], ACT.Exp).then_inc(w1_exp, 1)

        to_steps(1, 2 * H1)
        acc = row_pass(1, 2 * H1, H1 * D + 2 * H1, "act3", 0, 2 * H1)

        whT = A2[:, 0:384]
        lin = A2[:, 384:768]
        V = A2[:, 768:1152]
        gb_col = A2[:, 1152:1155]
        gb_wide = A2[:, 1280:1664]
        aggT = A2[:, 2048:2048 + 2 * 384]
        g_bc, b_bc, lb_bc = wnat[:, 0:D], wnat[:, D:2 * D], wnat[:, 2 * D:3 * D]
        f1_in, f1_late, f1_wt, f1_wk, f1_v, f1_vk = sem("f1_in"), sem("f1_late"), sem("f1_wt"), sem("f1_wk"), sem("f1_v"), sem("f1_vk")
        f1_mean, f1_turned, f1_kept, f1_y, f1_used = sem("f1_mean"), sem("f1_turned"), sem("f1_kept"), sem("f1_y"), sem("f1_used")
        f1_root, f1_rooted = sem("f1_root"), sem("f1_rooted")
        with nc.Block() as block:
            @block.sync
            def _(sp):
                sp.dma_start(lin.rearrange("p (h o) -> p h o", h=H1), L1_lW.rearrange("(h c) o -> c h o", h=H1)).then_inc(f1_in, 16)
                with nc.allow_non_contiguous_dma("three columns"):
                    sp.dma_start(gb_col.unsqueeze(2), L1_gb.rearrange("(h c) -> c h", h=H1).unsqueeze(2)).then_inc(f1_in, 16)
                sp.wait_ge(f1_wt, 1)
                for row, v in ((g_bc, L1_g), (b_bc, L1_b), (lb_bc, L1_lb)):
                    sp.dma_start(row, v.unsqueeze(0).broadcast_to([P, D])).then_inc(f1_late, 16)
                sp.wait_ge(f1_late, 48)

            @block.vector
            def _(dve):
                none, den, rec = small[:, 0, :], small[:, 1, :], small[:, 2, :]
                link(dve, dve.tensor_scalar(none, deg[:], 0.0, None, ALU.is_equal))
                for k in range(H1):
                    wl = small[:, 3 + k, :]
                    link(dve, dve.tensor_tensor(wl, acc[:, :, H1 * D + H1 + k], none, ALU.add))
                    link(dve, dve.tensor_tensor(den, acc[:, :, H1 * D + k], wl, ALU.add))
                    link(dve, dve.reciprocal(rec, den))
                    link(dve, dve.tensor_tensor(wl, wl, rec, ALU.mult))
                    mean = acc[:, :, k * D:(k + 1) * D]
                    link(dve, dve.tensor_tensor(mean, mean, per_node(rec), ALU.mult))
                    for b in range(NB):
                        last = dve.scalar_tensor_tensor(out=mean[:, b, :], in0=hs[:, b, :], scalar=wl[:, b:b + 1], in1=mean[:, b, :],
                                                        op0=ALU.mult, op1=ALU.add)
                    last.then_inc(f1_mean, 1)
                dve.wait_ge(f1_wt, 1)
                dve.tensor_copy(whT, ps[:, 7, 0:384])
                dve.wait_ge(f1_in, 32)
                dve.tensor_copy(gb_wide.rearrange("p (h m) -> p h m", h=H1), gb_col.unsqueeze(2).broadcast_to([P, H1, P])).then_inc(f1_wk, 1)
                dve.wait_ge(f1_v, 1)
                dve.tensor_copy(V, ps[:, 6, 0:384])
                dve.wait_ge(f1_late, 48)
                dve.tensor_tensor(bias_row[:], lb_bc, ps[:, 5, 0:D], ALU.add).then_inc(f1_vk, 1)
                dve.wait_ge(f1_vk, 1)
                for b in range(NB):
                    dve.wait_ge(f1_y, b + 1)
                    link(dve, dve.tensor_tensor(hs[:, b, :], hs[:, b, :], ps[:, 2 + b % 2, 0:D], ALU.add))
                    dve.tensor_tensor(hs[:, b, :], hs[:, b, :], bias_row[:], ALU.add).then_inc(f1_used, 1)
                dve.wait_ge(f1_used, NB)
                standardise(dve, (f1_root, f1_rooted), hs[:])
                link(dve, dve.tensor_tensor(hs[:], hs[:], per_feature(g_bc), ALU.mult))
                link(dve, dve.tensor_tensor(hs[:], hs[:], per_feature(b_bc), ALU.add))
                dve.tensor_tensor(xs[:], xs[:], hs[:], ALU.add)

            @block.scalar
            def _(act):
                for b in range(NB):
                    act.wait_ge(f1_turned, b + 1)
                    if b >= 2:
                        act.wait_ge(f1_y, b - 1)
                    act.copy(aggT[:, (b % 2) * 384:(b % 2 + 1) * 384], ps[:, b % 2, 0:384]).then_inc(f1_kept, 1)
                std_root(act, f1_root, f1_rooted)

            @block.tensor
            def _(pe):
                for k in range(H1):
                    mm = pe.transpose(ps[:, 7, k * P:(k + 1) * P], wnat[:, k * P:(k + 1) * P], ident[:])
                mm.then_inc(f1_wt, 1)
                pe.wait_ge(f1_wk, 1)
                for k in range(H1):
                    pe.matmul(ps[:, 6, k * P:(k + 1) * P], whT[:, k * P:(k + 1) * P], lin[:, k * P:(k + 1) * P], start=True, stop=True)
                for k in range(H1):
                    mm = pe.matmul(ps[:, 5, 0:P], gb_wide[:, k * P:(k + 1) * P], lin[:, k * P:(k + 1) * P], start=(k == 0), stop=(k == H1 - 1))
                mm.then_inc(f1_v, 1)
                pe.wait_ge(f1_mean, H1)
                pe.wait_ge(f1_vk, 1)

                def turn(b):
                    if b >= 2:
                        pe.wait_ge(f1_kept, b - 1)
                    for k in range(H1):
                        mm = pe.transpose(ps[:, b % 2, k * P:(k + 1) * P], acc[:, b, k * P:(k + 1) * P], ident[:])
                    mm.then_inc(f1_turned, 1)

                turn(0)
                for b in range(NB):
                    if b + 1 < NB:
                        turn(b + 1)
                    pe.wait_ge(f1_kept, b + 1)
                    if b >= 2:
                        pe.wait_ge(f1_used, b - 1)
                    for k in range(H1):
                        mm = pe.matmul(ps[:, 2 + b % 2, 0:P], aggT[:, (b % 2) * 384 + k * P:(b % 2) * 384 + (k + 1) * P], V[:, k * P:(k + 1) * P],
                                       start=(k == 0), stop=(k == H1 - 1))
                    mm.then_inc(f1_y, 1)

        end_layer()

        Wd = wbuf[:, 1144:1152]
        bd_bc = bias_row[:, 0:K2]
        coef2 = scal[:, :, :].rearrange("p k b -> p (k b)")[:, 0:NB * K2].rearrange("p (b k) -> p b k", k=K2)
        dis = small[:, 8, :]
        a2_in, a2_root, a2_rooted, a2_norm = sem("a2_in"), sem("a2_root"), sem("a2_rooted"), sem("a2_norm")
        a2_turned, a2_kept, a2_done, a2_table = sem("a2_turned"), sem("a2_kept"), sem("a2_done"), sem("a2_table")
        a2_shift, a2_exp, a2_scaled = sem("a2_shift"), sem("a2_exp"), sem("a2_scaled")
        with nc.Block() as block:
            @block.sync
            def _(sp):
                sp.dma_start(Wd, L2_Wd).then_inc(a2_in, 16)
                sp.dma_start(bd_bc, L2_bd.unsqueeze(0).broadcast_to([P, K2])).then_inc(a2_in, 16)
                write_table(sp, hs[:], (a2_scaled, 1), a2_table)

            @block.vector
            def _(dve):
                standardise(dve, (a2_root, a2_rooted), xs[:])
                dve.tensor_scalar(hs[:], hs[:], 0.0, None, ALU.max).then_inc(a2_norm, 1)
                dve.tensor_scalar(dis, deg[:], 1.0, None, ALU.add)
                dve.wait_ge(a2_in, 32)
                dve.wait_ge(a2_done, 1)
                got = ps[:, 2, 0:NB * K2].rearrange("p (b k) -> p b k", k=K2)
                link(dve, dve.tensor_tensor(coef2, got, bd_bc.unsqueeze(1).broadcast_to([P, NB, K2]), ALU.add))
                link(dve, dve.tensor_reduce(small[:, 3, :], coef2, AX.X, ALU.max))
                link(dve, dve.tensor_tensor(coef2, coef2, small[:, 3, :].unsqueeze(2).broadcast_to([P, NB, K2]), ALU.subtract))
                dve.sem_inc(a2_shift, 1)
                dve.wait_ge(a2_exp, 2)
                link(dve, dve.tensor_reduce(small[:, 4, :], coef2, AX.X, ALU.add))
                link(dve, dve.reciprocal(small[:, 5, :], small[:, 4, :]))
                link(dve, dve.reciprocal(dis, dis))
                dve.tensor_tensor(coef2, coef2, small[:, 5, :].unsqueeze(2).broadcast_to([P, NB, K2]), ALU.mult)
                dve.tensor_tensor(hs[:], hs[:], per_node(dis), ALU.mult).then_inc(a2_scaled, 1)

            @block.scalar
            def _(act):
                std_root(act, a2_root, a2_rooted)
                keep_blocks(act, hT, a2_turned, a2_kept)
                act.wait_ge(a2_shift, 1)
                act.activation(dis, dis, ACT.Sqrt).then_inc(a2_exp, 1)
                act.activation(coef2, coef2, ACT.Exp).then_inc(a2_exp, 1)

            @block.tensor
            def _(pe):
                pe.wait_ge(a2_in, 32)
                turn_blocks(pe, hs, a2_norm, a2_turned, a2_kept)
                node_products(pe, hT, Wd, K2, (a2_kept, TG), a2_done, per_bank=NB)

        acc = row_pass(2, 0, D, "none", 0, 0)

        W2 = wbuf[:, 0:K2 * D]
        b2_bc = A3[:, 0:K2 * D]
        biased = A3[:, K2 * D:3 * K2 * D].rearrange("p (i z) -> p i z", i=2)
        scaled = A3[:, 3 * K2 * D:5 * K2 * D].rearrange("p (i z) -> p i z", i=2)
        aT = A2[:, 0:NP].rearrange("p (b f) -> p b f", f=D)
        f2_in, f2_agg, f2_turned, f2_kept = sem("f2_in"), sem("f2_agg"), sem("f2_turned"), sem("f2_kept")
        f2_mul, f2_biased, f2_scaled, f2_sum = sem("f2_mul"), sem("f2_biased"), sem("f2_scaled"), sem("f2_sum")
        with nc.Block() as block:
            @block.sync
            def _(sp):
                sp.dma_start(W2.rearrange("p (k o) -> p k o", k=K2), L2_W.rearrange("k i o -> i k o")).then_inc(f2_in, 16)
                sp.dma_start(b2_bc, L2_b.rearrange("k o -> (k o)").unsqueeze(0).broadcast_to([P, K2 * D])).then_inc(f2_in, 16)
                sp.wait_ge(f2_in, 32)

            @block.vector
            def _(dve):
                link(dve, dve.tensor_tensor(acc, acc, hs[:], ALU.add))
                dve.tensor_tensor(acc, acc, per_node(dis), ALU.mult).then_inc(f2_agg, 1)
                dve.wait_ge(f2_in, 32)

                def reduce(b):
                    dve.wait_ge(f2_scaled, b + 1)
                    link(dve, dve.tensor_reduce(hs[:, b, :], scaled[:, b % 2, :].rearrange("p (k o) -> p o k", k=K2), AX.X, ALU.add))
                    dve.tensor_tensor(xs[:, b, :], xs[:, b, :], hs[:, b, :], ALU.add).then_inc(f2_sum, 1)

                for b in range(NB):
                    dve.wait_ge(f2_mul, b + 1)
                    if b >= 2:
                        dve.wait_ge(f2_scaled, b - 1)
                    dve.tensor_tensor(biased[:, b % 2, :].rearrange("p (i z) -> p i z", i=2), ps[:, 2 + 2 * (b % 2):4 + 2 * (b % 2), :],
                                      b2_bc.rearrange("p (i z) -> p i z", i=2), ALU.add).then_inc(f2_biased, 1)
                    if b:
                        reduce(b - 1)
                reduce(NB - 1)

            @block.scalar
            def _(act):
                keep_blocks(act, aT, f2_turned, f2_kept)
                for b in range(NB):
                    act.wait_ge(f2_biased, b + 1)
                    if b >= 2:
                        act.wait_ge(f2_sum, b - 1)
                    for k in range(K2):
                        last = act.activation(scaled[:, b % 2, k * D:(k + 1) * D], biased[:, b % 2, k * D:(k + 1) * D], ACT.Relu,
                                              scale=coef2[:, b, k:k + 1])
                    last.then_inc(f2_scaled, 1)

            @block.tensor
            def _(pe):
                turn_blocks(pe, acc, f2_agg, f2_turned, f2_kept)
                pe.wait_ge(f2_in, 32)
                pe.wait_ge(f2_kept, TG)
                for b in range(NB):
                    if b >= 2:
                        pe.wait_ge(f2_biased, b - 1)
                    for i in range(2):
                        mm = pe.matmul(ps[:, 2 + 2 * (b % 2) + i, :], aT[:, b, :], W2[:, i * 512:(i + 1) * 512], start=True, stop=True)
                    mm.then_inc(f2_mul, 1)

        end_layer()

        att3 = wnat[:, 0:2 * D]
        Wp, Wsk = wbuf[:, 0:D], wbuf[:, D:2 * D]
        a3_in, a3_root, a3_rooted, a3_norm = sem("a3_in"), sem("a3_root"), sem("a3_rooted"), sem("a3_norm")
        a3_turned, a3_kept, a3_done, a3_used = sem("a3_turned"), sem("a3_kept"), sem("a3_done"), sem("a3_used")
        a3_seed, a3_seeded, a3_table = sem("a3_seed"), sem("a3_seeded"), sem("a3_table")
        with nc.Block() as block:
            @block.sync
            def _(sp):
                sp.dma_start(Wp, L3_Wp).then_inc(a3_in, 16)
                sp.dma_start(Wsk, L3_Ws).then_inc(a3_in, 16)
                sp.dma_start(att3[:, 0:D], L3_as.rearrange("o h c -> o (h c)").broadcast_to([P, D])).then_inc(a3_in, 16)
                sp.dma_start(att3[:, D:2 * D], L3_at.rearrange("o h c -> o (h c)").broadcast_to([P, D])).then_inc(a3_in, 16)
                write_table(sp, hW, (a3_used, TG), a3_table)

            @block.gpsimd
            def _(pool):
                pool.wait_ge(a3_seed, 1)
                scatter_seeds(pool, a3_seeded)

            @block.vector
            def _(dve):
                standardise(dve, (a3_root, a3_rooted), xs[:])
                dve.tensor_scalar(hs[:], hs[:], 0.0, None, ALU.max).then_inc(a3_norm, 1)
                for g in range(TG):
                    bs, got = bank_squares(g)
                    dve.wait_ge(a3_done, g + 1)
                    dve.tensor_copy(hW[:, bs, :], got).then_inc(a3_used, 1)
                dve.wait_ge(a3_used, TG)
                dve.wait_ge(a3_in, 64)
                by_head = tmp.rearrange("p b (k c) -> p b k c", c=C3)
                link(dve, dve.tensor_tensor(tmp, hW, per_feature(att3[:, 0:D]), ALU.mult))
                link(dve, dve.tensor_reduce(scal[:, 0:H3, :].rearrange("p k b -> p b k"), by_head, AX.X, ALU.add))
                link(dve, dve.tensor_tensor(tmp, hW, per_feature(att3[:, D:2 * D]), ALU.mult))
                dve.tensor_reduce(seed_vals, by_head, AX.X, ALU.add).then_inc(a3_seed, 1)

            @block.scalar
            def _(act):
                std_root(act, a3_root, a3_rooted)
                keep_blocks(act, hT, a3_turned, a3_kept)

            @block.tensor
            def _(pe):
                turn_blocks(pe, hs, a3_norm, a3_turned, a3_kept)
                pe.wait_ge(a3_in, 64)
                wide_products(pe, hT, Wp, a3_kept, a3_done, a3_used)

        gather_scalars(3, H3)
        db3_in = sem("db3_in")
        with nc.Block() as block:
            @block.sync
            def _(sp):
                sp.dma_start(A3[:, 0:EC * KW], seeds_edges.rearrange("(p c) k -> p (c k)", p=P)).then_inc(db3_in, 16)
                sp.wait_ge(db3_in, 16)
        copy_down(3, H3)
        edge_no = A1[:, 0:EC]
        top = carry_col[:, 0, 0:1]
        neg_top = carry_col[:, 1, 0:1]
        w3_iota, w3_top, w3_row, w3_rowmax, w3_bc, w3_neg = sem("w3_iota"), sem("w3_top"), sem("w3_row"), sem("w3_rowmax"), sem("w3_bc"), sem("w3_neg")
        w3_exp = sem("w3_exp")
        with nc.Block() as block:
            @block.gpsimd
            def _(pool):
                pool.iota(edge_no, [[1, EC]], base=0, channel_multiplier=EC, allow_small_or_imprecise_dtypes=True).then_inc(w3_iota, 1)

            @block.vector
            def _(dve):
                flat = A2[:, :]
                link(dve, dve.tensor_tensor(flat, flat, A3[:, 0:EC * KW], ALU.add))
                link(dve, dve.scalar_tensor_tensor(out=flat, in0=flat, scalar=0.2, in1=flat, op0=ALU.mult, op1=ALU.max))
                dve.wait_ge(w3_iota, 1)
                link(dve, dve.tensor_scalar(scan_tmp[:], edge_no, float(E), -BIG, ALU.is_ge, ALU.mult))
                link(dve, dve.tensor_tensor(SE, SE, scan_tmp[:].unsqueeze(2).broadcast_to([P, EC, KW]), ALU.add))
                dve.tensor_reduce(top, flat, AX.X, ALU.max).then_inc(w3_top, 1)
                dve.wait_ge(w3_row, 1)
                dve.tensor_reduce(carry_row[0:1, 3, 0:1], ps[0:1, 0, 0:P], AX.X, ALU.max).then_inc(w3_rowmax, 1)
                dve.wait_ge(w3_bc, 1)
                dve.tensor_scalar(neg_top, ps[:, 1, 0:1], -1.0, None, ALU.mult).then_inc(w3_neg, 1)

            @block.tensor
            def _(pe):
                pe.wait_ge(w3_top, 1)
                pe.transpose(ps[0:1, 0, 0:P], top, ident[:]).then_inc(w3_row, 1)
                pe.wait_ge(w3_rowmax, 1)
                pe.matmul(ps[:, 1, 0:1], ones[0:1, :], carry_row[0:1, 3, 0:1], start=True, stop=True).then_inc(w3_bc, 1)

            @block.scalar
            def _(act):
                act.wait_ge(w3_neg, 1)
                act.activation(A2[:, :], A2[:, :], ACT.Exp, bias=neg_top).then_inc(w3_exp, 1)

        to_steps(3, H3)
        acc = row_pass(3, H3, D + H3, "dve8", 0, H3)

        hT3 = A2[:, 0:NP].rearrange("p (b f) -> p b f", f=D)
        z = A3[:, 0:NP].rearrange("p (b f) -> p b f", f=D)
        f3_start, f3_turned, f3_kept, f3_done, f3_used = sem("f3_start"), sem("f3_turned"), sem("f3_kept"), sem("f3_done"), sem("f3_used")
        f3_low, f3_exp, f3_x, f3_out = sem("f3_low"), sem("f3_exp"), sem("f3_x"), sem("f3_out")
        with nc.Block() as block:
            @block.vector
            def _(dve):
                den = scal[:, 0:H3, :].rearrange("p k b -> p (k b)").rearrange("p (b k) -> p b k", k=H3)
                rec = scal[:, H3:2 * H3, :].rearrange("p k b -> p (k b)").rearrange("p (b k) -> p b k", k=H3)
                dve.memset(small[:, 0, 0:1], 0.0).then_inc(f3_start, 1)
                link(dve, dve.tensor_scalar(den, acc[:, :, D:D + H3], 1e-16, None, ALU.add))
                link(dve, dve.reciprocal(rec, den))
                link(dve, dve.tensor_tensor(z.rearrange("p b (k c) -> p b k c", c=C3), acc[:, :, 0:D].rearrange("p b (k c) -> p b k c", c=C3),
                                            rec.unsqueeze(3).broadcast_to([P, NB, H3, C3]), ALU.mult))
                for g in range(TG):
                    bs, got = bank_squares(g)
                    dve.wait_ge(f3_done, g + 1)
                    dve.tensor_tensor(z[:, bs, :], z[:, bs, :], got, ALU.add).then_inc(f3_used, 1)
                dve.wait_ge(f3_used, TG)
                dve.tensor_scalar(tmp, z, 0.0, None, ALU.min).then_inc(f3_low, 1)
                link(dve, dve.scalar_tensor_tensor(out=xs[:], in0=z, scalar=0.0, in1=xs[:], op0=ALU.max, op1=ALU.add))
                dve.wait_ge(f3_exp, 1)
                dve.scalar_tensor_tensor(out=xs[:], in0=tmp, scalar=-1.0, in1=xs[:], op0=ALU.add, op1=ALU.add).then_inc(f3_x, 1)

            @block.scalar
            def _(act):
                keep_blocks(act, hT3, f3_turned, f3_kept)
                act.wait_ge(f3_low, 1)
                act.activation(tmp, tmp, ACT.Exp).then_inc(f3_exp, 1)

            @block.tensor
            def _(pe):
                turn_blocks(pe, hs, f3_start, f3_turned, f3_kept)
                wide_products(pe, hT3, Wsk, f3_kept, f3_done, f3_used)

            @block.sync
            def _(sp):
                sp.wait_ge(f3_x, 1)
                sp.dma_start(out[0:(NB - 1) * P, :].rearrange("(b p) f -> p b f", p=P), xs[:, 0:NB - 1, :]).then_inc(f3_out, 16)
                sp.dma_start(out[(NB - 1) * P:N, :], xs[0:TAIL, NB - 1, :]).then_inc(f3_out, 16)
                sp.wait_ge(f3_out, 32)


_INS = ['x', 'src', 'dst', 'edge_attr_16', 'L0_gnn_biclique_mask', 'L0_gnn_W', 'L0_gnn_attn', 'L1_gnn_W', 'L1_gnn_W_edge',
        'L1_gnn_att_src', 'L1_gnn_att_dst', 'L1_gnn_att_edge', 'L1_gnn_gat_bias', 'L1_gnn_lin_W', 'L1_gnn_lin_b', 'L1_gnn_ln_g',
        'L1_gnn_ln_b', 'L2_gnn_W', 'L2_gnn_b', 'L2_gnn_W_dict', 'L2_gnn_b_dict', 'L3_gnn_W_proj', 'L3_gnn_W_skip', 'L3_gnn_a_src',
        'L3_gnn_a_tgt']
_OUTS = [((N, D), 'float32')]


def kernel(**inputs):
    import numpy as _np
    import concourse.bacc as _bacc
    from concourse import mybir as _mybir
    from concourse.bass_utils import run_bass_kernel_spmd as _run

    nc = _bacc.Bacc("TRN2", target_bir_lowering=False, num_devices=1)
    arrays, args = {}, []
    for name in _INS:
        a = _np.ascontiguousarray(inputs[name])
        arrays[f"in_{name}_dram"] = a
        args.append(nc.dram_tensor(f"in_{name}_dram", a.shape, _mybir.dt.from_np(a.dtype), kind="ExternalInput").ap())
    for i, (shape, dtype) in enumerate(_OUTS):
        dt = _mybir.dt.from_np(_np.dtype(dtype))
        args.append(nc.dram_tensor(f"out_{i}_dram", shape, dt, kind="ExternalOutput").ap())
    build_gnn(nc, *args)
    r = _run(nc, [arrays], core_ids=[0])
    got = tuple(r.results[0][f"out_{i}_dram"] for i in range(len(_OUTS)))
    return got[0]
```

```python
from contextlib import ExitStack

import concourse.bass as bass
from concourse import mybir

F32 = mybir.dt.float32
I32 = mybir.dt.int32
ALU = mybir.AluOpType
ACT = mybir.ActivationFunctionType
AX = mybir.AxisListType

P = 128
N = 3125
E = 100000
D = 128
NB = -(-N // P)
NP = NB * P
TAIL = N - (NB - 1) * P
EC = -(-E // P) + 2
EC = 16 * (-(-E // (16 * P)))
EP = EC * P
PAD = EP - E
PAD_DST = NP
KW = 8
EA = 16
H1 = 3
H3 = 8
C3 = D // H3
K2 = 8
GROUP = 2
BODY = 32
HAND = 4
DEPTH = 2
TILES = -(-E // P)
GROUPS_NEEDED = (TILES + NB - 1 + NB * (GROUP - 1)) // GROUP
STEPS = BODY * (-(-GROUPS_NEEDED * GROUP // BODY))
GROUPS = STEPS // GROUP
NCH = 8
CH = STEPS // NCH
ACCW = H1 * D + 2 * H1
RW = D + KW
BIG = 1.0e37
LN_EPS = 1e-5
assert CH <= P and STEPS == NCH * CH and BODY % (HAND * DEPTH) == 0


def build_gnn(nc, x, src, dst, edge_attr, L0_mask, L0_W, L0_attn, L1_W, L1_We, L1_as, L1_ad, L1_ae,
              L1_gb, L1_lW, L1_lb, L1_g, L1_b, L2_W, L2_b, L2_Wd, L2_bd, L3_Wp, L3_Ws, L3_as, L3_at, out):
    ctx = ExitStack()
    with ctx:
        def sb(name, shape, dt=F32):
            return ctx.enter_context(nc.sbuf_tensor(name, shape, dt))

        layer_sems = []

        def sem(name):
            layer_sems.append(nc.alloc_semaphore(name))
            return layer_sems[-1]

        def end_layer():
            nc.clear_and_free_semaphores(layer_sems)
            nc.all_engine_barrier()
            layer_sems.clear()

        def dram(name, shape, dt=F32):
            return nc.dram_tensor(name, shape, dt).ap()

        src_flat = dram("src_flat", (EP // P, P), I32)
        dst_flat = dram("dst_flat", (EP // P, P), I32)
        dst_ext = dram("dst_ext", (EP + 2,), I32)
        tables = [dram(f"table{L}", (NP, w)) for L, w in enumerate((D + 1, D + H1, D, D + H3))]
        dst_by_step = dram("dst_by_step", (STEPS * P + 2,))
        runs = dram("runs", (STEPS, 4 * P))
        row_pens_out = dram("row_pens_out", (2, STEPS))
        edge_rows = dram("edge_rows", (EP // P, P * KW))
        seeds = dram("seeds", (EP + NP, KW))
        seeds_edges = seeds[0:EP, :]

        xs = sb("xs", [P, NB, D])
        hs = sb("hs", [P, NB, D])
        A1 = sb("A1", [P, 2 * NP + NB * RW])
        A2 = sb("A2", [P, EC * KW])
        A3 = sb("A3", [P, STEPS * KW])
        a_edge = sb("a_edge", [P, EC, H1])
        gath = sb("gath", [P, BODY, RW])
        onehot = sb("onehot", [P, HAND * DEPTH, P])
        weighted = sb("weighted", [P, HAND * DEPTH, ACCW])
        idx_step = sb("idx_step", [P, STEPS + 2 * BODY], I32)
        idx_ring = sb("idx_ring", [P, 2, BODY], I32)
        dst_step = sb("dst_step", [P, STEPS + HAND])
        keep_f = sb("keep_f", [P, EC])
        scan_tmp = sb("scan_tmp", [P, EC])
        iota_row = sb("iota_row", [P, P])
        iota_p = sb("iota_p", [P, 1])
        iota_hi = sb("iota_hi", [P, NB])
        ident = sb("ident", [P, P])
        tri = sb("tri", [P, P])
        ones = sb("ones", [P, P])
        carry_row = sb("carry_row", [KW, 6, P + 1])
        carry_col = sb("carry_col", [P, 4, KW])
        blk_reg = sb("blk_reg", [1, GROUPS], I32)
        deg = sb("deg", [P, NB])
        seed_idx = sb("seed_idx", [P, NB], I32)
        small = sb("small", [P, 16, NB])
        scal = sb("scal", [P, 2 * KW, NB])
        row_pens = sb("row_pens", [H1, 2, STEPS])
        borders = sb("borders", [BODY, 2, 4, P])
        scores = sb("scores", [P, BODY, KW])
        topped = sb("topped", [P, BODY, H1])
        shifted = sb("shifted", [P, BODY, KW])
        weights = sb("weights", [P, BODY, KW])
        run_f = sb("run_f", [BODY, H1, P])
        run_b = sb("run_b", [BODY, H1, P])
        row_f = sb("row_f", [H1, BODY + 1])
        row_b = sb("row_b", [H1, BODY + 1])
        row_col = sb("row_col", [BODY, 2, KW])
        edge_cols = sb("edge_cols", [P, 2, KW])
        last_max = sb("last_max", [P, KW])
        rescale = sb("rescale", [P, 3, KW])
        first_hot = sb("first_hot", [P, 1])
        pick_first = sb("pick_first", [P, P])
        pick_last = sb("pick_last", [P, P])
        wbuf = sb("wbuf", [P, 3 * 384])
        wnat = sb("wnat", [P, 384])
        bias_row = sb("bias_row", [P, D])
        ps = ctx.enter_context(nc.psum_tensor("ps", [P, 8, 512], F32))

        seed_vals = A2[:, 0:NB * KW].rearrange("p (b k) -> p b k", k=KW)
        SE = A2[:, :].rearrange("p (c k) -> p c k", k=KW)
        DB = A3[:, 0:EC * KW].rearrange("p (c k) -> p c k", k=KW)
        WS = A3[:, :].rearrange("p (s k) -> p s k", k=KW)
        tmp = A1[:, 0:NP].rearrange("p (b f) -> p b f", f=D)
        hT = A1[:, NP:2 * NP].rearrange("p (b f) -> p b f", f=D)
        tab = A1[:, 2 * NP:2 * NP + NB * RW].rearrange("p (b w) -> p b w", w=RW)
        hW = tab[:, :, 0:D]

        dve_chain = ctx.enter_context(nc.semaphore("dve_chain"))
        dve_count = [0]

        def link(dve, ins):
            dve_count[0] += 1
            ins.then_inc(dve_chain, 1)
            dve.wait_ge(dve_chain, dve_count[0])

        loaded = sem("loaded")
        pads_set = sem("pads_set")
        iota_set = sem("iota_set")
        pad_i = A2[0:1, 0:3 * PAD + 4].bitcast(I32)
        with nc.Block() as block:
            @block.sync
            def _(sp):
                sp.dma_start(src_flat.rearrange("a b -> (a b)")[0:E].unsqueeze(0), src.unsqueeze(0)).then_inc(loaded, 16)
                sp.dma_start(dst_flat.rearrange("a b -> (a b)")[0:E].unsqueeze(0), dst.unsqueeze(0)).then_inc(loaded, 16)
                sp.dma_start(dst_ext[1:E + 1].unsqueeze(0), dst.unsqueeze(0)).then_inc(loaded, 16)
                sp.dma_start(xs[:, 0:NB - 1, :], x[0:(NB - 1) * P, :].rearrange("(b p) f -> p b f", p=P)).then_inc(loaded, 16)
                sp.wait_ge(pads_set, 5)
                sp.dma_start(xs[0:TAIL, NB - 1, :], x[(NB - 1) * P:N, :]).then_inc(loaded, 16)
                sp.dma_start(src_flat.rearrange("a b -> (a b)")[E:EP].unsqueeze(0), pad_i[:, 0:PAD]).then_inc(loaded, 16)
                sp.dma_start(dst_flat.rearrange("a b -> (a b)")[E:EP].unsqueeze(0), pad_i[:, PAD:2 * PAD]).then_inc(loaded, 16)
                sp.dma_start(dst_ext[E + 1:EP + 2].unsqueeze(0), pad_i[:, PAD:2 * PAD + 1]).then_inc(loaded, 16)
                sp.dma_start(dst_ext[0:1].unsqueeze(0), pad_i[:, 2 * PAD + 2:2 * PAD + 3]).then_inc(loaded, 16)
                sp.dma_start(seeds.rearrange("(p a) k -> p (a k)", p=P), A3[:, 0:(EP + NP) * KW // P]).then_inc(loaded, 16)
                sp.wait_ge(loaded, 10 * 16)

            @block.vector
            def _(dve):
                dve.memset(pad_i[:, 0:PAD], 0).then_inc(pads_set, 1)
                dve.memset(pad_i[:, PAD:2 * PAD + 2], PAD_DST).then_inc(pads_set, 1)
                dve.memset(pad_i[:, 2 * PAD + 2:2 * PAD + 4], -1).then_inc(pads_set, 1)
                dve.memset(xs[:, NB - 1, :], 0.0).then_inc(pads_set, 1)
                dve.memset(A3[:], 0.0).then_inc(pads_set, 1)
                dve.memset(ones[:], 1.0)
                dve.memset(idx_step[:, STEPS:STEPS + 2 * BODY], 0)
                dve.memset(dst_step[:, STEPS:STEPS + HAND], -1.0)
                dve.wait_ge(iota_set, 3)
                dve.tensor_scalar(ident[:], iota_row[:], iota_p[:, 0:1], None, ALU.is_equal)
                dve.tensor_scalar(tri[:], iota_row[:], iota_p[:, 0:1], None, ALU.is_gt)
                dve.tensor_scalar(pick_first[:], iota_p[:, 0:1].broadcast_to([P, P]), 0.0, None, ALU.is_equal)
                dve.tensor_scalar(pick_last[:], iota_p[:, 0:1].broadcast_to([P, P]), float(P - 1), None, ALU.is_equal)

            @block.gpsimd
            def _(pool):
                pool.iota(iota_row[:], [[1, P]], base=0, channel_multiplier=0,
                          allow_small_or_imprecise_dtypes=True).then_inc(iota_set, 1)
                pool.iota(iota_p[:], [[1, 1]], base=0, channel_multiplier=1,
                          allow_small_or_imprecise_dtypes=True).then_inc(iota_set, 1)
                pool.iota(iota_hi[:], [[1, NB]], base=0, channel_multiplier=0,
                          allow_small_or_imprecise_dtypes=True).then_inc(iota_set, 1)

        prev_i = A1[:, 0:EC].bitcast(I32)
        cur_i = A1[:, EC:2 * EC].bitcast(I32)
        last_i = A2[0:1, 0:EC].bitcast(I32)
        last_f = A2[0:1, EC:2 * EC]
        before = A2[0:NB, 2 * EC:3 * EC]
        in_or_after = A2[0:NB, 3 * EC:3 * EC + GROUPS]
        by_step = A2[0:NB, 4 * EC:4 * EC + STEPS].rearrange("p (g i) -> p g i", i=GROUP)
        group_no = A2[:, 6 * EC:6 * EC + GROUPS]
        plan = A3[:, 0:64]
        plan_i = A3[:, 64:128].bitcast(I32)
        step_no = A3[:, 128:128 + NCH]
        diff = A3[:, 160:160 + P]
        coef = A3[:, 320:322]
        tile_i = sb("tile_i", [P, NCH], I32)
        block_lo = sb("block_lo", [P, NCH])
        plan_in = sem("plan_in")
        plan_iota = sem("plan_iota")
        plan_ready = sem("plan_ready")
        plan_done = sem("plan_done")
        with nc.Block() as block:
            @block.sync
            def _(sp):
                sp.dma_start(prev_i, dst_ext[0:EP].rearrange("(p c) -> p c", p=P)).then_inc(plan_in, 16)
                sp.dma_start(cur_i, dst_ext[1:EP + 1].rearrange("(p c) -> p c", p=P)).then_inc(plan_in, 16)
                with nc.allow_non_contiguous_dma("one element per tile"):
                    sp.dma_start(last_i.unsqueeze(2), dst_flat[:, P - 1:P].unsqueeze(0)).then_inc(plan_in, 16)
            @block.gpsimd
            def _(pool):
                pool.iota(group_no, [[1, GROUPS]], base=0, channel_multiplier=0,
                          allow_small_or_imprecise_dtypes=True).then_inc(plan_iota, 1)
                pool.iota(step_no, [[CH, NCH]], base=0, channel_multiplier=1,
                          allow_small_or_imprecise_dtypes=True).then_inc(plan_iota, 1)

            @block.tensor
            def _(pe):
                pe.wait_ge(plan_ready, 1)
                for q in range(2):
                    mm = pe.matmul(ps[0:NB, q, 0:EC // 2], ones[0:1, 0:NB], last_f[:, q * EC // 2:(q + 1) * EC // 2],
                                   start=True, stop=True)
                mm.then_inc(plan_done, 1)
                pe.wait_ge(plan_ready, 2)
                pe.matmul(ps[0:NB, 2, 0:1], tri[0:NB, 0:NB], plan[0:NB, 4:5], start=True, stop=True).then_inc(plan_done, 1)
                pe.wait_ge(plan_ready, 3)
                pe.matmul(ps[0:NB, 3, 0:1], diff[0:NB, 0:NB], plan[0:NB, 6:7], start=True, stop=True).then_inc(plan_done, 1)
                pe.wait_ge(plan_ready, 4)
                pe.matmul(ps[0:1, 4, 0:GROUPS], ones[0:NB, 0:1], in_or_after, start=True, stop=True)
                for c in range(NCH):
                    mm = pe.matmul(ps[0:CH, 5, 2 * c:2 * c + 2], by_step.rearrange("p g i -> p (g i)")[:, c * CH:(c + 1) * CH],
                                   coef[0:NB, :], start=True, stop=True)
                mm.then_inc(plan_done, 1)
            @block.vector
            def _(dve):
                dve.wait_ge(plan_in, 3 * 16)
                dve.tensor_copy(last_f, last_i).then_inc(plan_ready, 1)
                dve.wait_ge(plan_done, 1)
                link(dve, dve.tensor_scalar(plan[:, 0:1], iota_p[:], float(P), None, ALU.mult))
                link(dve, dve.tensor_scalar(plan[:, 1:2], plan[:, 0:1], float(P), None, ALU.add))
                for k in range(2):
                    link(dve, dve.tensor_scalar(before.rearrange("p (q c) -> p q c", q=2), ps[0:NB, 0:2, 0:EC // 2],
                                                plan[0:NB, k:k + 1], None, ALU.is_lt))
                    link(dve, dve.tensor_reduce(plan[0:NB, 2 + k:3 + k], before, AX.X, ALU.add))
                link(dve, dve.tensor_tensor(plan[0:NB, 5:6], plan[0:NB, 3:4], plan[0:NB, 2:3], ALU.subtract))
                link(dve, dve.tensor_scalar(plan_i[0:NB, 0:1], plan[0:NB, 5:6], 2.0, None, ALU.add))
                link(dve, dve.tensor_scalar(plan_i[0:NB, 1:2], plan_i[0:NB, 0:1], 1, None, ALU.arith_shift_right))
                dve.tensor_copy(plan[0:NB, 4:5], plan_i[0:NB, 1:2]).then_inc(plan_ready, 1)
                dve.wait_ge(plan_done, 2)
                link(dve, dve.tensor_copy(plan[0:NB, 7:8], ps[0:NB, 2, 0:1]))
                link(dve, dve.scalar_tensor_tensor(out=plan[0:NB, 6:7], in0=plan[0:NB, 7:8], scalar=-float(GROUP),
                                                   in1=plan[0:NB, 2:3], op0=ALU.mult, op1=ALU.add))
                link(dve, dve.tensor_scalar(plan[:, 8:9], iota_p[:], 1.0, None, ALU.add))
                link(dve, dve.tensor_scalar(diff, iota_row[:], plan[:, 8:9], None, ALU.is_equal))
                dve.tensor_tensor(diff, ident[:], diff, ALU.subtract).then_inc(plan_ready, 1)
                dve.wait_ge(plan_done, 3)
                dve.wait_ge(plan_iota, 2)
                link(dve, dve.memset(coef[:, 0:1], 1.0))
                link(dve, dve.tensor_copy(coef[0:NB, 1:2], ps[0:NB, 3, 0:1]))
                link(dve, dve.tensor_scalar(in_or_after, group_no[0:NB, :], plan[0:NB, 7:8], None, ALU.is_ge))
                dve.tensor_copy(by_step, in_or_after.unsqueeze(2).broadcast_to([NB, GROUPS, GROUP])).then_inc(plan_ready, 1)
                dve.wait_ge(plan_done, 4)
                dve.tensor_scalar(blk_reg[:], ps[0:1, 4, 0:GROUPS], -1.0, None, ALU.add)
                counts = ps[0:CH, 5, 0:2 * NCH].rearrange("p (c two) -> p c two", two=2)
                dve.tensor_scalar(block_lo[0:CH, :], counts[:, :, 0], float(P), -float(P), ALU.mult, ALU.add)
                link(dve, dve.tensor_tensor(plan[0:CH, 16:16 + NCH], counts[:, :, 1], step_no[0:CH, :], ALU.add))
                dve.tensor_scalar(tile_i[0:CH, :], plan[0:CH, 16:16 + NCH], float(EP // P - 1), None, ALU.min)
                link(dve, dve.tensor_tensor(keep_f[:], cur_i, prev_i, ALU.is_equal))
                link(dve, dve.tensor_reduce(scan_tmp[:, 0:1], keep_f[:], AX.X, ALU.min))
                dve.tensor_copy(carry_col[:, 0, :], scan_tmp[:, 0:1].broadcast_to([P, KW]))

        src_rows = A1[:, 0:NCH * P].bitcast(I32)
        dst_rows = A1[:, NCH * P:2 * NCH * P].bitcast(I32)
        src_rf = A1[:, 2 * NCH * P:3 * NCH * P]
        dst_rf = A1[:, 3 * NCH * P:4 * NCH * P]
        dst_whole = A1[:, 4 * NCH * P:5 * NCH * P]
        step_ends = A1[0:1, 5 * NCH * P:5 * NCH * P + 2]
        whole_out = sem("whole_out")
        ends_set = sem("ends_set")
        EQ = 14
        NQ = (EC * EA // P) // EQ
        ea_in = A2[:, 0:EQ * P]
        ea_T = A2[:, EQ * P:2 * EQ * P]
        we_prod = A2[:, 2 * EQ * P:2 * EQ * P + 3 * 384]
        step_rows_in = sem("step_rows_in")
        ea_loaded = sem("ea_loaded")
        rows_f = sem("rows_f")
        rows_turned = sem("rows_turned")
        rows_kept = sem("rows_kept")
        carry_turned = sem("carry_turned")
        ve_col = sb("ve_col", [P, 4])
        ve_diag = sb("ve_diag", [P, 8 * H1])
        ve_ready = sem("ve_ready")
        ve_placed = sem("ve_placed")
        ea_turned = sem("ea_turned")
        ea_kept = sem("ea_kept")
        ae_done = sem("ae_done")
        ae_kept = sem("ae_kept")
        ea_zero = sem("ea_zero")
        w_in = sem("w_in")
        EA_ROWS = E * EA // P
        PER = EC * EA // P
        FULL = EA_ROWS // PER
        REST = EA_ROWS - FULL * PER
        ea_view = edge_attr.rearrange("(r j) c -> r (j c)", j=8)
        ve_dram = dram("ve_dram", (EA, H1))
        with nc.Block() as block:
            @block.gpsimd
            def _(pool):
                for c in range(NCH):
                    pool.indirect_dma_start(src_rows[0:CH, c * P:(c + 1) * P], None, src_flat,
                                            bass.IndirectOffsetOnAxis(ap=tile_i[0:CH, c:c + 1], axis=0)).then_inc(step_rows_in, 16)
                    pool.indirect_dma_start(dst_rows[0:CH, c * P:(c + 1) * P], None, dst_flat,
                                            bass.IndirectOffsetOnAxis(ap=tile_i[0:CH, c:c + 1], axis=0)).then_inc(step_rows_in, 16)

            @block.sync
            def _(sp):
                sp.dma_start(wnat[0:EA, :], L1_We).then_inc(w_in, 16)
                sp.dma_start(wbuf[0:EA, 0:384], L1_ae.rearrange("h c -> (h c)").unsqueeze(0).broadcast_to([EA, 384])).then_inc(w_in, 16)
                sp.wait_ge(ve_ready, 2)
                sp.dma_start(ve_dram, ve_col[0:EA, 0:H1]).then_inc(ve_placed, 16)
                sp.wait_ge(ve_placed, 16)
                with nc.allow_non_contiguous_dma("eight small squares"):
                    for j in range(8):
                        sp.dma_start(ve_diag[j * EA:(j + 1) * EA, j * H1:(j + 1) * H1], ve_dram).then_inc(ve_placed, 16)
                sp.wait_ge(ea_zero, 1)
                for q in range(NQ):
                    if q:
                        sp.wait_ge(ea_turned, q)
                    sp.dma_start(ea_in[0:FULL, :], ea_view[0:FULL * PER, :].rearrange("(p t) w -> p (t w)", t=PER)[:, q * EQ * P:(q + 1) * EQ * P]).then_inc(ea_loaded, 16)
                    here = min(max(REST - q * EQ, 0), EQ)
                    if here:
                        sp.dma_start(ea_in[FULL:FULL + 1, 0:here * P],
                                     ea_view[FULL * PER + q * EQ:FULL * PER + q * EQ + here, :].rearrange("t w -> (t w)").unsqueeze(0)).then_inc(ea_loaded, 16)
                sp.wait_ge(rows_f, NCH)
                sp.wait_ge(ends_set, 2)
                sp.dma_start(dst_by_step[1:1 + STEPS * P].rearrange("(c s e) -> s c e", c=NCH, s=CH),
                             dst_whole[0:CH, :].rearrange("s (c e) -> s c e", c=NCH)).then_inc(whole_out, 16)
                sp.dma_start(dst_by_step[0:1].unsqueeze(0), step_ends[:, 0:1]).then_inc(whole_out, 16)
                sp.dma_start(dst_by_step[1 + STEPS * P:2 + STEPS * P].unsqueeze(0), step_ends[:, 1:2]).then_inc(whole_out, 16)
                sp.wait_ge(whole_out, 48)
                sp.wait_ge(ea_loaded, 16 * (NQ + -(-REST // EQ)))
                sp.wait_ge(ve_placed, 16 * 9)

            @block.tensor
            def _(pe):
                pe.transpose(ps[0:KW, 0, 0:P], carry_col[:, 0, :], ident[:]).then_inc(carry_turned, 1)
                for c in range(NCH):
                    pe.wait_ge(rows_f, c + 1)
                    if c >= 2:
                        pe.wait_ge(rows_kept, c - 1)
                    pe.transpose(ps[:, 1 + c % 2, 0:CH], src_rf[0:CH, c * P:(c + 1) * P], ident[0:CH, 0:CH])
                    pe.transpose(ps[:, 1 + c % 2, P:P + CH], dst_rf[0:CH, c * P:(c + 1) * P], ident[0:CH, 0:CH]).then_inc(rows_turned, 1)
                pe.wait_ge(ve_placed, 16 * 9)
                for q in range(NQ):
                    pe.wait_ge(ea_loaded, 16 * (q + 1 + min(q + 1, -(-REST // EQ))))
                    if q:
                        pe.wait_ge(ea_kept, q)
                    for t in range(EQ):
                        mm = pe.transpose(ps[:, 3 + t // 4, (t % 4) * P:(t % 4 + 1) * P], ea_in[:, t * P:(t + 1) * P], ident[:])
                    mm.then_inc(ea_turned, 1)
                    pe.wait_ge(ea_kept, q + 1)
                    if q:
                        pe.wait_ge(ae_kept, q)
                    for t in range(EQ):
                        mm = pe.matmul(ps[:, 7, t * 24:(t + 1) * 24], ea_T[:, t * P:(t + 1) * P], ve_diag[:], start=True, stop=True)
                    mm.then_inc(ae_done, 1)

            @block.scalar
            def _(act):
                for q in range(NQ):
                    act.wait_ge(ea_turned, q + 1)
                    if q:
                        act.wait_ge(ae_done, q)
                    act.copy(ea_T[:, 0:12 * P].rearrange("p (b c) -> p b c", c=512), ps[:, 3:6, :])
                    act.copy(ea_T[:, 12 * P:EQ * P], ps[:, 6, 0:2 * P]).then_inc(ea_kept, 1)
                    act.wait_ge(ae_done, q + 1)
                    act.copy(a_edge[:, q * EQ * 8:(q + 1) * EQ * 8, :].rearrange("p c h -> p (c h)"), ps[:, 7, 0:EQ * 24]).then_inc(ae_kept, 1)

            @block.vector
            def _(dve):
                dve.memset(ea_in, 0.0).then_inc(ea_zero, 1)
                dve.memset(step_ends[:, 0:1], -1.0).then_inc(ends_set, 1)
                dve.memset(step_ends[:, 1:2], -2.0).then_inc(ends_set, 1)
                dve.memset(ve_diag[:], 0.0).then_inc(ve_ready, 1)
                dve.wait_ge(w_in, 32)
                link(dve, dve.tensor_tensor(we_prod[0:EA, 0:384], wnat[0:EA, :], wbuf[0:EA, 0:384], ALU.mult))
                dve.tensor_reduce(ve_col[0:EA, 0:H1], we_prod[0:EA, 0:384].rearrange("p (h c) -> p h c", c=P), AX.X, ALU.add).then_inc(ve_ready, 1)
                dve.wait_ge(step_rows_in, 2 * NCH * 16)
                for c in range(NCH):
                    dve.tensor_copy(src_rf[0:CH, c * P:(c + 1) * P], src_rows[0:CH, c * P:(c + 1) * P])
                    dve.tensor_copy(dst_whole[0:CH, c * P:(c + 1) * P], dst_rows[0:CH, c * P:(c + 1) * P])
                    dve.tensor_scalar(dst_rf[0:CH, c * P:(c + 1) * P], dst_rows[0:CH, c * P:(c + 1) * P],
                                      block_lo[0:CH, c:c + 1], None, ALU.subtract).then_inc(rows_f, 1)
                dve.wait_ge(carry_turned, 1)
                dve.tensor_copy(carry_row[:, 0, 0:P], ps[0:KW, 0, 0:P])
                for c in range(NCH):
                    dve.wait_ge(rows_turned, c + 1)
                    dve.tensor_copy(idx_step[:, c * CH:(c + 1) * CH], ps[:, 1 + c % 2, 0:CH])
                    dve.tensor_copy(dst_step[:, c * CH:(c + 1) * CH], ps[:, 1 + c % 2, P:P + CH]).then_inc(rows_kept, 1)

        prev_d, cur_d, next_d = (A1[:, i * NCH * P:(i + 1) * NCH * P] for i in range(3))
        border_rows = A1[:, 3 * NCH * P:7 * NCH * P].rearrange("s (c a e) -> s c a e", c=NCH, a=4)
        pens_raw = A2[0:H1, 0:2 * STEPS].rearrange("k (a s) -> k a s", a=2)
        whole_in, border_set, borders_out, pens_in = sem("whole_in"), sem("border_set"), sem("borders_out"), sem("pens_in")
        with nc.Block() as block:
            @block.sync
            def _(sp):
                for off, t in enumerate((prev_d, cur_d, next_d)):
                    sp.dma_start(t[0:CH, :].rearrange("s (c e) -> s c e", c=NCH),
                                 dst_by_step[off:off + STEPS * P].rearrange("(c s e) -> s c e", c=NCH, s=CH)).then_inc(whole_in, 16)
                sp.wait_ge(border_set, 1)
                sp.dma_start(runs.rearrange("(c s) w -> s c w", c=NCH), border_rows[0:CH, :, :, :].rearrange("s c a e -> s c (a e)")).then_inc(borders_out, 16)
                with nc.allow_non_contiguous_dma("one element per step"):
                    for way, e in ((0, P - 1), (1, 0)):
                        sp.dma_start(row_pens_out[way].rearrange("(c s) -> s c", c=NCH).unsqueeze(2),
                                     border_rows[0:CH, :, 2 + way, e:e + 1]).then_inc(borders_out, 16)
                sp.wait_ge(borders_out, 48)
                for k in range(H1):
                    sp.dma_start(pens_raw[k:k + 1, :, :], row_pens_out.unsqueeze(0)).then_inc(pens_in, 16)
                sp.wait_ge(pens_in, 16 * H1)

            @block.vector
            def _(dve):
                dve.wait_ge(whole_in, 48)
                by_chunk = lambda t: t[0:CH, :].rearrange("s (c e) -> s c e", c=NCH)
                dve.tensor_tensor(border_rows[0:CH, :, 0, :], by_chunk(cur_d), by_chunk(prev_d), ALU.is_equal)
                link(dve, dve.tensor_tensor(border_rows[0:CH, :, 1, :], by_chunk(cur_d), by_chunk(next_d), ALU.is_equal))
                link(dve, dve.tensor_scalar(border_rows[0:CH, :, 0:2, :], border_rows[0:CH, :, 0:2, :], BIG, -BIG, ALU.mult, ALU.add))
                for c in range(NCH):
                    f, b = border_rows[0:CH, c, 0, :], border_rows[0:CH, c, 1, :][:, ::-1]
                    dve.tensor_tensor_scan(border_rows[0:CH, c, 2, :], f, f, 0.0, ALU.min, ALU.min)
                    last = dve.tensor_tensor_scan(border_rows[0:CH, c, 3, :][:, ::-1], b, b, 0.0, ALU.min, ALU.min)
                last.then_inc(border_set, 1)
                dve.wait_ge(pens_in, 16 * H1)
                dve.tensor_copy(row_pens[:, 0, :], pens_raw[:, 0, :])
                dve.tensor_copy(row_pens[:, 1, :], pens_raw[:, 1, ::-1])

        end_layer()
        def per_node(v):
            return v.unsqueeze(2).broadcast_to([P, NB, D])

        def per_feature(v):
            return v.unsqueeze(1).broadcast_to([P, NB, D])

        def standardise(dve, act_sync, of):
            to_act, from_act = act_sync
            mean, var, rec = small[:, 0, :], small[:, 1, :], small[:, 2, :]
            link(dve, dve.tensor_reduce(mean, of, AX.X, ALU.add))
            link(dve, dve.tensor_scalar(mean, mean, 1.0 / D, None, ALU.mult))
            link(dve, dve.tensor_tensor(hs[:], of, per_node(mean), ALU.subtract))
            link(dve, dve.tensor_tensor(tmp, hs[:], hs[:], ALU.mult))
            link(dve, dve.tensor_reduce(var, tmp, AX.X, ALU.add))
            dve.tensor_scalar(var, var, 1.0 / D, LN_EPS, ALU.mult, ALU.add).then_inc(to_act, 1)
            dve.wait_ge(from_act, 1)
            link(dve, dve.reciprocal(rec, var))
            link(dve, dve.tensor_tensor(hs[:], hs[:], per_node(rec), ALU.mult))

        def std_root(act, to_act, from_act):
            act.wait_ge(to_act, 1)
            act.activation(small[:, 1, :], small[:, 1, :], ACT.Sqrt).then_inc(from_act, 1)

        def turn_blocks(pe, source, ready, turned, kept, first=0):
            for b in range(NB):
                g = b // 4
                if b % 4 == 0:
                    pe.wait_ge(ready, first + 1)
                    if g >= 2:
                        pe.wait_ge(kept, g - 1)
                mm = pe.transpose(ps[:, g % 2, (b % 4) * P:(b % 4 + 1) * P], source[:, b, :], ident[:])
                if b % 4 == 3 or b == NB - 1:
                    mm.then_inc(turned, 1)

        def keep_blocks(act, target, turned, kept, scale=None):
            for g in range(-(-NB // 4)):
                n = min(4, NB - 4 * g)
                act.wait_ge(turned, g + 1)
                got = ps[:, g % 2, 0:n * P].rearrange("p (b f) -> p b f", f=P)
                act.activation(target[:, 4 * g:4 * g + n, :], got, ACT.Copy if scale is None else ACT.Identity,
                               scale=1.0 if scale is None else scale).then_inc(kept, 1)

        def scans(L, jobs):
            ends_ready = sem(f"L{L}_ends_ready")
            ends_turned = sem(f"L{L}_ends_turned")
            starts_ready = sem(f"L{L}_starts_ready")
            starts_turned = sem(f"L{L}_starts_turned")

            def run(dve, k, job, out, initial):
                K, source, draft, target, factor, frow, op0, op1, neutral, rev = job
                way = slice(None, None, -1) if rev else slice(None)
                return dve.tensor_tensor_scan(out[:, way], factor[:][:, way], source(k)[:, way], initial, op0, op1)

            with nc.Block() as block:
                @block.vector
                def _(dve):
                    for n, job in enumerate(jobs):
                        K, source, draft, target, factor, frow, op0, op1, neutral, rev = job
                        for k in range(K):
                            link(dve, run(dve, k, job, draft(k), neutral))
                            end = draft(k)[:, 0:1] if rev else draft(k)[:, EC - 1:EC]
                            last = dve.tensor_copy(carry_col[:, n, k:k + 1], end)
                        last.then_inc(ends_ready, 1)
                    for n, job in enumerate(jobs):
                        K, source, draft, target, factor, frow, op0, op1, neutral, rev = job
                        dve.wait_ge(ends_turned, n + 1)
                        ends = carry_row[0:K, 3, 0:P]
                        link(dve, dve.tensor_copy(ends, ps[0:K, n, 0:P]))
                        if rev:
                            dve.memset(carry_row[0:K, 4 + n, P:P + 1], neutral)
                            link(dve, dve.tensor_tensor_scan(carry_row[0:K, 4 + n, 0:P][:, ::-1], carry_row[0:K, frow, 0:P][:, ::-1],
                                                             ends[:, ::-1], neutral, op0, op1))
                        else:
                            dve.memset(carry_row[0:K, 4 + n, 0:1], neutral)
                            link(dve, dve.tensor_tensor_scan(carry_row[0:K, 4 + n, 1:P + 1], carry_row[0:K, frow, 0:P],
                                                             ends, neutral, op0, op1))
                        dve.sem_inc(starts_ready, 1)
                    for n, job in enumerate(jobs):
                        K, source, draft, target, factor, frow, op0, op1, neutral, rev = job
                        dve.wait_ge(starts_turned, n + 1)
                        link(dve, dve.tensor_copy(carry_col[:, 2 + n, 0:K], ps[:, 2 + n, 0:K]))
                        for k in range(K):
                            link(dve, run(dve, k, job, target(k), carry_col[:, 2 + n, k:k + 1]))

                @block.tensor
                def _(pe):
                    for n, job in enumerate(jobs):
                        K = job[0]
                        pe.wait_ge(ends_ready, n + 1)
                        pe.transpose(ps[0:K, n, 0:P], carry_col[:, n, 0:K], ident[:]).then_inc(ends_turned, 1)
                    for n, job in enumerate(jobs):
                        K, rev = job[0], job[-1]
                        pe.wait_ge(starts_ready, n + 1)
                        starts = carry_row[0:K, 4 + n, 1:P + 1] if rev else carry_row[0:K, 4 + n, 0:P]
                        pe.transpose(ps[:, 2 + n, 0:K], starts, ident[0:K, 0:K]).then_inc(starts_turned, 1)

        def copy_down(L, K):
            scans(f"{L}c", [(K, lambda k: DB[:, :, k], lambda k: A1[:, k * EC:(k + 1) * EC], lambda k: DB[:, :, k],
                             keep_f, 0, ALU.mult, ALU.add, 0.0, False)])

        def to_steps(L, K):
            out_done = sem(f"L{L}_edge_rows_out")
            chunk_in = [sem(f"L{L}_chunk_in{c}") for c in range(NCH)]
            chunk_turned = sem(f"L{L}_chunk_turned")
            chunk_kept = sem(f"L{L}_chunk_kept")
            rows = A1[:, 0:NCH * P * KW].rearrange("p (c e k) -> p c e k", c=NCH, k=KW)
            with nc.Block() as block:
                @block.sync
                def _(sp):
                    sp.dma_start(edge_rows.rearrange("a b -> (a b)").rearrange("(p c) -> p c", p=P),
                                 SE.rearrange("p c k -> p (c k)")).then_inc(out_done, 16)
                    sp.wait_ge(out_done, 16)

                @block.gpsimd
                def _(pool):
                    pool.wait_ge(out_done, 16)
                    for c in range(NCH):
                        pool.indirect_dma_start(rows[0:CH, c, :, :].rearrange("p e k -> p (e k)"), None, edge_rows,
                                                bass.IndirectOffsetOnAxis(ap=tile_i[0:CH, c:c + 1], axis=0)).then_inc(chunk_in[c], 16)

                @block.tensor
                def _(pe):
                    for c in range(NCH):
                        pe.wait_ge(chunk_in[c], 16)
                        if c >= 2:
                            pe.wait_ge(chunk_kept, c - 1)
                        for k in range(K):
                            mm = pe.transpose(ps[:, (c % 2) * 2 + k // 4, (k % 4) * CH:(k % 4 + 1) * CH], rows[0:CH, c, :, k],
                                              ident[0:CH, 0:CH])
                        mm.then_inc(chunk_turned, 1)

                @block.vector
                def _(dve):
                    for c in range(NCH):
                        dve.wait_ge(chunk_turned, c + 1)
                        for g in range(-(-K // 4)):
                            n = min(4, K - 4 * g)
                            last = dve.tensor_copy(WS[:, c * CH:(c + 1) * CH, 4 * g:4 * g + n],
                                                   ps[:, (c % 2) * 2 + g, 0:n * CH].rearrange("p (k s) -> p s k", k=n))
                        last.then_inc(chunk_kept, 1)

        def row_pass(L, W):
            table = tables[L]
            width = table.shape[1]
            K = (1, H1, 0, H3)[L]
            HANDS = BODY // HAND
            BODIES = STEPS // BODY
            GPH = HAND // GROUP
            TURNS = {0: 5, 1: 5, 2: 0, 3: 2}[L]
            LINKS = {0: 6, 1: 9, 2: 0, 3: 3}[L]
            rows_in = [[sem(f"L{L}_rows_in{q}{h}") for h in range(HANDS)] for q in range(2)]
            borders_in = [sem(f"L{L}_borders_in{q}") for q in range(2)]
            idx_copied = sem(f"L{L}_idx_copied")
            rows_used = sem(f"L{L}_rows_used")
            dve_rows = sem(f"L{L}_dve_rows")
            extras_ready = sem(f"L{L}_extras_ready")
            hot_ready = sem(f"L{L}_hot_ready")
            multiplied = sem(f"L{L}_multiplied")
            flushed = sem(f"L{L}_flushed")
            given = sem(f"L{L}_given")
            turned = sem(f"L{L}_turned")
            prep_chain = sem(f"L{L}_prep_chain")
            shifted_ready = sem(f"L{L}_shifted_ready")
            exponent_ready = sem(f"L{L}_exponent_ready")
            weights_ready = sem(f"L{L}_weights_ready")
            factor_ready = sem(f"L{L}_factor_ready")
            extras_copied = sem(f"L{L}_extras_copied")
            acc_scaled = sem(f"L{L}_acc_scaled")
            pool_turns = sem(f"L{L}_pool_turns")
            act_turns = sem(f"L{L}_act_turns")
            pe_turns = sem(f"L{L}_pe_turns")
            acc = A1[:, 0:NB * W].rearrange("p (b w) -> p b w", w=W)
            ring = [gath, A2[:, 0:BODY * RW].rearrange("p (s w) -> p s w", w=RW)]
            nmul = {0: D, 1: H1 * D, 2: 0, 3: D}[L]

            def loop(eng, body):
                with eng.Fori(0, BODIES // 2 - 1) as u:
                    for q in range(2):
                        body(u * 2 + q, q, False)
                for q in range(2):
                    body(BODIES - 2 + q, q, q == 1)

            with nc.Block() as block:
                @block.gpsimd
                def _(pool):
                    def body(i, q, last):
                        pool.wait_ge(idx_copied, i + 1)
                        pool.sem_inc(pool_turns, 1)
                        for h in range(HANDS):
                            if L == 2:
                                pool.wait_ge(flushed, i * (HANDS * GPH) + (h + 1) * GPH)
                            else:
                                pool.wait_ge(rows_used, i * HANDS + h + 1)
                            pool.sem_inc(pool_turns, 1)
                            if L == 1:
                                pool.wait_ge(dve_rows, i * HANDS + h + 1)
                                pool.sem_inc(pool_turns, 1)
                            for j in range(HAND):
                                s = h * HAND + j
                                pool.indirect_dma_start(ring[q][:, s, 0:width], None, table,
                                                        bass.IndirectOffsetOnAxis(ap=idx_ring[:, q, s:s + 1], axis=0)).then_inc(rows_in[q][h], 16)
                    loop(pool, body)

                @block.sync
                def _(sp):
                    if L > 1:
                        return
                    def load(i, q):
                        sp.dma_start(borders[:, q, :, :].rearrange("s a e -> s (a e)"), runs[bass.ds(i * BODY, BODY), :]).then_inc(borders_in[q], 16)
                    for q in range(2):
                        sp.dma_start(borders[:, q, :, :].rearrange("s a e -> s (a e)"), runs[q * BODY:(q + 1) * BODY, :]).then_inc(borders_in[q], 16)
                    with sp.Fori(0, BODIES // 2 - 1) as u:
                        for q in range(2):
                            sp.wait_ge(given, (u * 2 + q) * TURNS + 4)
                            load(u * 2 + q + 2, q)
                    for q in range(2):
                        sp.wait_ge(borders_in[q], 16 * (BODIES // 2))

                @block.scalar
                def _(act):
                    act.copy(idx_ring[:].rearrange("p a b -> p (a b)"), idx_step[:, 0:2 * BODY]).then_inc(idx_copied, 2)
                    if L < 2:
                        act.sem_inc(rows_used, 2 * HANDS)
                    if L == 3:
                        act.sem_inc(extras_ready, 1)

                    def body(i, q, last):
                        if L == 2:
                            for h in range(HANDS):
                                act.wait_ge(rows_in[q][h], (i + 2 - q) * (8 * HAND))
                                act.sem_inc(act_turns, 1)
                        if L < 2:
                            act.wait_ge(shifted_ready, i + 1)
                            act.sem_inc(act_turns, 1)
                            act.wait_ge(rows_used, i * HANDS + 2 * HANDS)
                            act.sem_inc(act_turns, 1)
                            if L == 1:
                                act.wait_ge(dve_rows, i * HANDS + 2 * HANDS)
                                act.sem_inc(act_turns, 1)
                            n = 2 * H1 if L == 1 else 1
                            act.activation(weights[:, :, 0:n], shifted[:, :, 0:n], ACT.Exp).then_inc(weights_ready, 1)
                            act.wait_ge(exponent_ready, i + 1)
                            act.sem_inc(act_turns, 1)
                            act.activation(rescale[:, 1, 0:K], rescale[:, 0, 0:K], ACT.Exp).then_inc(factor_ready, 1)
                            act.wait_ge(weights_ready, i + 1)
                            act.sem_inc(act_turns, 1)
                            if L == 0:
                                act.copy(weights[:, :, 1:5], WS[:, bass.ds(i * BODY, BODY), 1:5]).then_inc(extras_copied, 1)
                                act.wait_ge(extras_copied, i + 1)
                                act.sem_inc(act_turns, 1)
                        if L == 3:
                            act.wait_ge(shifted_ready, i + 1)
                            act.sem_inc(act_turns, 1)
                            act.activation(rescale[:, 1, 0:1], rescale[:, 0, 0:1], ACT.Exp).then_inc(factor_ready, 1)
                            act.wait_ge(rows_used, i * HANDS + 2 * HANDS)
                            act.sem_inc(act_turns, 1)
                            act.wait_ge(extras_ready, i * HANDS + 1)
                            act.sem_inc(act_turns, 1)
                            act.activation(weights[:], scores[:], ACT.Exp, bias=rescale[:, 2, 0:1]).then_inc(weights_ready, 1)
                            act.wait_ge(weights_ready, i + 1)
                            act.sem_inc(act_turns, 1)
                        act.copy(idx_ring[:, q, :], idx_step[:, bass.ds(i * BODY + 2 * BODY, BODY)] if not isinstance(i, int) else
                                 idx_step[:, min(i + 2, BODIES) * BODY:min(i + 2, BODIES) * BODY + BODY]).then_inc(idx_copied, 1)
                        if L == 2:
                            return
                        for h in range(HANDS):
                            act.wait_ge(multiplied, i * HANDS + h + 1)
                            act.sem_inc(act_turns, 1)
                            slot = (h % DEPTH) * HAND
                            act_last = act.copy(weighted[:, slot:slot + HAND, nmul:W], weights[:, h * HAND:(h + 1) * HAND, 0:W - nmul])
                            if L == 3:
                                act_last.then_inc(extras_ready, 1)
                                continue
                            for j in range(HAND):
                                for k in range(1 if L == 0 else H1 - 1):
                                    s = h * HAND + j
                                    act_last = act.activation(weighted[:, slot + j, k * D:(k + 1) * D], ring[q][:, s, 0:D], ACT.Copy,
                                                              scale=weights[:, s, k:k + 1])
                            act_last.then_inc(rows_used, 1)
                    loop(act, body)

                @block.vector
                def _(dve):
                    link(dve, dve.memset(A1[:, 0:NB * W], 0.0))
                    if L < 2:
                        dve.memset(row_f[0:K, 0:BODY + 1], -BIG)
                        dve.memset(row_b[0:K, 0:BODY + 1], -BIG)
                        link(dve, dve.memset(last_max[:], -BIG))
                    if L == 1:
                        dve.sem_inc(dve_rows, 2 * HANDS)
                    if L == 3:
                        dve.sem_inc(rows_used, 2 * HANDS)
                        link(dve, dve.memset(carry_row[0:1, 3, 0:2], -BIG))

                    chain = [0]

                    def tie(i, ins):
                        chain[0] += 1
                        ins.then_inc(prep_chain, 1)
                        dve.wait_ge(prep_chain, i * LINKS + chain[0])

                    def hot(i, h):
                        dve.wait_ge(multiplied, i * HANDS + h + 1)
                        for j in range(HAND):
                            col = i * BODY + h * HAND + j
                            col = dst_step[:, col:col + 1] if isinstance(i, int) else dst_step[:, bass.ds(col, 1)]
                            last = dve.tensor_scalar(onehot[:, (h % DEPTH) * HAND + j, :], iota_row[:], col, None, ALU.is_equal)
                        last.then_inc(hot_ready, 1)

                    def steps_of(i, k0, k1):
                        return WS[:, i * BODY:(i + 1) * BODY, k0:k1] if isinstance(i, int) else WS[:, bass.ds(i * BODY, BODY), k0:k1]

                    def rows_landed(i, q):
                        for h in range(HANDS):
                            dve.wait_ge(rows_in[q][h], (i + 2 - q) * (8 * HAND))

                    def score(i, q):
                        rows_landed(i, q)
                        chain[0] = 0
                        if L == 0:
                            dve.tensor_copy(topped[:, :, 0:1], ring[q][:, :, D:D + 1]).then_inc(given, 1)
                            return
                        s = scores[:, :, 0:H1]
                        tie(i, dve.tensor_tensor(s, ring[q][:, :, D:D + H1], steps_of(i, 0, H1), ALU.add))
                        tie(i, dve.scalar_tensor_tensor(out=s, in0=s, scalar=0.2, in1=s, op0=ALU.mult, op1=ALU.max))
                        dve.tensor_tensor(topped[:], s, steps_of(i, H1, 2 * H1), ALU.max).then_inc(given, 1)

                    def run_maxima(i, q):
                        dve.wait_ge(borders_in[q], (i + 2 - q) * 8)
                        dve.wait_ge(turned, i * TURNS + 1)
                        for k in range(K):
                            v = ps[0:BODY, 4, k * P:(k + 1) * P]
                            dve.tensor_tensor_scan(run_f[:, k, :], borders[:, q, 0, :], v, -BIG, ALU.add, ALU.max)
                            last = dve.tensor_tensor_scan(run_b[:, k, :][:, ::-1], borders[:, q, 1, :][:, ::-1], v[:, ::-1], -BIG, ALU.add, ALU.max)
                        last.then_inc(given, 1)

                    def step_maxima(i, q):
                        dve.wait_ge(turned, i * TURNS + 2)
                        tie(i, dve.tensor_copy(row_f[0:K, 0:1], row_f[0:K, BODY:BODY + 1]))
                        start, turn = i * BODY, (i * -BODY) + (STEPS - BODY)
                        if isinstance(i, int):
                            pens_f, pens_b = row_pens[0:K, 0, start:start + BODY], row_pens[0:K, 1, turn:turn + BODY]
                        else:
                            pens_f, pens_b = row_pens[0:K, 0, bass.ds(start, BODY)], row_pens[0:K, 1, bass.ds(turn, BODY)]
                        dve.tensor_tensor_scan(row_f[0:K, 1:BODY + 1], pens_f, ps[0:K, 5, 0:BODY], row_f[0:K, 0:1], ALU.add, ALU.max)
                        dve.tensor_tensor_scan(row_b[0:K, 0:BODY][:, ::-1], pens_b, ps[0:K, 5, BODY:2 * BODY][:, ::-1],
                                               -BIG, ALU.add, ALU.max).then_inc(given, 1)

                    def join(i, q):
                        dve.wait_ge(turned, i * TURNS + 3)
                        tie(i, dve.tensor_copy(row_col[:, :, 0:K], ps[0:BODY, 5, 64:64 + 2 * KW].rearrange("s (a k) -> s a k", a=2)[:, :, 0:K]))
                        for way in range(2):
                            for k in range(K):
                                ins = dve.scalar_tensor_tensor(out=run_f[:, k, :], in0=borders[:, q, 2 + way, :], scalar=row_col[:, way, k:k + 1],
                                                               in1=run_f[:, k, :], op0=ALU.add, op1=ALU.max)
                                if k == K - 1:
                                    tie(i, ins)
                        dve.tensor_tensor(run_f[:, 0:K, :], run_f[:, 0:K, :], run_b[:, 0:K, :], ALU.max).then_inc(given, 1)

                    def shift(i, q):
                        dve.wait_ge(turned, i * TURNS + 4)
                        got = ps[:, 6, 0:K * BODY].rearrange("p (k s) -> p s k", k=K)
                        dve.tensor_copy(edge_cols[:, 0, 0:K], got[:, 0, :])
                        first = dst_step[:, i * BODY:i * BODY + 1] if isinstance(i, int) else dst_step[:, bass.ds(i * BODY, 1)]
                        dve.tensor_copy(edge_cols[:, 0, K:K + 1], first)
                        dve.tensor_copy(edge_cols[:, 1, 0:K], got[:, BODY - 1, :]).then_inc(given, 1)
                        if L == 0:
                            dve.tensor_tensor(shifted[:, :, 0:1], topped[:, :, 0:1], got, ALU.subtract).then_inc(shifted_ready, 1)
                            return
                        dve.tensor_tensor(shifted[:, :, 0:H1], scores[:, :, 0:H1], got, ALU.subtract)
                        tie(i, dve.tensor_tensor(shifted[:, :, H1:2 * H1], steps_of(i, H1, 2 * H1), got, ALU.subtract))
                        dve.tensor_tensor(shifted[:, :, H1:2 * H1], shifted[:, :, H1:2 * H1],
                                          steps_of(i, 2 * H1, 2 * H1 + 1).broadcast_to([P, BODY, H1]), ALU.add).then_inc(shifted_ready, 1)

                    def exponent(i, q):
                        dve.wait_ge(turned, i * TURNS + 5)
                        dve.tensor_scalar(first_hot[:], ps[:, 7, K:K + 1], iota_p[:, 0:1], None, ALU.is_equal)
                        tie(i, dve.tensor_tensor(rescale[:, 0, 0:K], last_max[:, 0:K], ps[:, 7, 0:K], ALU.subtract))
                        dve.tensor_scalar(rescale[:, 0, 0:K], rescale[:, 0, 0:K], 0.0, None, ALU.min).then_inc(exponent_ready, 1)
                        tie(i, dve.tensor_copy(last_max[:, 0:K], ps[:, 7, 16:16 + K]))

                    def score3(i, q):
                        rows_landed(i, q)
                        chain[0] = 0
                        tie(i, dve.tensor_tensor(scores[:], ring[q][:, :, D:D + H3], steps_of(i, 0, H3), ALU.add))
                        tie(i, dve.scalar_tensor_tensor(out=scores[:], in0=scores[:], scalar=0.2, in1=scores[:], op0=ALU.mult, op1=ALU.max))
                        dve.tensor_reduce(last_max[:, 0:1], scores[:], AX.XY, ALU.max).then_inc(given, 1)

                    def top3(i, q):
                        dve.wait_ge(turned, i * TURNS + 1)
                        dve.tensor_copy(carry_row[0:1, 3, 1:2], carry_row[0:1, 3, 0:1])
                        tie(i, dve.tensor_reduce(carry_row[0:1, 3, 2:3], ps[0:1, 4, 0:P], AX.X, ALU.max))
                        dve.tensor_tensor(carry_row[0:1, 3, 0:1], carry_row[0:1, 3, 2:3], carry_row[0:1, 3, 1:2], ALU.max).then_inc(given, 1)

                    def shift3(i, q):
                        dve.wait_ge(turned, i * TURNS + 2)
                        dve.tensor_scalar(rescale[:, 2, 0:1], ps[:, 5, 0:1], -1.0, None, ALU.mult)
                        dve.tensor_copy(edge_cols[:, 0, 0:2], ps[:, 5, 0:2]).then_inc(acc_scaled, 1)
                        dve.wait_ge(acc_scaled, i * 2 + 1)
                        dve.tensor_tensor(rescale[:, 0, 0:1], edge_cols[:, 0, 1:2], edge_cols[:, 0, 0:1], ALU.subtract).then_inc(shifted_ready, 1)

                    stages = {0: {2: score, 3: run_maxima, 4: step_maxima, 5: join, 6: shift, 7: exponent},
                              2: {}, 3: {4: score3, 5: top3, 6: shift3}}
                    stages[1] = stages[0]

                    def scale_acc(i):
                        dve.wait_ge(factor_ready, i + 1)
                        if L == 3:
                            dve.wait_ge(flushed, (i + 2) * (HANDS * GPH))
                            dve.tensor_scalar(A1[:, 0:NB * W], A1[:, 0:NB * W], rescale[:, 1, 0:1], None, ALU.mult).then_inc(acc_scaled, 1)
                            return
                        dve.scalar_tensor_tensor(out=rescale[:, 2, 0:K], in0=rescale[:, 1, 0:K], scalar=-1.0,
                                                 in1=first_hot[:].broadcast_to([P, K]), op0=ALU.add, op1=ALU.mult).then_inc(acc_scaled, 1)
                        dve.wait_ge(acc_scaled, i * 3 + 1)
                        dve.tensor_scalar(rescale[:, 2, 0:K], rescale[:, 2, 0:K], 1.0, None, ALU.add).then_inc(acc_scaled, 1)
                        b = group_block(i, 0)
                        dve.wait_ge(acc_scaled, i * 3 + 2)
                        if L == 0:
                            a = acc[:, bass.ds(b, 1), 0:D + 1].rearrange("p o w -> p (o w)")
                            dve.wait_ge(flushed, (i + 2) * (HANDS * GPH))
                            dve.tensor_scalar(a, a, rescale[:, 2, 0:1], None, ALU.mult).then_inc(acc_scaled, 1)
                            return
                        dve.wait_ge(flushed, (i + 2) * (HANDS * GPH))
                        a = acc[:, bass.ds(b, 1), 0:H1 * D].rearrange("p o (k f) -> p (o k) f", k=H1)
                        dve.tensor_tensor(a, a, rescale[:, 2, 0:K].unsqueeze(2).broadcast_to([P, H1, D]), ALU.mult)
                        a = acc[:, bass.ds(b, 1), H1 * D:W].rearrange("p o (a k) -> p (o a) k", a=2)
                        dve.tensor_tensor(a, a, rescale[:, 2, 0:K].unsqueeze(1).broadcast_to([P, 2, H1]), ALU.mult).then_inc(acc_scaled, 1)

                    def group_block(i, g):
                        gg = i * (BODY // GROUP) + g
                        col = blk_reg[0:1, gg:gg + 1] if isinstance(gg, int) else blk_reg[0:1, bass.ds(gg, 1)]
                        return dve.value_load(col, min_val=0, max_val=NB - 1)

                    def weigh(i, q, h):
                        dve.wait_ge(multiplied, i * HANDS + h + 1)
                        for j in range(HAND):
                            s, slot = h * HAND + j, (h % DEPTH) * HAND + j
                            if L == 1:
                                ins = dve.tensor_scalar(weighted[:, slot, (H1 - 1) * D:H1 * D], ring[q][:, s, 0:D],
                                                        weights[:, s, H1 - 1:H1], None, ALU.mult)
                            else:
                                ins = dve.tensor_tensor(weighted[:, slot, 0:D].rearrange("p (k c) -> p k c", c=C3),
                                                        ring[q][:, s, 0:D].rearrange("p (k c) -> p k c", c=C3),
                                                        weights[:, s, :].unsqueeze(2).broadcast_to([P, H3, C3]), ALU.mult)
                        ins.then_inc(dve_rows if L == 1 else rows_used, 1)

                    def body(i, q, last):
                        if L in (1, 3):
                            dve.wait_ge(weights_ready, i + 1)
                            weigh(i, q, 0)
                        for h in range(HANDS):
                            if L in (1, 3) and h + 1 < HANDS:
                                weigh(i, q, h + 1)
                            hot(i, h + 1)
                            if h == 0 and L != 2:
                                scale_acc(i)
                            for g in range(GPH):
                                b = group_block(i, h * GPH + g)
                                a = acc[:, bass.ds(b, 1), :].rearrange("p o w -> p (o w)")
                                if g == 0:
                                    dve.wait_ge(multiplied, i * HANDS + h + 1 + DEPTH)
                                    if h == 0 and L != 2:
                                        dve.wait_ge(acc_scaled, (i + 1) * (2 if L == 3 else 3))
                                dve.wait_ge(flushed, i * (HANDS * GPH) + h * GPH + g + 2 * HANDS * GPH)
                                dve.tensor_tensor(a, a, ps[:, (h % DEPTH) * GPH + g, 0:W], ALU.add).then_inc(flushed, 1)
                            if h in stages[L] and not last:
                                stages[L][h](i + 1, 1 - q)

                    hot(0, 0)
                    for h in sorted(stages[L]):
                        stages[L][h](0, 0)
                    loop(dve, body)

                @block.tensor
                def _(pe):
                    pe.sem_inc(multiplied, DEPTH)
                    pe.sem_inc(flushed, 2 * HANDS * GPH)

                    def after(i, n):
                        pe.wait_ge(given, i * TURNS + n)
                        pe.sem_inc(pe_turns, 1)

                    def turn_scores(i, q):
                        after(i, 1)
                        for k in range(K):
                            mm = pe.transpose(ps[0:BODY, 4, k * P:(k + 1) * P], topped[:, :, k], ident[:])
                        mm.then_inc(turned, 1)

                    def turn_ends(i, q):
                        after(i, 2)
                        pe.transpose(ps[0:K, 5, 0:BODY], run_f[:, 0:K, P - 1], ident[0:BODY, 0:BODY])
                        pe.transpose(ps[0:K, 5, BODY:2 * BODY], run_b[:, 0:K, 0], ident[0:BODY, 0:BODY]).then_inc(turned, 1)

                    def turn_rows(i, q):
                        after(i, 3)
                        pe.transpose(ps[0:BODY, 5, 64:64 + K], row_f[0:K, 0:BODY], ident[0:K, 0:K])
                        pe.transpose(ps[0:BODY, 5, 64 + KW:64 + KW + K], row_b[0:K, 1:BODY + 1], ident[0:K, 0:K]).then_inc(turned, 1)

                    def turn_back(i, q):
                        after(i, 4)
                        for k in range(K):
                            mm = pe.transpose(ps[:, 6, k * BODY:(k + 1) * BODY], run_f[:, k, :], ident[0:BODY, 0:BODY])
                        mm.then_inc(turned, 1)

                    def spread(i, q):
                        after(i, 5)
                        pe.matmul(ps[:, 7, 0:K + 1], pick_first[:], edge_cols[:, 0, 0:K + 1], start=True, stop=True)
                        pe.matmul(ps[:, 7, 16:16 + K], pick_last[:], edge_cols[:, 1, 0:K], start=True, stop=True).then_inc(turned, 1)

                    def turn_top3(i, q):
                        after(i, 1)
                        pe.transpose(ps[0:1, 4, 0:P], last_max[:, 0:1], ident[:]).then_inc(turned, 1)

                    def spread3(i, q):
                        after(i, 2)
                        pe.matmul(ps[:, 5, 0:2], ones[0:1, :], carry_row[0:1, 3, 0:2], start=True, stop=True).then_inc(turned, 1)

                    stages = {0: {3: turn_scores, 4: turn_ends, 5: turn_rows, 6: turn_back, 7: spread},
                              2: {}, 3: {5: turn_top3, 6: spread3}}
                    stages[1] = stages[0]

                    def body(i, q, last):
                        for h in range(HANDS):
                            pe.wait_ge(hot_ready, i * HANDS + h + 1)
                            if L == 2:
                                pe.wait_ge(rows_in[q][h], (i + 2 - q) * (8 * HAND))
                            else:
                                pe.wait_ge(rows_used, i * HANDS + h + 1 + 2 * HANDS)
                            if L == 1:
                                pe.wait_ge(dve_rows, i * HANDS + h + 1 + 2 * HANDS)
                            if L == 3:
                                pe.wait_ge(extras_ready, i * HANDS + h + 2)
                            for j in range(HAND):
                                s = (h % DEPTH) * HAND + j
                                rhs = ring[q][:, h * HAND + j, 0:D] if L == 2 else weighted[:, s, 0:W]
                                mm = pe.matmul(ps[:, (h % DEPTH) * GPH + j // GROUP, 0:W], onehot[:, s, :], rhs,
                                               start=(j % GROUP == 0), stop=(j % GROUP == GROUP - 1))
                            mm.then_inc(multiplied, 1)
                            if h in stages[L] and not last:
                                stages[L][h](i + 1, 1 - q)

                    for h in sorted(stages[L]):
                        stages[L][h](0, 0)
                    loop(pe, body)
            return acc

        def node_products(pe, lhs, rhs, width, ready, done, per_bank=4):
            pe.wait_ge(*ready)
            for b in range(NB):
                mm = pe.matmul(ps[:, 2 + b // per_bank, (b % per_bank) * width:(b % per_bank + 1) * width], lhs[:, b, :], rhs, start=True, stop=True)
            mm.then_inc(done, 1)

        TG = -(-NB // 4)

        def wide_products(pe, lhs, rhs, kept, done, used):
            for b in range(NB):
                g = b // 4
                if b % 4 == 0:
                    pe.wait_ge(kept, TG)
                    if g >= 2:
                        pe.wait_ge(used, g - 1)
                mm = pe.matmul(ps[:, 2 + g % 2, (b % 4) * P:(b % 4 + 1) * P], lhs[:, b, :], rhs, start=True, stop=True)
                if b % 4 == 3 or b == NB - 1:
                    mm.then_inc(done, 1)

        def bank_squares(g):
            n = min(4, NB - 4 * g)
            return slice(4 * g, 4 * g + n), ps[:, 2 + g % 2, 0:n * P].rearrange("p (b f) -> p b f", f=P)

        def write_table(sp, L, source, ready, out_done):
            sp.wait_ge(*ready)
            sp.dma_start(tables[L].rearrange("(b p) w -> p b w", p=P), source).then_inc(out_done, 16)
            sp.wait_ge(out_done, 16)

        wT = wbuf[:, 0:P]
        mask_col = ve_col[:, 3:4]
        attn_bc = bias_row
        a0_in, a0_root, a0_rooted, a0_norm = sem("a0_in"), sem("a0_root"), sem("a0_rooted"), sem("a0_norm")
        a0_turned, a0_kept, a0_done, a0_used = sem("a0_turned"), sem("a0_kept"), sem("a0_done"), sem("a0_used")
        a0_wt, a0_wk, a0_table, a0_scored = sem("a0_wt"), sem("a0_wk"), sem("a0_table"), sem("a0_scored")
        with nc.Block() as block:
            @block.sync
            def _(sp):
                sp.dma_start(wnat[:, 0:P], L0_W).then_inc(a0_in, 16)
                with nc.allow_non_contiguous_dma("one column"):
                    sp.dma_start(mask_col, L0_mask.unsqueeze(1)).then_inc(a0_in, 16)
                sp.dma_start(attn_bc[:], L0_attn.unsqueeze(0).broadcast_to([P, D])).then_inc(a0_in, 16)
                write_table(sp, 0, tab[:, :, 0:D + 1], (a0_scored, 1), a0_table)

            @block.vector
            def _(dve):
                standardise(dve, (a0_root, a0_rooted), xs[:])
                dve.tensor_scalar(hs[:], hs[:], 0.0, None, ALU.max).then_inc(a0_norm, 1)
                dve.wait_ge(a0_wt, 1)
                dve.tensor_copy(wT, ps[:, 4, 0:P]).then_inc(a0_wk, 1)
                for g in range(TG):
                    bs, got = bank_squares(g)
                    dve.wait_ge(a0_done, g + 1)
                    dve.tensor_copy(hW[:, bs, :], got).then_inc(a0_used, 1)
                dve.wait_ge(a0_used, TG)
                dve.wait_ge(a0_in, 48)
                link(dve, dve.tensor_tensor(tmp, hW, per_feature(attn_bc[:]), ALU.mult))
                link(dve, dve.tensor_reduce(scal[:, 0, :], tmp, AX.X, ALU.add))
                dve.scalar_tensor_tensor(out=tab[:, :, D], in0=scal[:, 0, :], scalar=0.01, in1=scal[:, 0, :],
                                         op0=ALU.mult, op1=ALU.max).then_inc(a0_scored, 1)

            @block.scalar
            def _(act):
                std_root(act, a0_root, a0_rooted)
                act.wait_ge(a0_in, 48)
                keep_blocks(act, hT, a0_turned, a0_kept, scale=mask_col)

            @block.tensor
            def _(pe):
                pe.wait_ge(a0_in, 48)
                pe.transpose(ps[:, 4, 0:P], wnat[:, 0:P], ident[:]).then_inc(a0_wt, 1)
                turn_blocks(pe, hs, a0_norm, a0_turned, a0_kept)
                pe.wait_ge(a0_wk, 1)
                wide_products(pe, hT, wT, a0_kept, a0_done, a0_used)

        with nc.Block() as block:
            @block.vector
            def _(dve):
                dve.memset(SE[:, :, 0:1], 0.0)
                dve.tensor_copy(SE[:, :, 1:1 + H1], a_edge[:])
                dve.memset(SE[:, :, 4:5], 1.0)
                dve.memset(SE[:, :, 5:KW], 0.0)

        to_steps(0, 5)
        acc = row_pass(0, D + 5)

        loop_score = sb("loop_score", [P, H1, NB])
        f0_ready, f0_done, f0_blocks = sem("f0_ready"), sem("f0_done"), sem("f0_blocks")
        with nc.Block() as block:
            @block.vector
            def _(dve):
                den, rec = small[:, 0, :], small[:, 1, :]
                dve.tensor_copy(deg[:], acc[:, :, D + 4])
                link(dve, dve.tensor_scalar(den, acc[:, :, D], 0.5, None, ALU.max))
                link(dve, dve.reciprocal(rec, den))
                link(dve, dve.tensor_tensor(hs[:], acc[:, :, 0:D], per_node(rec), ALU.mult))
                link(dve, dve.scalar_tensor_tensor(out=xs[:], in0=hs[:], scalar=0.0, in1=xs[:], op0=ALU.max, op1=ALU.add))
                link(dve, dve.tensor_scalar(den, deg[:], 1.0, None, ALU.max))
                link(dve, dve.reciprocal(rec, den))
                for k in range(H1):
                    dve.tensor_tensor(loop_score[:, k, :], acc[:, :, D + 1 + k], rec, ALU.mult)
                dve.wait_ge(f0_done, 1)
                totals, upto, node_no, first = small[:, 2, :], small[:, 3, :], small[:, 4, :], small[:, 5, :]
                link(dve, dve.tensor_copy(totals, ps[:, 1, 0:NB]))
                link(dve, dve.tensor_tensor_scan(upto, ones[:, 0:NB], totals, 0.0, ALU.mult, ALU.add))
                link(dve, dve.tensor_tensor(upto, upto, totals, ALU.subtract))
                link(dve, dve.tensor_tensor(first, upto, ps[:, 0, 0:NB], ALU.add))
                link(dve, dve.tensor_scalar(node_no, iota_hi[:], float(P), iota_p[:, 0:1], ALU.mult, ALU.add))
                link(dve, dve.tensor_scalar(node_no, node_no, float(EP), None, ALU.add))
                link(dve, dve.tensor_tensor(node_no, node_no, first, ALU.subtract))
                link(dve, dve.tensor_scalar(den, deg[:], 0.0, None, ALU.is_equal))
                link(dve, dve.tensor_tensor(node_no, node_no, den, ALU.mult))
                link(dve, dve.tensor_tensor(seed_idx[:], node_no, first, ALU.add))

            @block.tensor
            def _(pe):
                pe.matmul(ps[:, 0, 0:NB], tri[:], acc[:, :, D + 4], start=True, stop=True)
                pe.matmul(ps[:, 1, 0:NB], ones[:], acc[:, :, D + 4], start=True, stop=True).then_inc(f0_done, 1)

        def scatter_seeds(pool, done):
            for b in range(NB):
                pool.indirect_dma_start(seeds, bass.IndirectOffsetOnAxis(ap=seed_idx[:, b:b + 1], axis=0),
                                        seed_vals[:, b, :], None).then_inc(done, 16)
            pool.wait_ge(done, 16 * NB)

        end_layer()

        U = wbuf[:, 1152 - 2 * H1:1152]
        att_bc = A2[:, 1024:1024 + 2 * 384]
        u_prods = A2[:, 2048:2048 + 768]
        a1_in, a1_root, a1_rooted, a1_norm = sem("a1_in"), sem("a1_root"), sem("a1_rooted"), sem("a1_norm")
        a1_turned, a1_kept, a1_done = sem("a1_turned"), sem("a1_kept"), sem("a1_done")
        a1_u, a1_seed, a1_seeded, a1_table = sem("a1_u"), sem("a1_seed"), sem("a1_seeded"), sem("a1_table")
        with nc.Block() as block:
            @block.sync
            def _(sp):
                sp.dma_start(wnat[:], L1_W).then_inc(a1_in, 16)
                sp.dma_start(att_bc[:, 0:384], L1_as.rearrange("h c -> (h c)").unsqueeze(0).broadcast_to([P, 384])).then_inc(a1_in, 16)
                sp.dma_start(att_bc[:, 384:768], L1_ad.rearrange("h c -> (h c)").unsqueeze(0).broadcast_to([P, 384])).then_inc(a1_in, 16)
                write_table(sp, 1, tab[:, :, 0:D + H1], (a1_seed, 1), a1_table)

            @block.gpsimd
            def _(pool):
                pool.wait_ge(a1_seed, 1)
                scatter_seeds(pool, a1_seeded)

            @block.vector
            def _(dve):
                dve.memset(A2[:, 0:NB * KW], 0.0)
                standardise(dve, (a1_root, a1_rooted), xs[:])
                dve.tensor_scalar(hs[:], hs[:], 0.0, None, ALU.max).then_inc(a1_norm, 1)
                dve.wait_ge(a1_norm, 1)
                dve.tensor_copy(tab[:, :, 0:D], hs[:])
                dve.wait_ge(a1_in, 48)
                for k in range(2):
                    u_prod = u_prods[:, k * 384:(k + 1) * 384]
                    link(dve, dve.tensor_tensor(u_prod, wnat[:], att_bc[:, k * 384:(k + 1) * 384], ALU.mult))
                    last = dve.tensor_reduce(U[:, k * H1:(k + 1) * H1], u_prod.rearrange("p (h c) -> p h c", c=D), AX.X, ALU.add)
                last.then_inc(a1_u, 1)
                dve.wait_ge(a1_done, 1)
                got = ps[:, 2, 0:NB * 2 * H1].rearrange("p (b k) -> p k b", k=2 * H1)
                link(dve, dve.tensor_copy(scal[:, 0:2 * H1, :], got))
                dve.tensor_copy(tab[:, :, D:D + H1].rearrange("p b k -> p k b"), scal[:, 0:H1, :])
                dve.tensor_copy(seed_vals[:, :, 0:H1].rearrange("p b k -> p k b"), scal[:, H1:2 * H1, :])
                link(dve, dve.tensor_tensor(loop_score[:], loop_score[:], scal[:, 0:H1, :], ALU.add))
                link(dve, dve.tensor_tensor(loop_score[:], loop_score[:], scal[:, H1:2 * H1, :], ALU.add))
                dve.scalar_tensor_tensor(out=seed_vals[:, :, H1:2 * H1].rearrange("p b k -> p k b"), in0=loop_score[:], scalar=0.2,
                                         in1=loop_score[:], op0=ALU.mult, op1=ALU.max).then_inc(a1_seed, 1)

            @block.scalar
            def _(act):
                std_root(act, a1_root, a1_rooted)
                keep_blocks(act, hT, a1_turned, a1_kept)

            @block.tensor
            def _(pe):
                turn_blocks(pe, hs, a1_norm, a1_turned, a1_kept)
                pe.wait_ge(a1_kept, TG)
                node_products(pe, hT, U, 2 * H1, (a1_u, 1), a1_done, per_bank=NB)

        db1_in = sem("db1_in")
        with nc.Block() as block:
            @block.sync
            def _(sp):
                sp.dma_start(A3[:, 0:EC * KW], seeds_edges.rearrange("(p c) k -> p (c k)", p=P)).then_inc(db1_in, 16)
                sp.wait_ge(db1_in, 16)
        copy_down(1, 2 * H1)
        with nc.Block() as block:
            @block.vector
            def _(dve):
                dve.tensor_tensor(SE[:, :, 0:H1], DB[:, :, 0:H1], a_edge[:], ALU.add)
                dve.tensor_copy(SE[:, :, H1:2 * H1], DB[:, :, H1:2 * H1])
                dve.tensor_scalar(SE[:, :, 2 * H1], keep_f[:], -BIG, None, ALU.mult)
                dve.memset(SE[:, :, 2 * H1 + 1:KW], 0.0)

        to_steps(1, 2 * H1 + 1)
        acc = row_pass(1, H1 * D + 2 * H1)

        whT = A2[:, 0:384]
        lin = A2[:, 384:768]
        V = A2[:, 768:1152]
        gb_col = A2[:, 1152:1155]
        gb_wide = A2[:, 1280:1664]
        aggT = A2[:, 2048:2048 + 2 * 384]
        g_bc, b_bc, lb_bc = wnat[:, 0:D], wnat[:, D:2 * D], wnat[:, 2 * D:3 * D]
        f1_in, f1_late, f1_wt, f1_wk, f1_v, f1_vk = sem("f1_in"), sem("f1_late"), sem("f1_wt"), sem("f1_wk"), sem("f1_v"), sem("f1_vk")
        f1_mean, f1_turned, f1_kept, f1_y, f1_used = sem("f1_mean"), sem("f1_turned"), sem("f1_kept"), sem("f1_y"), sem("f1_used")
        f1_root, f1_rooted = sem("f1_root"), sem("f1_rooted")
        with nc.Block() as block:
            @block.sync
            def _(sp):
                sp.dma_start(lin.rearrange("p (h o) -> p h o", h=H1), L1_lW.rearrange("(h c) o -> c h o", h=H1)).then_inc(f1_in, 16)
                with nc.allow_non_contiguous_dma("three columns"):
                    sp.dma_start(gb_col.unsqueeze(2), L1_gb.rearrange("(h c) -> c h", h=H1).unsqueeze(2)).then_inc(f1_in, 16)
                sp.wait_ge(f1_wt, 1)
                for row, v in ((g_bc, L1_g), (b_bc, L1_b), (lb_bc, L1_lb)):
                    sp.dma_start(row, v.unsqueeze(0).broadcast_to([P, D])).then_inc(f1_late, 16)
                sp.wait_ge(f1_late, 48)

            @block.vector
            def _(dve):
                none, den, rec = small[:, 0, :], small[:, 1, :], small[:, 2, :]
                link(dve, dve.tensor_scalar(none, deg[:], 0.0, None, ALU.is_equal))
                for k in range(H1):
                    wl = small[:, 3 + k, :]
                    link(dve, dve.tensor_tensor(wl, acc[:, :, H1 * D + H1 + k], none, ALU.add))
                    link(dve, dve.tensor_tensor(den, acc[:, :, H1 * D + k], wl, ALU.add))
                    link(dve, dve.reciprocal(rec, den))
                    link(dve, dve.tensor_tensor(wl, wl, rec, ALU.mult))
                    mean = acc[:, :, k * D:(k + 1) * D]
                    link(dve, dve.tensor_tensor(mean, mean, per_node(rec), ALU.mult))
                    for b in range(NB):
                        last = dve.scalar_tensor_tensor(out=mean[:, b, :], in0=hs[:, b, :], scalar=wl[:, b:b + 1], in1=mean[:, b, :],
                                                        op0=ALU.mult, op1=ALU.add)
                    last.then_inc(f1_mean, 1)
                dve.wait_ge(f1_wt, 1)
                dve.tensor_copy(whT, ps[:, 7, 0:384])
                dve.wait_ge(f1_in, 32)
                dve.tensor_copy(gb_wide.rearrange("p (h m) -> p h m", h=H1), gb_col.unsqueeze(2).broadcast_to([P, H1, P])).then_inc(f1_wk, 1)
                dve.wait_ge(f1_v, 1)
                dve.tensor_copy(V, ps[:, 6, 0:384])
                dve.wait_ge(f1_late, 48)
                dve.tensor_tensor(bias_row[:], lb_bc, ps[:, 5, 0:D], ALU.add).then_inc(f1_vk, 1)
                dve.wait_ge(f1_vk, 1)
                for b in range(NB):
                    dve.wait_ge(f1_y, b + 1)
                    link(dve, dve.tensor_tensor(hs[:, b, :], hs[:, b, :], ps[:, 2 + b % 2, 0:D], ALU.add))
                    dve.tensor_tensor(hs[:, b, :], hs[:, b, :], bias_row[:], ALU.add).then_inc(f1_used, 1)
                dve.wait_ge(f1_used, NB)
                standardise(dve, (f1_root, f1_rooted), hs[:])
                link(dve, dve.tensor_tensor(hs[:], hs[:], per_feature(g_bc), ALU.mult))
                link(dve, dve.tensor_tensor(hs[:], hs[:], per_feature(b_bc), ALU.add))
                dve.tensor_tensor(xs[:], xs[:], hs[:], ALU.add)

            @block.scalar
            def _(act):
                for b in range(NB):
                    act.wait_ge(f1_turned, b + 1)
                    if b >= 2:
                        act.wait_ge(f1_y, b - 1)
                    act.copy(aggT[:, (b % 2) * 384:(b % 2 + 1) * 384], ps[:, b % 2, 0:384]).then_inc(f1_kept, 1)
                std_root(act, f1_root, f1_rooted)

            @block.tensor
            def _(pe):
                for k in range(H1):
                    mm = pe.transpose(ps[:, 7, k * P:(k + 1) * P], wnat[:, k * P:(k + 1) * P], ident[:])
                mm.then_inc(f1_wt, 1)
                pe.wait_ge(f1_wk, 1)
                for k in range(H1):
                    pe.matmul(ps[:, 6, k * P:(k + 1) * P], whT[:, k * P:(k + 1) * P], lin[:, k * P:(k + 1) * P], start=True, stop=True)
                for k in range(H1):
                    mm = pe.matmul(ps[:, 5, 0:P], gb_wide[:, k * P:(k + 1) * P], lin[:, k * P:(k + 1) * P], start=(k == 0), stop=(k == H1 - 1))
                mm.then_inc(f1_v, 1)
                pe.wait_ge(f1_mean, H1)
                pe.wait_ge(f1_vk, 1)

                def turn(b):
                    if b >= 2:
                        pe.wait_ge(f1_kept, b - 1)
                    for k in range(H1):
                        mm = pe.transpose(ps[:, b % 2, k * P:(k + 1) * P], acc[:, b, k * P:(k + 1) * P], ident[:])
                    mm.then_inc(f1_turned, 1)

                turn(0)
                for b in range(NB):
                    if b + 1 < NB:
                        turn(b + 1)
                    pe.wait_ge(f1_kept, b + 1)
                    if b >= 2:
                        pe.wait_ge(f1_used, b - 1)
                    for k in range(H1):
                        mm = pe.matmul(ps[:, 2 + b % 2, 0:P], aggT[:, (b % 2) * 384 + k * P:(b % 2) * 384 + (k + 1) * P], V[:, k * P:(k + 1) * P],
                                       start=(k == 0), stop=(k == H1 - 1))
                    mm.then_inc(f1_y, 1)

        end_layer()

        Wd = wbuf[:, 1144:1152]
        bd_bc = bias_row[:, 0:K2]
        coef2 = scal[:, :, :].rearrange("p k b -> p (k b)")[:, 0:NB * K2].rearrange("p (b k) -> p b k", k=K2)
        dis = small[:, 8, :]
        a2_in, a2_root, a2_rooted, a2_norm = sem("a2_in"), sem("a2_root"), sem("a2_rooted"), sem("a2_norm")
        a2_turned, a2_kept, a2_done, a2_table = sem("a2_turned"), sem("a2_kept"), sem("a2_done"), sem("a2_table")
        a2_shift, a2_exp, a2_scaled = sem("a2_shift"), sem("a2_exp"), sem("a2_scaled")
        with nc.Block() as block:
            @block.sync
            def _(sp):
                sp.dma_start(Wd, L2_Wd).then_inc(a2_in, 16)
                sp.dma_start(bd_bc, L2_bd.unsqueeze(0).broadcast_to([P, K2])).then_inc(a2_in, 16)
                write_table(sp, 2, hs[:], (a2_scaled, 1), a2_table)

            @block.vector
            def _(dve):
                standardise(dve, (a2_root, a2_rooted), xs[:])
                dve.tensor_scalar(hs[:], hs[:], 0.0, None, ALU.max).then_inc(a2_norm, 1)
                dve.tensor_scalar(dis, deg[:], 1.0, None, ALU.add)
                dve.wait_ge(a2_in, 32)
                dve.wait_ge(a2_done, 1)
                got = ps[:, 2, 0:NB * K2].rearrange("p (b k) -> p b k", k=K2)
                link(dve, dve.tensor_tensor(coef2, got, bd_bc.unsqueeze(1).broadcast_to([P, NB, K2]), ALU.add))
                link(dve, dve.tensor_reduce(small[:, 3, :], coef2, AX.X, ALU.max))
                link(dve, dve.tensor_tensor(coef2, coef2, small[:, 3, :].unsqueeze(2).broadcast_to([P, NB, K2]), ALU.subtract))
                dve.sem_inc(a2_shift, 1)
                dve.wait_ge(a2_exp, 2)
                link(dve, dve.tensor_reduce(small[:, 4, :], coef2, AX.X, ALU.add))
                link(dve, dve.reciprocal(small[:, 5, :], small[:, 4, :]))
                link(dve, dve.reciprocal(dis, dis))
                dve.tensor_tensor(coef2, coef2, small[:, 5, :].unsqueeze(2).broadcast_to([P, NB, K2]), ALU.mult)
                dve.tensor_tensor(hs[:], hs[:], per_node(dis), ALU.mult).then_inc(a2_scaled, 1)

            @block.scalar
            def _(act):
                std_root(act, a2_root, a2_rooted)
                keep_blocks(act, hT, a2_turned, a2_kept)
                act.wait_ge(a2_shift, 1)
                act.activation(dis, dis, ACT.Sqrt).then_inc(a2_exp, 1)
                act.activation(coef2, coef2, ACT.Exp).then_inc(a2_exp, 1)

            @block.tensor
            def _(pe):
                pe.wait_ge(a2_in, 32)
                turn_blocks(pe, hs, a2_norm, a2_turned, a2_kept)
                node_products(pe, hT, Wd, K2, (a2_kept, TG), a2_done, per_bank=NB)

        acc = row_pass(2, D)

        W2 = wbuf[:, 0:K2 * D]
        b2_bc = A3[:, 0:K2 * D]
        biased = A3[:, K2 * D:3 * K2 * D].rearrange("p (i z) -> p i z", i=2)
        scaled = A3[:, 3 * K2 * D:5 * K2 * D].rearrange("p (i z) -> p i z", i=2)
        aT = A2[:, 0:NP].rearrange("p (b f) -> p b f", f=D)
        f2_in, f2_agg, f2_turned, f2_kept = sem("f2_in"), sem("f2_agg"), sem("f2_turned"), sem("f2_kept")
        f2_mul, f2_biased, f2_scaled, f2_sum = sem("f2_mul"), sem("f2_biased"), sem("f2_scaled"), sem("f2_sum")
        with nc.Block() as block:
            @block.sync
            def _(sp):
                sp.dma_start(W2.rearrange("p (k o) -> p k o", k=K2), L2_W.rearrange("k i o -> i k o")).then_inc(f2_in, 16)
                sp.dma_start(b2_bc, L2_b.rearrange("k o -> (k o)").unsqueeze(0).broadcast_to([P, K2 * D])).then_inc(f2_in, 16)
                sp.wait_ge(f2_in, 32)

            @block.vector
            def _(dve):
                link(dve, dve.tensor_tensor(acc, acc, hs[:], ALU.add))
                dve.tensor_tensor(acc, acc, per_node(dis), ALU.mult).then_inc(f2_agg, 1)
                dve.wait_ge(f2_in, 32)

                def reduce(b):
                    dve.wait_ge(f2_scaled, b + 1)
                    link(dve, dve.tensor_reduce(hs[:, b, :], scaled[:, b % 2, :].rearrange("p (k o) -> p o k", k=K2), AX.X, ALU.add))
                    dve.tensor_tensor(xs[:, b, :], xs[:, b, :], hs[:, b, :], ALU.add).then_inc(f2_sum, 1)

                for b in range(NB):
                    dve.wait_ge(f2_mul, b + 1)
                    if b >= 2:
                        dve.wait_ge(f2_scaled, b - 1)
                    dve.tensor_tensor(biased[:, b % 2, :].rearrange("p (i z) -> p i z", i=2), ps[:, 2 + 2 * (b % 2):4 + 2 * (b % 2), :],
                                      b2_bc.rearrange("p (i z) -> p i z", i=2), ALU.add).then_inc(f2_biased, 1)
                    if b:
                        reduce(b - 1)
                reduce(NB - 1)

            @block.scalar
            def _(act):
                keep_blocks(act, aT, f2_turned, f2_kept)
                for b in range(NB):
                    act.wait_ge(f2_biased, b + 1)
                    if b >= 2:
                        act.wait_ge(f2_sum, b - 1)
                    for k in range(K2):
                        last = act.activation(scaled[:, b % 2, k * D:(k + 1) * D], biased[:, b % 2, k * D:(k + 1) * D], ACT.Relu,
                                              scale=coef2[:, b, k:k + 1])
                    last.then_inc(f2_scaled, 1)

            @block.tensor
            def _(pe):
                turn_blocks(pe, acc, f2_agg, f2_turned, f2_kept)
                pe.wait_ge(f2_in, 32)
                pe.wait_ge(f2_kept, TG)
                for b in range(NB):
                    if b >= 2:
                        pe.wait_ge(f2_biased, b - 1)
                    for i in range(2):
                        mm = pe.matmul(ps[:, 2 + 2 * (b % 2) + i, :], aT[:, b, :], W2[:, i * 512:(i + 1) * 512], start=True, stop=True)
                    mm.then_inc(f2_mul, 1)

        end_layer()

        att3 = wnat[:, 0:2 * D]
        Wp, Wsk = wbuf[:, 0:D], wbuf[:, D:2 * D]
        a3_in, a3_root, a3_rooted, a3_norm = sem("a3_in"), sem("a3_root"), sem("a3_rooted"), sem("a3_norm")
        a3_turned, a3_kept, a3_done, a3_used = sem("a3_turned"), sem("a3_kept"), sem("a3_done"), sem("a3_used")
        a3_seed, a3_seeded, a3_table = sem("a3_seed"), sem("a3_seeded"), sem("a3_table")
        with nc.Block() as block:
            @block.sync
            def _(sp):
                sp.dma_start(Wp, L3_Wp).then_inc(a3_in, 16)
                sp.dma_start(Wsk, L3_Ws).then_inc(a3_in, 16)
                sp.dma_start(att3[:, 0:D], L3_as.rearrange("o h c -> o (h c)").broadcast_to([P, D])).then_inc(a3_in, 16)
                sp.dma_start(att3[:, D:2 * D], L3_at.rearrange("o h c -> o (h c)").broadcast_to([P, D])).then_inc(a3_in, 16)
                write_table(sp, 3, tab, (a3_seed, 1), a3_table)

            @block.gpsimd
            def _(pool):
                pool.wait_ge(a3_seed, 1)
                scatter_seeds(pool, a3_seeded)

            @block.vector
            def _(dve):
                standardise(dve, (a3_root, a3_rooted), xs[:])
                dve.tensor_scalar(hs[:], hs[:], 0.0, None, ALU.max).then_inc(a3_norm, 1)
                for g in range(TG):
                    bs, got = bank_squares(g)
                    dve.wait_ge(a3_done, g + 1)
                    dve.tensor_copy(hW[:, bs, :], got).then_inc(a3_used, 1)
                dve.wait_ge(a3_used, TG)
                dve.wait_ge(a3_in, 64)
                by_head = tmp.rearrange("p b (k c) -> p b k c", c=C3)
                link(dve, dve.tensor_tensor(tmp, hW, per_feature(att3[:, 0:D]), ALU.mult))
                link(dve, dve.tensor_reduce(tab[:, :, D:D + H3], by_head, AX.X, ALU.add))
                link(dve, dve.tensor_tensor(tmp, hW, per_feature(att3[:, D:2 * D]), ALU.mult))
                dve.tensor_reduce(seed_vals, by_head, AX.X, ALU.add).then_inc(a3_seed, 1)

            @block.scalar
            def _(act):
                std_root(act, a3_root, a3_rooted)
                keep_blocks(act, hT, a3_turned, a3_kept)

            @block.tensor
            def _(pe):
                turn_blocks(pe, hs, a3_norm, a3_turned, a3_kept)
                pe.wait_ge(a3_in, 64)
                wide_products(pe, hT, Wp, a3_kept, a3_done, a3_used)

        db3_in = sem("db3_in")
        with nc.Block() as block:
            @block.sync
            def _(sp):
                sp.dma_start(A3[:, 0:EC * KW], seeds_edges.rearrange("(p c) k -> p (c k)", p=P)).then_inc(db3_in, 16)
                sp.wait_ge(db3_in, 16)
        copy_down(3, H3)
        edge_no = A1[:, 0:EC]
        w3_iota = sem("w3_iota")
        with nc.Block() as block:
            @block.gpsimd
            def _(pool):
                pool.iota(edge_no, [[1, EC]], base=0, channel_multiplier=EC, allow_small_or_imprecise_dtypes=True).then_inc(w3_iota, 1)

            @block.vector
            def _(dve):
                dve.wait_ge(w3_iota, 1)
                link(dve, dve.tensor_scalar(scan_tmp[:], edge_no, float(E), -BIG, ALU.is_ge, ALU.mult))
                dve.tensor_tensor(SE, DB, scan_tmp[:].unsqueeze(2).broadcast_to([P, EC, KW]), ALU.add)

        to_steps(3, H3)
        acc = row_pass(3, D + H3)

        hT3 = A2[:, 0:NP].rearrange("p (b f) -> p b f", f=D)
        z = A3[:, 0:NP].rearrange("p (b f) -> p b f", f=D)
        f3_start, f3_turned, f3_kept, f3_done, f3_used = sem("f3_start"), sem("f3_turned"), sem("f3_kept"), sem("f3_done"), sem("f3_used")
        f3_low, f3_exp, f3_x, f3_out = sem("f3_low"), sem("f3_exp"), sem("f3_x"), sem("f3_out")
        with nc.Block() as block:
            @block.vector
            def _(dve):
                den = scal[:, 0:H3, :].rearrange("p k b -> p (k b)").rearrange("p (b k) -> p b k", k=H3)
                rec = scal[:, H3:2 * H3, :].rearrange("p k b -> p (k b)").rearrange("p (b k) -> p b k", k=H3)
                dve.memset(small[:, 0, 0:1], 0.0).then_inc(f3_start, 1)
                link(dve, dve.tensor_scalar(den, acc[:, :, D:D + H3], 1e-16, None, ALU.add))
                link(dve, dve.reciprocal(rec, den))
                link(dve, dve.tensor_tensor(z.rearrange("p b (k c) -> p b k c", c=C3), acc[:, :, 0:D].rearrange("p b (k c) -> p b k c", c=C3),
                                            rec.unsqueeze(3).broadcast_to([P, NB, H3, C3]), ALU.mult))
                for g in range(TG):
                    bs, got = bank_squares(g)
                    dve.wait_ge(f3_done, g + 1)
                    dve.tensor_tensor(z[:, bs, :], z[:, bs, :], got, ALU.add).then_inc(f3_used, 1)
                dve.wait_ge(f3_used, TG)
                dve.tensor_scalar(tmp, z, 0.0, None, ALU.min).then_inc(f3_low, 1)
                link(dve, dve.scalar_tensor_tensor(out=xs[:], in0=z, scalar=0.0, in1=xs[:], op0=ALU.max, op1=ALU.add))
                dve.wait_ge(f3_exp, 1)
                dve.scalar_tensor_tensor(out=xs[:], in0=tmp, scalar=-1.0, in1=xs[:], op0=ALU.add, op1=ALU.add).then_inc(f3_x, 1)

            @block.scalar
            def _(act):
                keep_blocks(act, hT3, f3_turned, f3_kept)
                act.wait_ge(f3_low, 1)
                act.activation(tmp, tmp, ACT.Exp).then_inc(f3_exp, 1)

            @block.tensor
            def _(pe):
                turn_blocks(pe, hs, f3_start, f3_turned, f3_kept)
                wide_products(pe, hT3, Wsk, f3_kept, f3_done, f3_used)

            @block.sync
            def _(sp):
                sp.wait_ge(f3_x, 1)
                sp.dma_start(out[0:(NB - 1) * P, :].rearrange("(b p) f -> p b f", p=P), xs[:, 0:NB - 1, :]).then_inc(f3_out, 16)
                sp.dma_start(out[(NB - 1) * P:N, :], xs[0:TAIL, NB - 1, :]).then_inc(f3_out, 16)
                sp.wait_ge(f3_out, 32)


_INS = ['x', 'src', 'dst', 'edge_attr_16', 'L0_gnn_biclique_mask', 'L0_gnn_W', 'L0_gnn_attn', 'L1_gnn_W', 'L1_gnn_W_edge',
        'L1_gnn_att_src', 'L1_gnn_att_dst', 'L1_gnn_att_edge', 'L1_gnn_gat_bias', 'L1_gnn_lin_W', 'L1_gnn_lin_b', 'L1_gnn_ln_g',
        'L1_gnn_ln_b', 'L2_gnn_W', 'L2_gnn_b', 'L2_gnn_W_dict', 'L2_gnn_b_dict', 'L3_gnn_W_proj', 'L3_gnn_W_skip', 'L3_gnn_a_src',
        'L3_gnn_a_tgt']
_OUTS = [((N, D), 'float32')]


def kernel(**inputs):
    import numpy as _np
    import concourse.bacc as _bacc
    from concourse import mybir as _mybir
    from concourse.bass_utils import run_bass_kernel_spmd as _run

    nc = _bacc.Bacc("TRN2", target_bir_lowering=False, num_devices=1)
    arrays, args = {}, []
    for name in _INS:
        a = _np.ascontiguousarray(inputs[name])
        arrays[f"in_{name}_dram"] = a
        args.append(nc.dram_tensor(f"in_{name}_dram", a.shape, _mybir.dt.from_np(a.dtype), kind="ExternalInput").ap())
    for i, (shape, dtype) in enumerate(_OUTS):
        dt = _mybir.dt.from_np(_np.dtype(dtype))
        args.append(nc.dram_tensor(f"out_{i}_dram", shape, dt, kind="ExternalOutput").ap())
    build_gnn(nc, *args)
    r = _run(nc, [arrays], core_ids=[0])
    got = tuple(r.results[0][f"out_{i}_dram"] for i in range(len(_OUTS)))
    return got[0]
```

```python
from contextlib import ExitStack

import concourse.bass as bass
from concourse import mybir

F32 = mybir.dt.float32
I32 = mybir.dt.int32
ALU = mybir.AluOpType
ACT = mybir.ActivationFunctionType
AX = mybir.AxisListType

P = 128
N = 3125
E = 100000
D = 128
NB = -(-N // P)
NP = NB * P
TAIL = N - (NB - 1) * P
EC = 16 * (-(-E // (16 * P)))
EP = EC * P
PAD = EP - E
PAD_DST = NP
KW = 8
EA = 16
H1 = 3
H3 = 8
C3 = D // H3
K2 = 8
GROUP = 2
BODY = 32
HAND = 4
DVE_STEPS = 2
DEPTH = 2
AHEAD = {0: (0, 0, 0, 4), 1: (8, 23, 27, 31), 2: (0, 0, 0, 0), 3: (8, 26, 31, 32)}
TILES = -(-E // P)
GROUPS_NEEDED = (TILES + NB - 1 + NB * (GROUP - 1)) // GROUP
STEPS = BODY * (-(-GROUPS_NEEDED * GROUP // BODY))
GROUPS = STEPS // GROUP
NCH = 8
CH = STEPS // NCH
ACCW = H1 * D + 2 * H1
RW = D + KW
BIG = 1.0e37
LN_EPS = 1e-5
assert CH <= P and STEPS == NCH * CH and BODY % (2 * HAND * DEPTH) == 0


def build_gnn(nc, x, src, dst, edge_attr, L0_mask, L0_W, L0_attn, L1_W, L1_We, L1_as, L1_ad, L1_ae,
              L1_gb, L1_lW, L1_lb, L1_g, L1_b, L2_W, L2_b, L2_Wd, L2_bd, L3_Wp, L3_Ws, L3_as, L3_at, out):
    ctx = ExitStack()
    with ctx:
        def sb(name, shape, dt=F32):
            return ctx.enter_context(nc.sbuf_tensor(name, shape, dt))

        layer_sems = []

        def sem(name):
            layer_sems.append(nc.alloc_semaphore(name))
            return layer_sems[-1]

        def end_layer():
            nc.clear_and_free_semaphores(layer_sems)
            nc.all_engine_barrier()
            layer_sems.clear()

        rows_in = {}

        def open_rows(L):
            rows_in.clear()
            rows_in[L] = [[sem(f"L{L}_rows_in{q}{h}") for h in range(BODY // HAND)] for q in range(2)]

        def dram(name, shape, dt=F32):
            return nc.dram_tensor(name, shape, dt).ap()

        src_flat = dram("src_flat", (EP // P, P), I32)
        dst_flat = dram("dst_flat", (EP // P, P), I32)
        dst_ext = dram("dst_ext", (EP + 2,), I32)
        tables = [dram(f"table{L}", (NP, w)) for L, w in enumerate((D + 1, D + H1, D, D + H3))]
        dst_by_step = dram("dst_by_step", (STEPS * P + 2,))
        runs = dram("runs", (STEPS, 4 * P))
        row_pens_out = dram("row_pens_out", (2, STEPS))
        edge_rows = dram("edge_rows", (EP // P, P * KW))
        seeds = dram("seeds", (EP + NP, KW))
        seeds_edges = seeds[0:EP, :]

        xs = sb("xs", [P, NB, D])
        hs = sb("hs", [P, NB, D])
        A1 = sb("A1", [P, 2 * NP + NB * RW])
        A2 = sb("A2", [P, EC * KW])
        A3 = sb("A3", [P, STEPS * KW])
        a_edge = sb("a_edge", [P, EC, H1])
        gath = sb("gath", [P, BODY, RW])
        onehot = sb("onehot", [P, HAND * DEPTH, P])
        weighted = sb("weighted", [P, HAND * DEPTH, ACCW])
        idx_step = sb("idx_step", [P, STEPS + 2 * BODY], I32)
        idx_ring = sb("idx_ring", [P, 2, BODY], I32)
        dst_step = sb("dst_step", [P, STEPS + 2 * HAND])
        keep_f = sb("keep_f", [P, EC])
        scan_tmp = sb("scan_tmp", [P, EC])
        iota_row = sb("iota_row", [P, P])
        iota_p = sb("iota_p", [P, 1])
        iota_hi = sb("iota_hi", [P, NB])
        ident = sb("ident", [P, P])
        tri = sb("tri", [P, P])
        ones = sb("ones", [P, P])
        carry_row = sb("carry_row", [KW, 6, P + 1])
        carry_col = sb("carry_col", [P, 4, KW])
        blk_reg = sb("blk_reg", [1, GROUPS], I32)
        deg = sb("deg", [P, NB])
        seed_idx = sb("seed_idx", [P, NB], I32)
        small = sb("small", [P, 16, NB])
        scal = sb("scal", [P, 2 * KW, NB])
        row_pens = sb("row_pens", [H1, 2, STEPS])
        borders = sb("borders", [BODY, 2, 4, P])
        scores = sb("scores", [P, BODY, KW])
        topped = sb("topped", [P, BODY, H1])
        shifted = sb("shifted", [P, BODY, KW])
        weights = sb("weights", [P, 2, BODY, KW])
        run_f = sb("run_f", [BODY, H1, P])
        run_b = sb("run_b", [BODY, H1, P])
        row_f = sb("row_f", [H1, BODY + 1])
        row_b = sb("row_b", [H1, BODY + 1])
        row_col = sb("row_col", [BODY, 2, KW])
        edge_cols = sb("edge_cols", [P, 2, KW])
        last_max = sb("last_max", [P, KW])
        rescale = sb("rescale", [P, 3, KW])
        first_hot = sb("first_hot", [P, 1])
        pick_first = sb("pick_first", [P, P])
        pick_last = sb("pick_last", [P, P])
        wbuf = sb("wbuf", [P, 3 * 384])
        wnat = sb("wnat", [P, 384])
        bias_row = sb("bias_row", [P, D])
        ps = ctx.enter_context(nc.psum_tensor("ps", [P, 8, 512], F32))

        seed_vals = A2[:, 0:NB * KW].rearrange("p (b k) -> p b k", k=KW)
        SE = A2[:, :].rearrange("p (c k) -> p c k", k=KW)
        DB = A3[:, 0:EC * KW].rearrange("p (c k) -> p c k", k=KW)
        WS = A3[:, :].rearrange("p (s k) -> p s k", k=KW)
        tmp = A1[:, 0:NP].rearrange("p (b f) -> p b f", f=D)
        hT = A1[:, NP:2 * NP].rearrange("p (b f) -> p b f", f=D)
        tab = A1[:, 2 * NP:2 * NP + NB * RW].rearrange("p (b w) -> p b w", w=RW)
        hW = tab[:, :, 0:D]

        dve_chain = ctx.enter_context(nc.semaphore("dve_chain"))
        dve_count = [0]

        def link(dve, ins):
            dve_count[0] += 1
            ins.then_inc(dve_chain, 1)
            dve.wait_ge(dve_chain, dve_count[0])

        TG = -(-NB // 4)

        def per_node(v):
            return v.unsqueeze(2).broadcast_to([P, NB, D])

        def per_feature(v):
            return v.unsqueeze(1).broadcast_to([P, NB, D])

        stats = scal[:].rearrange("p k b -> p (k b)")[:, 0:NB * 6].rearrange("p (b v) -> p b v", v=6)
        moments = scal[:].rearrange("p k b -> p (k b)")[:, NB * 6:NB * 8].rearrange("p (b v) -> p b v", v=2)

        def node_stats(dve, of):
            for b in range(NB):
                last = dve.bn_stats(stats[:, b, :], of[:, b, :])
            link(dve, last)

        def standardise(dve, act_sync, of, relu_done=None):
            to_act, from_act = act_sync
            rec = small[:, 2, :]
            for b in range(NB):
                last = dve.bn_aggr(moments[:, b, :], stats[:, b, :])
            link(dve, last)
            dve.tensor_scalar(small[:, 1, :], moments[:, :, 1], LN_EPS, None, ALU.add).then_inc(to_act, 1)
            dve.wait_ge(from_act, 1)
            link(dve, dve.reciprocal(rec, small[:, 1, :]))

            def relu(g):
                blocks = hs[:, 4 * g:min(4 * g + 4, NB), :]
                dve.tensor_scalar(blocks, blocks, 0.0, None, ALU.max).then_inc(relu_done, 1)

            for g in range(TG):
                for b in range(4 * g, min(4 * g + 4, NB)):
                    last = dve.tensor_scalar(hs[:, b, :], of[:, b, :], moments[:, b, 0:1], rec[:, b:b + 1], ALU.subtract, ALU.mult)
                dve_count[0] += 1
                last.then_inc(dve_chain, 1)
                if relu_done is not None and g:
                    dve.wait_ge(dve_chain, dve_count[0] - 1)
                    relu(g - 1)
            dve.wait_ge(dve_chain, dve_count[0])
            if relu_done is not None:
                relu(g)

        def std_root(act, to_act, from_act):
            act.wait_ge(to_act, 1)
            act.activation(small[:, 1, :], small[:, 1, :], ACT.Sqrt).then_inc(from_act, 1)

        loaded = sem("loaded")
        pads_set = sem("pads_set")
        iota_set = sem("iota_set")
        pad_i = A1[0:1, 8192:8192 + 3 * PAD + 4].bitcast(I32)
        x_in = sem("x_in")
        seeds_zeroed = sem("seeds_zeroed")
        EQ = 7
        NQ = (EC * EA // P) // EQ
        EA_SLOTS = 6
        ea_in = A2[:, 0:EA_SLOTS * EQ * P].rearrange("p (q w) -> p q w", q=EA_SLOTS)
        ea_loaded = [sem(f"ea_loaded{i}") for i in range(EA_SLOTS)]
        ea_zero = sem("ea_zero")
        EA_ROWS = E * EA // P
        PER = EC * EA // P
        FULL = EA_ROWS // PER
        REST = EA_ROWS - FULL * PER
        ea_view = edge_attr.rearrange("(r j) c -> r (j c)", j=8)

        def load_squares(act, q):
            slot = q % EA_SLOTS
            act.dma_start(ea_in[0:FULL, slot, :],
                          ea_view[0:FULL * PER, :].rearrange("(p t) w -> p (t w)", t=PER)[:, q * EQ * P:(q + 1) * EQ * P]).then_inc(ea_loaded[slot], 16)
            here = min(max(REST - q * EQ, 0), EQ)
            if here:
                act.dma_start(ea_in[FULL:FULL + 1, slot, 0:here * P],
                              ea_view[FULL * PER + q * EQ:FULL * PER + q * EQ + here, :].rearrange("t w -> (t w)").unsqueeze(0)).then_inc(ea_loaded[slot], 16)

        def ea_loads(q):
            return 16 * sum(2 if REST > k * EQ else 1 for k in range(q % EA_SLOTS, q + 1, EA_SLOTS))

        with nc.Block() as block:
            @block.sync
            def _(sp):
                sp.dma_start(src_flat.rearrange("a b -> (a b)")[0:E].unsqueeze(0), src.unsqueeze(0)).then_inc(loaded, 16)
                sp.dma_start(dst_flat.rearrange("a b -> (a b)")[0:E].unsqueeze(0), dst.unsqueeze(0)).then_inc(loaded, 16)
                sp.dma_start(dst_ext[1:E + 1].unsqueeze(0), dst.unsqueeze(0)).then_inc(loaded, 16)
                sp.wait_ge(pads_set, 3)
                sp.dma_start(src_flat.rearrange("a b -> (a b)")[E:EP].unsqueeze(0), pad_i[:, 0:PAD]).then_inc(loaded, 16)
                sp.dma_start(dst_flat.rearrange("a b -> (a b)")[E:EP].unsqueeze(0), pad_i[:, PAD:2 * PAD]).then_inc(loaded, 16)
                sp.dma_start(dst_ext[E + 1:EP + 2].unsqueeze(0), pad_i[:, PAD:2 * PAD + 1]).then_inc(loaded, 16)
                sp.dma_start(dst_ext[0:1].unsqueeze(0), pad_i[:, 2 * PAD + 2:2 * PAD + 3]).then_inc(loaded, 16)
                sp.dma_start(xs[:, 0:NB - 1, :], x[0:(NB - 1) * P, :].rearrange("(b p) f -> p b f", p=P)).then_inc(x_in, 16)
                sp.wait_ge(pads_set, 5)
                sp.dma_start(xs[0:TAIL, NB - 1, :], x[(NB - 1) * P:N, :]).then_inc(x_in, 16)
                sp.dma_start(seeds.rearrange("(p a) k -> p (a k)", p=P), A3[:, 0:(EP + NP) * KW // P]).then_inc(seeds_zeroed, 16)
                sp.wait_ge(loaded, 7 * 16)

            @block.scalar
            def _(act):
                act.wait_ge(ea_zero, 1)
                for q in range(EA_SLOTS):
                    load_squares(act, q)

            @block.vector
            def _(dve):
                dve.memset(pad_i[:, 0:PAD], 0).then_inc(pads_set, 1)
                dve.memset(pad_i[:, PAD:2 * PAD + 2], PAD_DST).then_inc(pads_set, 1)
                dve.memset(pad_i[:, 2 * PAD + 2:2 * PAD + 4], -1).then_inc(pads_set, 1)
                dve.memset(A2[:, 0:EA_SLOTS * EQ * P], 0.0).then_inc(ea_zero, 1)
                dve.memset(xs[:, NB - 1, :], 0.0).then_inc(pads_set, 1)
                dve.memset(A3[:], 0.0).then_inc(pads_set, 1)
                dve.memset(ones[:], 1.0)
                dve.memset(idx_step[:, STEPS:STEPS + 2 * BODY], 0)
                dve.memset(dst_step[:, STEPS:STEPS + 2 * HAND], -1.0)
                dve.wait_ge(iota_set, 3)
                dve.tensor_scalar(ident[:], iota_row[:], iota_p[:, 0:1], None, ALU.is_equal)
                dve.tensor_scalar(tri[:], iota_row[:], iota_p[:, 0:1], None, ALU.is_gt)
                dve.tensor_scalar(pick_first[:], iota_p[:, 0:1].broadcast_to([P, P]), 0.0, None, ALU.is_equal)
                dve.tensor_scalar(pick_last[:], iota_p[:, 0:1].broadcast_to([P, P]), float(P - 1), None, ALU.is_equal)

            @block.gpsimd
            def _(pool):
                pool.iota(iota_row[:], [[1, P]], base=0, channel_multiplier=0,
                          allow_small_or_imprecise_dtypes=True).then_inc(iota_set, 1)
                pool.iota(iota_p[:], [[1, 1]], base=0, channel_multiplier=1,
                          allow_small_or_imprecise_dtypes=True).then_inc(iota_set, 1)
                pool.iota(iota_hi[:], [[1, NB]], base=0, channel_multiplier=0,
                          allow_small_or_imprecise_dtypes=True).then_inc(iota_set, 1)

        prev_i = A1[:, 0:EC].bitcast(I32)
        cur_i = A1[:, EC:2 * EC].bitcast(I32)
        last_i = A1[0:1, 2 * EC:3 * EC].bitcast(I32)
        last_f = A1[0:1, 3 * EC:4 * EC]
        before = A1[0:NB, 4 * EC:5 * EC]
        in_or_after = A1[0:NB, 5 * EC:5 * EC + GROUPS]
        by_step = A1[0:NB, 6 * EC:6 * EC + STEPS].rearrange("p (g i) -> p g i", i=GROUP)
        group_no = A1[:, 8 * EC:8 * EC + GROUPS]
        plan = A1[:, 9 * EC:9 * EC + 64]
        plan_i = A1[:, 9 * EC + 64:9 * EC + 128].bitcast(I32)
        step_no = A1[:, 9 * EC + 128:9 * EC + 128 + NCH]
        diff = A1[:, 9 * EC + 160:9 * EC + 160 + P]
        coef = A1[:, 9 * EC + 320:9 * EC + 322]
        tile_i = sb("tile_i", [P, NCH], I32)
        block_lo = sb("block_lo", [P, NCH])
        we_prod = onehot[:].rearrange("p s w -> p (s w)")[:, 0:384]
        ve_col = sb("ve_col", [P, 4])
        ve_diag = sb("ve_diag", [P, 8 * H1])
        ve_ready = sem("ve_ready")
        ve_placed = sem("ve_placed")
        w_in = sem("w_in")
        ve_dram = dram("ve_dram", (EA, H1))
        plan_in = sem("plan_in")
        plan_iota = sem("plan_iota")
        plan_ready = sem("plan_ready")
        plan_done = sem("plan_done")
        with nc.Block() as block:
            @block.sync
            def _(sp):
                sp.dma_start(prev_i, dst_ext[0:EP].rearrange("(p c) -> p c", p=P)).then_inc(plan_in, 16)
                sp.dma_start(cur_i, dst_ext[1:EP + 1].rearrange("(p c) -> p c", p=P)).then_inc(plan_in, 16)
                with nc.allow_non_contiguous_dma("one element per tile"):
                    sp.dma_start(last_i.unsqueeze(2), dst_flat[:, P - 1:P].unsqueeze(0)).then_inc(plan_in, 16)
                sp.dma_start(wnat[0:EA, :], L1_We).then_inc(w_in, 16)
                sp.dma_start(wbuf[0:EA, 0:384], L1_ae.rearrange("h c -> (h c)").unsqueeze(0).broadcast_to([EA, 384])).then_inc(w_in, 16)
                sp.wait_ge(ve_ready, 2)
                sp.dma_start(ve_dram, ve_col[0:EA, 0:H1]).then_inc(ve_placed, 16)
                sp.wait_ge(ve_placed, 16)
                with nc.allow_non_contiguous_dma("eight small squares"):
                    for j in range(8):
                        sp.dma_start(ve_diag[j * EA:(j + 1) * EA, j * H1:(j + 1) * H1], ve_dram).then_inc(ve_placed, 16)
                sp.wait_ge(ve_placed, 16 * 9)
            @block.gpsimd
            def _(pool):
                pool.iota(group_no, [[1, GROUPS]], base=0, channel_multiplier=0,
                          allow_small_or_imprecise_dtypes=True).then_inc(plan_iota, 1)
                pool.iota(step_no, [[CH, NCH]], base=0, channel_multiplier=1,
                          allow_small_or_imprecise_dtypes=True).then_inc(plan_iota, 1)

            @block.tensor
            def _(pe):
                pe.wait_ge(plan_ready, 1)
                for q in range(2):
                    mm = pe.matmul(ps[0:NB, q, 0:EC // 2], ones[0:1, 0:NB], last_f[:, q * EC // 2:(q + 1) * EC // 2],
                                   start=True, stop=True)
                mm.then_inc(plan_done, 1)
                pe.wait_ge(plan_ready, 2)
                pe.matmul(ps[0:NB, 2, 0:1], tri[0:NB, 0:NB], plan[0:NB, 4:5], start=True, stop=True).then_inc(plan_done, 1)
                pe.wait_ge(plan_ready, 3)
                pe.matmul(ps[0:NB, 3, 0:1], diff[0:NB, 0:NB], plan[0:NB, 6:7], start=True, stop=True).then_inc(plan_done, 1)
                pe.wait_ge(plan_ready, 4)
                pe.matmul(ps[0:1, 4, 0:GROUPS], ones[0:NB, 0:1], in_or_after, start=True, stop=True)
                for c in range(NCH):
                    mm = pe.matmul(ps[0:CH, 5, 2 * c:2 * c + 2], by_step.rearrange("p g i -> p (g i)")[:, c * CH:(c + 1) * CH],
                                   coef[0:NB, :], start=True, stop=True)
                mm.then_inc(plan_done, 1)
            @block.vector
            def _(dve):
                dve.memset(ve_diag[:], 0.0).then_inc(ve_ready, 1)
                dve.wait_ge(w_in, 32)
                link(dve, dve.tensor_tensor(we_prod[0:EA, 0:384], wnat[0:EA, :], wbuf[0:EA, 0:384], ALU.mult))
                dve.tensor_reduce(ve_col[0:EA, 0:H1], we_prod[0:EA, 0:384].rearrange("p (h c) -> p h c", c=P), AX.X, ALU.add).then_inc(ve_ready, 1)
                dve.wait_ge(plan_in, 3 * 16)
                dve.tensor_copy(last_f, last_i).then_inc(plan_ready, 1)
                dve.wait_ge(plan_done, 1)
                link(dve, dve.tensor_scalar(plan[:, 0:1], iota_p[:], float(P), None, ALU.mult))
                link(dve, dve.tensor_scalar(plan[:, 1:2], plan[:, 0:1], float(P), None, ALU.add))
                for k in range(2):
                    link(dve, dve.tensor_scalar(before.rearrange("p (q c) -> p q c", q=2), ps[0:NB, 0:2, 0:EC // 2],
                                                plan[0:NB, k:k + 1], None, ALU.is_lt))
                    link(dve, dve.tensor_reduce(plan[0:NB, 2 + k:3 + k], before, AX.X, ALU.add))
                link(dve, dve.tensor_tensor(plan[0:NB, 5:6], plan[0:NB, 3:4], plan[0:NB, 2:3], ALU.subtract))
                link(dve, dve.tensor_scalar(plan_i[0:NB, 0:1], plan[0:NB, 5:6], 2.0, None, ALU.add))
                link(dve, dve.tensor_scalar(plan_i[0:NB, 1:2], plan_i[0:NB, 0:1], 1, None, ALU.arith_shift_right))
                dve.tensor_copy(plan[0:NB, 4:5], plan_i[0:NB, 1:2]).then_inc(plan_ready, 1)
                dve.wait_ge(plan_done, 2)
                link(dve, dve.tensor_copy(plan[0:NB, 7:8], ps[0:NB, 2, 0:1]))
                link(dve, dve.scalar_tensor_tensor(out=plan[0:NB, 6:7], in0=plan[0:NB, 7:8], scalar=-float(GROUP),
                                                   in1=plan[0:NB, 2:3], op0=ALU.mult, op1=ALU.add))
                link(dve, dve.tensor_scalar(plan[:, 8:9], iota_p[:], 1.0, None, ALU.add))
                link(dve, dve.tensor_scalar(diff, iota_row[:], plan[:, 8:9], None, ALU.is_equal))
                dve.tensor_tensor(diff, ident[:], diff, ALU.subtract).then_inc(plan_ready, 1)
                dve.wait_ge(plan_done, 3)
                dve.wait_ge(plan_iota, 2)
                link(dve, dve.memset(coef[:, 0:1], 1.0))
                link(dve, dve.tensor_copy(coef[0:NB, 1:2], ps[0:NB, 3, 0:1]))
                link(dve, dve.tensor_scalar(in_or_after, group_no[0:NB, :], plan[0:NB, 7:8], None, ALU.is_ge))
                dve.tensor_copy(by_step, in_or_after.unsqueeze(2).broadcast_to([NB, GROUPS, GROUP])).then_inc(plan_ready, 1)
                dve.wait_ge(plan_done, 4)
                dve.tensor_scalar(blk_reg[:], ps[0:1, 4, 0:GROUPS], -1.0, None, ALU.add)
                counts = ps[0:CH, 5, 0:2 * NCH].rearrange("p (c two) -> p c two", two=2)
                dve.tensor_scalar(block_lo[0:CH, :], counts[:, :, 0], float(P), -float(P), ALU.mult, ALU.add)
                link(dve, dve.tensor_tensor(plan[0:CH, 16:16 + NCH], counts[:, :, 1], step_no[0:CH, :], ALU.add))
                dve.tensor_scalar(tile_i[0:CH, :], plan[0:CH, 16:16 + NCH], float(EP // P - 1), None, ALU.min)
                link(dve, dve.tensor_tensor(keep_f[:], cur_i, prev_i, ALU.is_equal))
                link(dve, dve.tensor_reduce(scan_tmp[:, 0:1], keep_f[:], AX.X, ALU.min))
                dve.tensor_copy(carry_col[:, 0, :], scan_tmp[:, 0:1].broadcast_to([P, KW]))

        gath_flat = gath[:].rearrange("p s w -> p (s w)")
        weighted_flat = weighted[:].rearrange("p s w -> p (s w)")
        src_rows = gath_flat[:, 0:NCH * P].bitcast(I32)
        dst_rows = gath_flat[:, NCH * P:2 * NCH * P].bitcast(I32)
        src_rf = gath_flat[:, 2 * NCH * P:3 * NCH * P]
        dst_rf = gath_flat[:, 3 * NCH * P:4 * NCH * P]
        dst_whole = weighted_flat[:, 0:NCH * P]
        step_ends = weighted_flat[0:1, NCH * P:NCH * P + 2]
        whole_out = sem("whole_out")
        ends_set = sem("ends_set")
        ea_T = weighted_flat[:, NCH * P + 2:NCH * P + 2 + 2 * EQ * P].rearrange("p (q w) -> p q w", q=2)
        a0_root, a0_rooted, a0_norm = sem("a0_root"), sem("a0_rooted"), sem("a0_norm")
        step_rows_in = sem("step_rows_in")
        rows_f = sem("rows_f")
        rows_turned = sem("rows_turned")
        rows_kept = sem("rows_kept")
        carry_turned = sem("carry_turned")
        ea_turned = sem("ea_turned")
        ea_kept = sem("ea_kept")
        ae_done = sem("ae_done")
        ae_kept = sem("ae_kept")
        prev_d, cur_d, next_d = (A1[:, i * NCH * P:(i + 1) * NCH * P] for i in range(3))
        border_rows = A1[:, 3 * NCH * P:7 * NCH * P].rearrange("s (c a e) -> s c a e", c=NCH, a=4)
        pens_raw = A1[0:H1, 7 * NCH * P:7 * NCH * P + 2 * STEPS].rearrange("k (a s) -> k a s", a=2)
        whole_in, border_set, borders_out, pens_in = sem("whole_in"), sem("border_set"), sem("borders_out"), sem("pens_in")
        with nc.Block() as block:
            @block.gpsimd
            def _(pool):
                for c in range(NCH):
                    pool.indirect_dma_start(src_rows[0:CH, c * P:(c + 1) * P], None, src_flat,
                                            bass.IndirectOffsetOnAxis(ap=tile_i[0:CH, c:c + 1], axis=0)).then_inc(step_rows_in, 16)
                    pool.indirect_dma_start(dst_rows[0:CH, c * P:(c + 1) * P], None, dst_flat,
                                            bass.IndirectOffsetOnAxis(ap=tile_i[0:CH, c:c + 1], axis=0)).then_inc(step_rows_in, 16)

            @block.sync
            def _(sp):
                sp.wait_ge(rows_f, NCH)
                sp.wait_ge(ends_set, 2)
                sp.dma_start(dst_by_step[1:1 + STEPS * P].rearrange("(c s e) -> s c e", c=NCH, s=CH),
                             dst_whole[0:CH, :].rearrange("s (c e) -> s c e", c=NCH)).then_inc(whole_out, 16)
                sp.dma_start(dst_by_step[0:1].unsqueeze(0), step_ends[:, 0:1]).then_inc(whole_out, 16)
                sp.dma_start(dst_by_step[1 + STEPS * P:2 + STEPS * P].unsqueeze(0), step_ends[:, 1:2]).then_inc(whole_out, 16)
                sp.wait_ge(whole_out, 48)
                for off, t in enumerate((prev_d, cur_d, next_d)):
                    sp.dma_start(t[0:CH, :].rearrange("s (c e) -> s c e", c=NCH),
                                 dst_by_step[off:off + STEPS * P].rearrange("(c s e) -> s c e", c=NCH, s=CH)).then_inc(whole_in, 16)
                sp.wait_ge(border_set, 1)
                sp.dma_start(runs.rearrange("(c s) w -> s c w", c=NCH), border_rows[0:CH, :, :, :].rearrange("s c a e -> s c (a e)")).then_inc(borders_out, 16)
                with nc.allow_non_contiguous_dma("one element per step"):
                    for way, e in ((0, P - 1), (1, 0)):
                        sp.dma_start(row_pens_out[way].rearrange("(c s) -> s c", c=NCH).unsqueeze(2),
                                     border_rows[0:CH, :, 2 + way, e:e + 1]).then_inc(borders_out, 16)
                sp.wait_ge(borders_out, 48)
                for k in range(H1):
                    sp.dma_start(pens_raw[k:k + 1, :, :], row_pens_out.unsqueeze(0)).then_inc(pens_in, 16)
                sp.wait_ge(pens_in, 16 * H1)
                sp.wait_ge(seeds_zeroed, 16)

            @block.tensor
            def _(pe):
                pe.transpose(ps[0:KW, 0, 0:P], carry_col[:, 0, :], ident[:]).then_inc(carry_turned, 1)

                def turn_rows():
                    for c in range(NCH):
                        pe.wait_ge(rows_f, c + 1)
                        if c >= 2:
                            pe.wait_ge(rows_kept, c - 1)
                        pe.transpose(ps[:, 1 + c % 2, 0:CH], src_rf[0:CH, c * P:(c + 1) * P], ident[0:CH, 0:CH])
                        pe.transpose(ps[:, 1 + c % 2, P:P + CH], dst_rf[0:CH, c * P:(c + 1) * P], ident[0:CH, 0:CH]).then_inc(rows_turned, 1)

                def turn_squares(q):
                    pe.wait_ge(ea_loaded[q % EA_SLOTS], ea_loads(q))
                    if q >= 2:
                        pe.wait_ge(ea_kept, q - 1)
                    for t in range(EQ):
                        mm = pe.transpose(ps[:, 3 + 2 * (q % 2) + t // 4, (t % 4) * P:(t % 4 + 1) * P], ea_in[:, q % EA_SLOTS, t * P:(t + 1) * P], ident[:])
                    mm.then_inc(ea_turned, 1)

                turn_squares(0)
                pe.wait_ge(ve_placed, 16 * 9)
                for q in range(NQ):
                    if q + 1 < NQ:
                        turn_squares(q + 1)
                    pe.wait_ge(ea_kept, q + 1)
                    if q:
                        pe.wait_ge(ae_kept, q)
                    for t in range(EQ):
                        mm = pe.matmul(ps[:, 7, t * 24:(t + 1) * 24], ea_T[:, q % 2, t * P:(t + 1) * P], ve_diag[:], start=True, stop=True)
                    mm.then_inc(ae_done, 1)
                    if q == 3:
                        turn_rows()

            @block.scalar
            def _(act):
                def keep_scores(q):
                    act.wait_ge(ae_done, q + 1)
                    act.copy(a_edge[:, q * EQ * 8:(q + 1) * EQ * 8, :].rearrange("p c h -> p (c h)"),
                             ps[:, 7, 0:EQ * 24]).then_inc(ae_kept, 1)

                for q in range(NQ):
                    act.wait_ge(ea_turned, q + 1)
                    if q + EA_SLOTS < NQ:
                        load_squares(act, q + EA_SLOTS)
                    if q >= 2:
                        act.wait_ge(ae_done, q - 1)
                    first = 3 + 2 * (q % 2)
                    act.copy(ea_T[:, q % 2, 0:4 * P], ps[:, first, :])
                    act.copy(ea_T[:, q % 2, 4 * P:EQ * P], ps[:, first + 1, 0:(EQ - 4) * P]).then_inc(ea_kept, 1)
                    if q:
                        keep_scores(q - 1)
                    if q == 1:
                        std_root(act, a0_root, a0_rooted)
                keep_scores(NQ - 1)

            @block.vector
            def _(dve):
                dve.memset(step_ends[:, 0:1], -1.0).then_inc(ends_set, 1)
                dve.memset(step_ends[:, 1:2], -2.0).then_inc(ends_set, 1)
                dve.wait_ge(x_in, 32)
                node_stats(dve, xs)
                standardise(dve, (a0_root, a0_rooted), xs, relu_done=a0_norm)
                dve.wait_ge(step_rows_in, 2 * NCH * 16)
                for c in range(NCH):
                    dve.tensor_copy(src_rf[0:CH, c * P:(c + 1) * P], src_rows[0:CH, c * P:(c + 1) * P])
                    dve.tensor_copy(dst_whole[0:CH, c * P:(c + 1) * P], dst_rows[0:CH, c * P:(c + 1) * P])
                    dve.tensor_scalar(dst_rf[0:CH, c * P:(c + 1) * P], dst_rows[0:CH, c * P:(c + 1) * P],
                                      block_lo[0:CH, c:c + 1], None, ALU.subtract).then_inc(rows_f, 1)
                dve.wait_ge(carry_turned, 1)
                dve.tensor_copy(carry_row[:, 0, 0:P], ps[0:KW, 0, 0:P])
                for c in range(NCH):
                    dve.wait_ge(rows_turned, c + 1)
                    dve.tensor_copy(idx_step[:, c * CH:(c + 1) * CH], ps[:, 1 + c % 2, 0:CH])
                    dve.tensor_copy(dst_step[:, c * CH:(c + 1) * CH], ps[:, 1 + c % 2, P:P + CH]).then_inc(rows_kept, 1)
                dve.wait_ge(whole_in, 48)
                by_chunk = lambda t: t[0:CH, :].rearrange("s (c e) -> s c e", c=NCH)
                dve.tensor_tensor(border_rows[0:CH, :, 0, :], by_chunk(cur_d), by_chunk(prev_d), ALU.is_equal)
                link(dve, dve.tensor_tensor(border_rows[0:CH, :, 1, :], by_chunk(cur_d), by_chunk(next_d), ALU.is_equal))
                link(dve, dve.tensor_scalar(border_rows[0:CH, :, 0:2, :], border_rows[0:CH, :, 0:2, :], BIG, -BIG, ALU.mult, ALU.add))
                for c in range(NCH):
                    f, b = border_rows[0:CH, c, 0, :], border_rows[0:CH, c, 1, :][:, ::-1]
                    dve.tensor_tensor_scan(border_rows[0:CH, c, 2, :], f, f, 0.0, ALU.min, ALU.min)
                    last = dve.tensor_tensor_scan(border_rows[0:CH, c, 3, :][:, ::-1], b, b, 0.0, ALU.min, ALU.min)
                last.then_inc(border_set, 1)
                dve.wait_ge(pens_in, 16 * H1)
                dve.tensor_copy(row_pens[:, 0, :], pens_raw[:, 0, :])
                dve.tensor_copy(row_pens[:, 1, :], pens_raw[:, 1, ::-1])

        end_layer()
        open_rows(0)
        def turn_blocks(pe, source, ready, turned, kept, whole=False):
            for b in range(NB):
                g = b // 4
                if b % 4 == 0:
                    if ready is not None:
                        pe.wait_ge(ready, 1 if whole else g + 1)
                    if g >= 2:
                        pe.wait_ge(kept, g - 1)
                mm = pe.transpose(ps[:, g % 2, (b % 4) * P:(b % 4 + 1) * P], source[:, b, :], ident[:])
                if b % 4 == 3 or b == NB - 1:
                    mm.then_inc(turned, 1)

        def keep_blocks(act, target, turned, kept, scale=None):
            for g in range(TG):
                n = min(4, NB - 4 * g)
                act.wait_ge(turned, g + 1)
                got = ps[:, g % 2, 0:n * P].rearrange("p (b f) -> p b f", f=P)
                act.activation(target[:, 4 * g:4 * g + n, :], got, ACT.Copy if scale is None else ACT.Identity,
                               scale=1.0 if scale is None else scale).then_inc(kept, 1)

        def first_rows(pool, L, start, stop):
            for s in range(start, stop):
                pool.indirect_dma_start(gath[:, s, 0:tables[L].shape[1]], None, tables[L],
                                        bass.IndirectOffsetOnAxis(ap=idx_step[:, s:s + 1], axis=0)).then_inc(rows_in[L][0][s // HAND], 16)

        def scans(L, jobs):
            ends_ready = sem(f"L{L}_ends_ready")
            ends_turned = sem(f"L{L}_ends_turned")
            starts_ready = sem(f"L{L}_starts_ready")
            starts_turned = sem(f"L{L}_starts_turned")

            def run(dve, k, job, out, initial):
                K, source, draft, target, factor, frow, op0, op1, neutral, rev = job
                way = slice(None, None, -1) if rev else slice(None)
                return dve.tensor_tensor_scan(out[:, way], factor[:][:, way], source(k)[:, way], initial, op0, op1)

            with nc.Block() as block:
                @block.gpsimd
                def _(pool):
                    first_rows(pool, L, AHEAD[L][0], AHEAD[L][1])

                @block.vector
                def _(dve):
                    for n, job in enumerate(jobs):
                        K, source, draft, target, factor, frow, op0, op1, neutral, rev = job
                        for k in range(K):
                            link(dve, run(dve, k, job, draft(k), neutral))
                            end = draft(k)[:, 0:1] if rev else draft(k)[:, EC - 1:EC]
                            last = dve.tensor_copy(carry_col[:, n, k:k + 1], end)
                        last.then_inc(ends_ready, 1)
                    for n, job in enumerate(jobs):
                        K, source, draft, target, factor, frow, op0, op1, neutral, rev = job
                        dve.wait_ge(ends_turned, n + 1)
                        ends = carry_row[0:K, 3, 0:P]
                        link(dve, dve.tensor_copy(ends, ps[0:K, n, 0:P]))
                        if rev:
                            dve.memset(carry_row[0:K, 4 + n, P:P + 1], neutral)
                            link(dve, dve.tensor_tensor_scan(carry_row[0:K, 4 + n, 0:P][:, ::-1], carry_row[0:K, frow, 0:P][:, ::-1],
                                                             ends[:, ::-1], neutral, op0, op1))
                        else:
                            dve.memset(carry_row[0:K, 4 + n, 0:1], neutral)
                            link(dve, dve.tensor_tensor_scan(carry_row[0:K, 4 + n, 1:P + 1], carry_row[0:K, frow, 0:P],
                                                             ends, neutral, op0, op1))
                        dve.sem_inc(starts_ready, 1)
                    for n, job in enumerate(jobs):
                        K, source, draft, target, factor, frow, op0, op1, neutral, rev = job
                        dve.wait_ge(starts_turned, n + 1)
                        link(dve, dve.tensor_copy(carry_col[:, 2 + n, 0:K], ps[:, 2 + n, 0:K]))
                        for k in range(K):
                            link(dve, run(dve, k, job, target(k), carry_col[:, 2 + n, k:k + 1]))

                @block.tensor
                def _(pe):
                    for n, job in enumerate(jobs):
                        K = job[0]
                        pe.wait_ge(ends_ready, n + 1)
                        pe.transpose(ps[0:K, n, 0:P], carry_col[:, n, 0:K], ident[:]).then_inc(ends_turned, 1)
                    for n, job in enumerate(jobs):
                        K, rev = job[0], job[-1]
                        pe.wait_ge(starts_ready, n + 1)
                        starts = carry_row[0:K, 4 + n, 1:P + 1] if rev else carry_row[0:K, 4 + n, 0:P]
                        pe.transpose(ps[:, 2 + n, 0:K], starts, ident[0:K, 0:K]).then_inc(starts_turned, 1)

        def copy_down(L, K):
            scans(L, [(K, lambda k: DB[:, :, k], lambda k: A1[:, k * EC:(k + 1) * EC], lambda k: DB[:, :, k],
                             keep_f, 0, ALU.mult, ALU.add, 0.0, False)])

        def to_steps(L, K):
            out_done = sem(f"L{L}_edge_rows_out")
            chunk_in = [sem(f"L{L}_chunk_in{c}") for c in range(NCH)]
            chunk_turned = sem(f"L{L}_chunk_turned")
            chunk_kept = sem(f"L{L}_chunk_kept")
            rows = A1[:, 0:NCH * P * KW].rearrange("p (c e k) -> p c e k", c=NCH, k=KW)
            with nc.Block() as block:
                @block.sync
                def _(sp):
                    sp.dma_start(edge_rows.rearrange("a b -> (a b)").rearrange("(p c) -> p c", p=P),
                                 SE.rearrange("p c k -> p (c k)")).then_inc(out_done, 16)
                    sp.wait_ge(out_done, 16)

                @block.gpsimd
                def _(pool):
                    first_rows(pool, L, AHEAD[L][2], AHEAD[L][3])
                    pool.wait_ge(out_done, 16)
                    for c in range(NCH):
                        pool.indirect_dma_start(rows[0:CH, c, :, :].rearrange("p e k -> p (e k)"), None, edge_rows,
                                                bass.IndirectOffsetOnAxis(ap=tile_i[0:CH, c:c + 1], axis=0)).then_inc(chunk_in[c], 16)

                @block.tensor
                def _(pe):
                    for c in range(NCH):
                        pe.wait_ge(chunk_in[c], 16)
                        if c >= 2:
                            pe.wait_ge(chunk_kept, c - 1)
                        for k in range(K):
                            mm = pe.transpose(ps[:, (c % 2) * 2 + k // 4, (k % 4) * CH:(k % 4 + 1) * CH], rows[0:CH, c, :, k],
                                              ident[0:CH, 0:CH])
                        mm.then_inc(chunk_turned, 1)

                @block.vector
                def _(dve):
                    for c in range(NCH):
                        dve.wait_ge(chunk_turned, c + 1)
                        for g in range(-(-K // 4)):
                            n = min(4, K - 4 * g)
                            last = dve.tensor_copy(WS[:, c * CH:(c + 1) * CH, 4 * g:4 * g + n],
                                                   ps[:, (c % 2) * 2 + g, 0:n * CH].rearrange("p (k s) -> p s k", k=n))
                        last.then_inc(chunk_kept, 1)

        def row_pass(L, W):
            table = tables[L]
            width = table.shape[1]
            K = (1, H1, 0, H3)[L]
            HANDS = BODY // HAND
            BODIES = STEPS // BODY
            GPH = HAND // GROUP
            TURNS = {0: 5, 1: 5, 2: 0, 3: 2}[L]
            LINKS = {0: 6, 1: 9, 2: 0, 3: 3}[L]
            rows_of = rows_in[L]
            borders_in = [sem(f"L{L}_borders_in{q}") for q in range(2)]
            idx_copied = sem(f"L{L}_idx_copied")
            rows_used = sem(f"L{L}_rows_used")
            dve_rows = sem(f"L{L}_dve_rows")
            extras_ready = sem(f"L{L}_extras_ready")
            hot_ready = sem(f"L{L}_hot_ready")
            multiplied = sem(f"L{L}_multiplied")
            flushed = sem(f"L{L}_flushed")
            given = sem(f"L{L}_given")
            turned = sem(f"L{L}_turned")
            prep_chain = sem(f"L{L}_prep_chain")
            shifted_ready = sem(f"L{L}_shifted_ready")
            exponent_ready = sem(f"L{L}_exponent_ready")
            weights_ready = sem(f"L{L}_weights_ready")
            factor_ready = sem(f"L{L}_factor_ready")
            extras_copied = sem(f"L{L}_extras_copied")
            acc_scaled = sem(f"L{L}_acc_scaled")
            pool_turns = sem(f"L{L}_pool_turns")
            act_turns = sem(f"L{L}_act_turns")
            pe_turns = sem(f"L{L}_pe_turns")
            acc = A1[:, 0:NB * W].rearrange("p (b w) -> p b w", w=W)
            ring = [gath, A2[:, 0:BODY * RW].rearrange("p (s w) -> p s w", w=RW)]
            LEAD = 2 if L == 1 else 1
            SLOTS = LEAD * DEPTH
            hots = [onehot[:, j, :] for j in range(DEPTH * HAND)] + [wbuf[:, j * P:(j + 1) * P] for j in range(DEPTH * HAND)]
            spare = ((a_edge[:].rearrange("p c h -> p (c h)"), 6), (scan_tmp[:], 2))
            row_parts = [weighted[:]] + [t[:, 0:n * ACCW].rearrange("p (s w) -> p s w", w=ACCW) for t, n in spare]

            def row_slots(s, n):
                got, start = [], 0
                for part in row_parts:
                    a, b = max(s, start), min(s + n, start + part.shape[1])
                    if a < b:
                        got.append((a, part[:, a - start:b - start, :]))
                    start += part.shape[1]
                return got

            nmul = {0: D, 1: H1 * D, 2: 0, 3: D}[L]

            def loop(eng, body):
                with eng.Fori(0, BODIES // 2 - 1) as u:
                    for q in range(2):
                        body(u * 2 + q, q, False)
                for q in range(2):
                    body(BODIES - 2 + q, q, q == 1)

            with nc.Block() as block:
                @block.gpsimd
                def _(pool):
                    def body(i, q):
                        pool.wait_ge(idx_copied, i + 1)
                        pool.sem_inc(pool_turns, 1)
                        for h in range(HANDS):
                            if L == 2:
                                pool.wait_ge(flushed, i * (HANDS * GPH) + (h + 1) * GPH)
                            else:
                                pool.wait_ge(rows_used, i * HANDS + h + 1)
                            pool.sem_inc(pool_turns, 1)
                            if L == 1:
                                pool.wait_ge(dve_rows, i * HANDS + h + 1)
                                pool.sem_inc(pool_turns, 1)
                            for j in range(HAND):
                                s = h * HAND + j
                                pool.indirect_dma_start(ring[q][:, s, 0:width], None, table,
                                                        bass.IndirectOffsetOnAxis(ap=idx_ring[:, q, s:s + 1], axis=0)).then_inc(rows_of[q][h], 16)

                    first_rows(pool, L, AHEAD[L][3], BODY)
                    with pool.Fori(0, BODIES // 2 - 1) as u:
                        body(u * 2 + 1, 1)
                        body(u * 2 + 2, 0)
                    body(BODIES - 1, 1)

                @block.sync
                def _(sp):
                    if L > 1:
                        return
                    def load(i, q):
                        sp.dma_start(borders[:, q, :, :].rearrange("s a e -> s (a e)"), runs[bass.ds(i * BODY, BODY), :]).then_inc(borders_in[q], 16)
                    for q in range(2):
                        sp.dma_start(borders[:, q, :, :].rearrange("s a e -> s (a e)"), runs[q * BODY:(q + 1) * BODY, :]).then_inc(borders_in[q], 16)
                    with sp.Fori(0, BODIES // 2 - 1) as u:
                        for q in range(2):
                            sp.wait_ge(given, (u * 2 + q) * TURNS + 4)
                            load(u * 2 + q + 2, q)
                    for q in range(2):
                        sp.wait_ge(borders_in[q], 16 * (BODIES // 2))

                @block.scalar
                def _(act):
                    act.copy(idx_ring[:].rearrange("p a b -> p (a b)"), idx_step[:, 0:2 * BODY]).then_inc(idx_copied, 2)
                    if L < 2:
                        act.sem_inc(rows_used, 2 * HANDS)
                    if L == 3:
                        act.sem_inc(extras_ready, 2 * HANDS)

                    def weigh_edges(i, q):
                        act.wait_ge(shifted_ready, i + 1)
                        act.sem_inc(act_turns, 1)
                        act.wait_ge(rows_used, i * HANDS + HANDS)
                        act.sem_inc(act_turns, 1)
                        if L == 1:
                            act.wait_ge(dve_rows, i * HANDS + HANDS)
                            act.sem_inc(act_turns, 1)
                        if L == 3:
                            act.wait_ge(extras_ready, i * HANDS + HANDS)
                            act.sem_inc(act_turns, 1)
                            act.activation(weights[:, q], scores[:], ACT.Exp, bias=rescale[:, 2, 0:1]).then_inc(weights_ready, 1)
                            return
                        n = 2 * H1 if L == 1 else 1
                        act.activation(weights[:, q, :, 0:n], shifted[:, :, 0:n], ACT.Exp).then_inc(weights_ready, 1)
                        if L == 0:
                            steps = WS[:, i * BODY:(i + 1) * BODY, 1:5] if isinstance(i, int) else WS[:, bass.ds(i * BODY, BODY), 1:5]
                            act.copy(weights[:, q, :, 1:5], steps).then_inc(extras_copied, 1)

                    def factor(i, q):
                        if L < 2:
                            act.wait_ge(exponent_ready, i + 1)
                            act.sem_inc(act_turns, 1)
                        n = 1 if L == 3 else K
                        act.activation(rescale[:, 1, 0:n], rescale[:, 0, 0:n], ACT.Exp).then_inc(factor_ready, 1)

                    def body(i, q, last):
                        if L == 2:
                            for h in range(HANDS):
                                act.wait_ge(rows_of[q][h], (i + 2 - q) * (8 * HAND))
                                act.sem_inc(act_turns, 1)
                        else:
                            act.wait_ge(weights_ready, i + 1)
                            act.sem_inc(act_turns, 1)
                        if L == 0:
                            act.wait_ge(extras_copied, i + 1)
                            act.sem_inc(act_turns, 1)
                        act.wait_ge(idx_copied, i + 2)
                        act.sem_inc(act_turns, 1)
                        act.copy(idx_ring[:, q, :], idx_step[:, bass.ds(i * BODY + 2 * BODY, BODY)] if not isinstance(i, int) else
                                 idx_step[:, min(i + 2, BODIES) * BODY:min(i + 2, BODIES) * BODY + BODY]).then_inc(idx_copied, 1)
                        if L == 2:
                            return
                        for h in range(HANDS):
                            act.wait_ge(multiplied, i * HANDS + h + 1)
                            act.sem_inc(act_turns, 1)
                            slot = (h % SLOTS) * HAND
                            for a, part in row_slots(slot, HAND):
                                first = h * HAND + a - slot
                                act_last = act.copy(part[:, :, nmul:W], weights[:, q, first:first + part.shape[1], 0:W - nmul])
                            if L == 3:
                                act_last.then_inc(extras_ready, 1)
                            else:
                                for j in range(HAND):
                                    for k in range(1 if L == 0 else H1 - 1 if j < DVE_STEPS else H1):
                                        s = h * HAND + j
                                        act_last = act.activation(row_slots(slot + j, 1)[0][1][:, 0, k * D:(k + 1) * D], ring[q][:, s, 0:D], ACT.Copy,
                                                                  scale=weights[:, q, s, k:k + 1])
                                act_last.then_inc(rows_used, 1)
                            if h == 0:
                                factor(i, q)
                        if not last:
                            weigh_edges(i + 1, 1 - q)

                    if L != 2:
                        weigh_edges(0, 0)
                    loop(act, body)

                @block.vector
                def _(dve):
                    link(dve, dve.memset(A1[:, 0:NB * W], 0.0))
                    if L < 2:
                        dve.memset(row_f[0:K, 0:BODY + 1], -BIG)
                        dve.memset(row_b[0:K, 0:BODY + 1], -BIG)
                        link(dve, dve.memset(last_max[:], -BIG))
                    if L == 1:
                        dve.sem_inc(dve_rows, 2 * HANDS)
                    if L == 3:
                        dve.sem_inc(rows_used, 2 * HANDS)
                        link(dve, dve.memset(carry_row[0:1, 3, 0:2], -BIG))

                    chain = [0]

                    def tie(i, ins):
                        chain[0] += 1
                        ins.then_inc(prep_chain, 1)
                        dve.wait_ge(prep_chain, i * LINKS + chain[0])

                    def hot(i, h):
                        dve.wait_ge(multiplied, i * HANDS + h + 1)
                        for j in range(HAND):
                            col = i * BODY + h * HAND + j
                            col = dst_step[:, col:col + 1] if isinstance(i, int) else dst_step[:, bass.ds(col, 1)]
                            last = dve.tensor_scalar(hots[(h % SLOTS) * HAND + j], iota_row[:], col, None, ALU.is_equal)
                        last.then_inc(hot_ready, 1)

                    def steps_of(i, k0, k1):
                        return WS[:, i * BODY:(i + 1) * BODY, k0:k1] if isinstance(i, int) else WS[:, bass.ds(i * BODY, BODY), k0:k1]

                    def rows_landed(i, q):
                        for h in range(HANDS):
                            dve.wait_ge(rows_of[q][h], (i + 2 - q) * (8 * HAND))

                    def score(i, q):
                        rows_landed(i, q)
                        chain[0] = 0
                        if L == 0:
                            dve.tensor_copy(topped[:, :, 0:1], ring[q][:, :, D:D + 1]).then_inc(given, 1)
                            return
                        s = scores[:, :, 0:H1]
                        tie(i, dve.tensor_tensor(s, ring[q][:, :, D:D + H1], steps_of(i, 0, H1), ALU.add))
                        tie(i, dve.scalar_tensor_tensor(out=s, in0=s, scalar=0.2, in1=s, op0=ALU.mult, op1=ALU.max))
                        dve.tensor_tensor(topped[:], s, steps_of(i, H1, 2 * H1), ALU.max).then_inc(given, 1)

                    def run_maxima(i, q):
                        dve.wait_ge(borders_in[q], (i + 2 - q) * 8)
                        dve.wait_ge(turned, i * TURNS + 1)
                        for k in range(K):
                            v = ps[0:BODY, 4, k * P:(k + 1) * P]
                            dve.tensor_tensor_scan(run_f[:, k, :], borders[:, q, 0, :], v, -BIG, ALU.add, ALU.max)
                            last = dve.tensor_tensor_scan(run_b[:, k, :][:, ::-1], borders[:, q, 1, :][:, ::-1], v[:, ::-1], -BIG, ALU.add, ALU.max)
                        last.then_inc(given, 1)

                    def step_maxima(i, q):
                        dve.wait_ge(turned, i * TURNS + 2)
                        tie(i, dve.tensor_copy(row_f[0:K, 0:1], row_f[0:K, BODY:BODY + 1]))
                        start, turn = i * BODY, (i * -BODY) + (STEPS - BODY)
                        if isinstance(i, int):
                            pens_f, pens_b = row_pens[0:K, 0, start:start + BODY], row_pens[0:K, 1, turn:turn + BODY]
                        else:
                            pens_f, pens_b = row_pens[0:K, 0, bass.ds(start, BODY)], row_pens[0:K, 1, bass.ds(turn, BODY)]
                        dve.tensor_tensor_scan(row_f[0:K, 1:BODY + 1], pens_f, ps[0:K, 5, 0:BODY], row_f[0:K, 0:1], ALU.add, ALU.max)
                        dve.tensor_tensor_scan(row_b[0:K, 0:BODY][:, ::-1], pens_b, ps[0:K, 5, BODY:2 * BODY][:, ::-1],
                                               -BIG, ALU.add, ALU.max).then_inc(given, 1)

                    def join(i, q):
                        dve.wait_ge(turned, i * TURNS + 3)
                        tie(i, dve.tensor_copy(row_col[:, :, 0:K], ps[0:BODY, 5, 64:64 + 2 * KW].rearrange("s (a k) -> s a k", a=2)[:, :, 0:K]))
                        for way in range(2):
                            for k in range(K):
                                ins = dve.scalar_tensor_tensor(out=run_f[:, k, :], in0=borders[:, q, 2 + way, :], scalar=row_col[:, way, k:k + 1],
                                                               in1=run_f[:, k, :], op0=ALU.add, op1=ALU.max)
                                if k == K - 1:
                                    tie(i, ins)
                        dve.tensor_tensor(run_f[:, 0:K, :], run_f[:, 0:K, :], run_b[:, 0:K, :], ALU.max).then_inc(given, 1)

                    def shift(i, q):
                        dve.wait_ge(turned, i * TURNS + 4)
                        got = ps[:, 6, 0:K * BODY].rearrange("p (k s) -> p s k", k=K)
                        dve.tensor_copy(edge_cols[:, 0, 0:K], got[:, 0, :])
                        first = dst_step[:, i * BODY:i * BODY + 1] if isinstance(i, int) else dst_step[:, bass.ds(i * BODY, 1)]
                        dve.tensor_copy(edge_cols[:, 0, K:K + 1], first)
                        dve.tensor_copy(edge_cols[:, 1, 0:K], got[:, BODY - 1, :]).then_inc(given, 1)
                        if L == 0:
                            dve.tensor_tensor(shifted[:, :, 0:1], topped[:, :, 0:1], got, ALU.subtract).then_inc(shifted_ready, 1)
                            return
                        dve.tensor_tensor(shifted[:, :, 0:H1], scores[:, :, 0:H1], got, ALU.subtract)
                        tie(i, dve.tensor_tensor(shifted[:, :, H1:2 * H1], steps_of(i, H1, 2 * H1), got, ALU.subtract))
                        dve.tensor_tensor(shifted[:, :, H1:2 * H1], shifted[:, :, H1:2 * H1],
                                          steps_of(i, 2 * H1, 2 * H1 + 1).broadcast_to([P, BODY, H1]), ALU.add).then_inc(shifted_ready, 1)

                    def exponent(i, q):
                        dve.wait_ge(turned, i * TURNS + 5)
                        dve.tensor_scalar(first_hot[:], ps[:, 7, K:K + 1], iota_p[:, 0:1], None, ALU.is_equal)
                        tie(i, dve.tensor_tensor(rescale[:, 0, 0:K], last_max[:, 0:K], ps[:, 7, 0:K], ALU.subtract))
                        dve.tensor_scalar(rescale[:, 0, 0:K], rescale[:, 0, 0:K], 0.0, None, ALU.min).then_inc(exponent_ready, 1)
                        tie(i, dve.tensor_copy(last_max[:, 0:K], ps[:, 7, 16:16 + K]))

                    def score3(i, q):
                        rows_landed(i, q)
                        chain[0] = 0
                        tie(i, dve.tensor_tensor(scores[:], ring[q][:, :, D:D + H3], steps_of(i, 0, H3), ALU.add))
                        tie(i, dve.scalar_tensor_tensor(out=scores[:], in0=scores[:], scalar=0.2, in1=scores[:], op0=ALU.mult, op1=ALU.max))
                        dve.tensor_reduce(last_max[:, 0:1], scores[:], AX.XY, ALU.max).then_inc(given, 1)

                    def top3(i, q):
                        dve.wait_ge(turned, i * TURNS + 1)
                        dve.tensor_copy(carry_row[0:1, 3, 1:2], carry_row[0:1, 3, 0:1])
                        tie(i, dve.tensor_reduce(carry_row[0:1, 3, 2:3], ps[0:1, 4, 0:P], AX.X, ALU.max))
                        dve.tensor_tensor(carry_row[0:1, 3, 0:1], carry_row[0:1, 3, 2:3], carry_row[0:1, 3, 1:2], ALU.max).then_inc(given, 1)

                    def shift3(i, q):
                        dve.wait_ge(turned, i * TURNS + 2)
                        dve.tensor_scalar(rescale[:, 2, 0:1], ps[:, 5, 0:1], -1.0, None, ALU.mult)
                        dve.tensor_copy(edge_cols[:, 0, 0:2], ps[:, 5, 0:2]).then_inc(acc_scaled, 1)
                        dve.wait_ge(acc_scaled, i * 2 + 1)
                        dve.tensor_tensor(rescale[:, 0, 0:1], edge_cols[:, 0, 1:2], edge_cols[:, 0, 0:1], ALU.subtract).then_inc(shifted_ready, 1)

                    stages = {0: {1: score, 2: run_maxima, 3: step_maxima, 4: join, 5: shift, 6: exponent},
                              2: {}, 3: {3: score3, 4: top3, 5: shift3}}
                    stages[1] = stages[0]

                    def scale_acc(i):
                        dve.wait_ge(factor_ready, i + 1)
                        if L == 3:
                            dve.wait_ge(flushed, (i + 2) * (HANDS * GPH))
                            dve.tensor_scalar(A1[:, 0:NB * W], A1[:, 0:NB * W], rescale[:, 1, 0:1], None, ALU.mult).then_inc(acc_scaled, 1)
                            return
                        dve.scalar_tensor_tensor(out=rescale[:, 2, 0:K], in0=rescale[:, 1, 0:K], scalar=-1.0,
                                                 in1=first_hot[:].broadcast_to([P, K]), op0=ALU.add, op1=ALU.mult).then_inc(acc_scaled, 1)
                        dve.wait_ge(acc_scaled, i * 3 + 1)
                        dve.tensor_scalar(rescale[:, 2, 0:K], rescale[:, 2, 0:K], 1.0, None, ALU.add).then_inc(acc_scaled, 1)
                        b = group_block(i, 0)
                        dve.wait_ge(acc_scaled, i * 3 + 2)
                        if L == 0:
                            a = acc[:, bass.ds(b, 1), 0:D + 1].rearrange("p o w -> p (o w)")
                            dve.wait_ge(flushed, (i + 2) * (HANDS * GPH))
                            dve.tensor_scalar(a, a, rescale[:, 2, 0:1], None, ALU.mult).then_inc(acc_scaled, 1)
                            return
                        dve.wait_ge(flushed, (i + 2) * (HANDS * GPH))
                        a = acc[:, bass.ds(b, 1), 0:H1 * D].rearrange("p o (k f) -> p (o k) f", k=H1)
                        dve.tensor_tensor(a, a, rescale[:, 2, 0:K].unsqueeze(2).broadcast_to([P, H1, D]), ALU.mult)
                        a = acc[:, bass.ds(b, 1), H1 * D:W].rearrange("p o (a k) -> p (o a) k", a=2)
                        dve.tensor_tensor(a, a, rescale[:, 2, 0:K].unsqueeze(1).broadcast_to([P, 2, H1]), ALU.mult).then_inc(acc_scaled, 1)

                    def group_block(i, g):
                        gg = i * (BODY // GROUP) + g
                        col = blk_reg[0:1, gg:gg + 1] if isinstance(gg, int) else blk_reg[0:1, bass.ds(gg, 1)]
                        return dve.value_load(col, min_val=0, max_val=NB - 1)

                    def weigh(i, q, h):
                        if h == 0:
                            dve.wait_ge(weights_ready, i + 1)
                        dve.wait_ge(multiplied, i * HANDS + h + 1)
                        for j in range(DVE_STEPS if L == 1 else HAND):
                            s, slot = h * HAND + j, row_slots((h % SLOTS) * HAND + j, 1)[0][1][:, 0, :]
                            if L == 1:
                                ins = dve.tensor_scalar(slot[:, (H1 - 1) * D:H1 * D], ring[q][:, s, 0:D],
                                                        weights[:, q, s, H1 - 1:H1], None, ALU.mult)
                            else:
                                ins = dve.tensor_tensor(slot[:, 0:D].rearrange("p (k c) -> p k c", c=C3),
                                                        ring[q][:, s, 0:D].rearrange("p (k c) -> p k c", c=C3),
                                                        weights[:, q, s, :].unsqueeze(2).broadcast_to([P, H3, C3]), ALU.mult)
                        ins.then_inc(dve_rows if L == 1 else rows_used, 1)

                    def body(i, q, last):
                        for h in range(HANDS):
                            ahead = h + LEAD
                            if L in (1, 3) and ahead < HANDS:
                                weigh(i, q, ahead)
                            elif L in (1, 3) and not last:
                                weigh(i + 1, 1 - q, ahead - HANDS)
                            hot(i, ahead)
                            if h == 0 and L != 2:
                                scale_acc(i)
                            for g in range(GPH):
                                b = group_block(i, h * GPH + g)
                                a = acc[:, bass.ds(b, 1), :].rearrange("p o w -> p (o w)")
                                if g == 0:
                                    dve.wait_ge(multiplied, i * HANDS + h + 1 + SLOTS)
                                    if h == 0 and L != 2:
                                        dve.wait_ge(acc_scaled, (i + 1) * (2 if L == 3 else 3))
                                dve.wait_ge(flushed, i * (HANDS * GPH) + h * GPH + g + 2 * HANDS * GPH)
                                dve.tensor_tensor(a, a, ps[:, (h % DEPTH) * GPH + g, 0:W], ALU.add).then_inc(flushed, 1)
                            if h in stages[L] and not last:
                                stages[L][h](i + 1, 1 - q)

                    for h in range(LEAD):
                        hot(0, h)
                    for h in sorted(stages[L]):
                        stages[L][h](0, 0)
                    if L in (1, 3):
                        for h in range(LEAD):
                            weigh(0, 0, h)
                    loop(dve, body)

                @block.tensor
                def _(pe):
                    pe.sem_inc(multiplied, SLOTS)
                    pe.sem_inc(flushed, 2 * HANDS * GPH)

                    def after(i, n):
                        pe.wait_ge(given, i * TURNS + n)
                        pe.sem_inc(pe_turns, 1)

                    def turn_scores(i, q):
                        after(i, 1)
                        for k in range(K):
                            mm = pe.transpose(ps[0:BODY, 4, k * P:(k + 1) * P], topped[:, :, k], ident[:])
                        mm.then_inc(turned, 1)

                    def turn_ends(i, q):
                        after(i, 2)
                        pe.transpose(ps[0:K, 5, 0:BODY], run_f[:, 0:K, P - 1], ident[0:BODY, 0:BODY])
                        pe.transpose(ps[0:K, 5, BODY:2 * BODY], run_b[:, 0:K, 0], ident[0:BODY, 0:BODY]).then_inc(turned, 1)

                    def turn_rows(i, q):
                        after(i, 3)
                        pe.transpose(ps[0:BODY, 5, 64:64 + K], row_f[0:K, 0:BODY], ident[0:K, 0:K])
                        pe.transpose(ps[0:BODY, 5, 64 + KW:64 + KW + K], row_b[0:K, 1:BODY + 1], ident[0:K, 0:K]).then_inc(turned, 1)

                    def turn_back(i, q):
                        after(i, 4)
                        for k in range(K):
                            mm = pe.transpose(ps[:, 6, k * BODY:(k + 1) * BODY], run_f[:, k, :], ident[0:BODY, 0:BODY])
                        mm.then_inc(turned, 1)

                    def spread(i, q):
                        after(i, 5)
                        pe.matmul(ps[:, 7, 0:K + 1], pick_first[:], edge_cols[:, 0, 0:K + 1], start=True, stop=True)
                        pe.matmul(ps[:, 7, 16:16 + K], pick_last[:], edge_cols[:, 1, 0:K], start=True, stop=True).then_inc(turned, 1)

                    def turn_top3(i, q):
                        after(i, 1)
                        pe.transpose(ps[0:1, 4, 0:P], last_max[:, 0:1], ident[:]).then_inc(turned, 1)

                    def spread3(i, q):
                        after(i, 2)
                        pe.matmul(ps[:, 5, 0:2], ones[0:1, :], carry_row[0:1, 3, 0:2], start=True, stop=True).then_inc(turned, 1)

                    stages = {0: {2: turn_scores, 3: turn_ends, 4: turn_rows, 5: turn_back, 6: spread},
                              2: {}, 3: {4: turn_top3, 5: spread3}}
                    stages[1] = stages[0]

                    def body(i, q, last):
                        for h in range(HANDS):
                            pe.wait_ge(hot_ready, i * HANDS + h + 1)
                            pe.wait_ge(flushed, i * (HANDS * GPH) + (h + 1 + 2 * HANDS - DEPTH) * GPH)
                            if L == 2:
                                pe.wait_ge(rows_of[q][h], (i + 2 - q) * (8 * HAND))
                            else:
                                pe.wait_ge(rows_used, i * HANDS + h + 1 + 2 * HANDS)
                            if L == 1:
                                pe.wait_ge(dve_rows, i * HANDS + h + 1 + 2 * HANDS)
                            if L == 3:
                                pe.wait_ge(extras_ready, i * HANDS + h + 1 + 2 * HANDS)
                            for j in range(HAND):
                                s = (h % SLOTS) * HAND + j
                                rhs = ring[q][:, h * HAND + j, 0:D] if L == 2 else row_slots(s, 1)[0][1][:, 0, 0:W]
                                mm = pe.matmul(ps[:, (h % DEPTH) * GPH + j // GROUP, 0:W], hots[s], rhs,
                                               start=(j % GROUP == 0), stop=(j % GROUP == GROUP - 1))
                            mm.then_inc(multiplied, 1)
                            if h in stages[L] and not last:
                                stages[L][h](i + 1, 1 - q)

                    for h in sorted(stages[L]):
                        stages[L][h](0, 0)
                    loop(pe, body)
            return acc

        def node_products(pe, lhs, rhs, width, ready, done, per_bank=4):
            pe.wait_ge(*ready)
            for b in range(NB):
                mm = pe.matmul(ps[:, 2 + b // per_bank, (b % per_bank) * width:(b % per_bank + 1) * width], lhs[:, b, :], rhs, start=True, stop=True)
            mm.then_inc(done, 1)


        def wide_products(pe, lhs, rhs, kept, done, used):
            for b in range(NB):
                g = b // 4
                if b % 4 == 0:
                    pe.wait_ge(kept, g + 1)
                    if g >= 2:
                        pe.wait_ge(used, g - 1)
                mm = pe.matmul(ps[:, 2 + g % 2, (b % 4) * P:(b % 4 + 1) * P], lhs[:, b, :], rhs, start=True, stop=True)
                if b % 4 == 3 or b == NB - 1:
                    mm.then_inc(done, 1)

        def bank_squares(g):
            n = min(4, NB - 4 * g)
            return slice(4 * g, 4 * g + n), ps[:, 2 + g % 2, 0:n * P].rearrange("p (b f) -> p b f", f=P)

        def write_table(sp, L, source, ready, out_done):
            sp.wait_ge(*ready)
            sp.dma_start(tables[L].rearrange("(b p) w -> p b w", p=P), source).then_inc(out_done, 16)
            sp.wait_ge(out_done, 16)

        wT = wbuf[:, 0:P]
        mask_col = ve_col[:, 3:4]
        attn_bc = bias_row
        a0_in = sem("a0_in")
        a0_turned, a0_kept, a0_done, a0_used = sem("a0_turned"), sem("a0_kept"), sem("a0_done"), sem("a0_used")
        a0_wt, a0_wk, a0_table, a0_scored = sem("a0_wt"), sem("a0_wk"), sem("a0_table"), sem("a0_scored")
        with nc.Block() as block:
            @block.sync
            def _(sp):
                sp.dma_start(wnat[:, 0:P], L0_W).then_inc(a0_in, 16)
                with nc.allow_non_contiguous_dma("one column"):
                    sp.dma_start(mask_col, L0_mask.unsqueeze(1)).then_inc(a0_in, 16)
                sp.dma_start(attn_bc[:], L0_attn.unsqueeze(0).broadcast_to([P, D])).then_inc(a0_in, 16)
                write_table(sp, 0, tab[:, :, 0:D + 1], (a0_scored, 1), a0_table)

            @block.vector
            def _(dve):
                dve.memset(SE[:, :, 0:1], 0.0)
                dve.tensor_copy(SE[:, :, 1:1 + H1], a_edge[:])
                dve.memset(SE[:, :, 4:5], 1.0)
                dve.memset(SE[:, :, 5:KW], 0.0)
                dve.wait_ge(a0_wt, 1)
                dve.tensor_copy(wT, ps[:, 4, 0:P]).then_inc(a0_wk, 1)
                for g in range(TG):
                    bs, got = bank_squares(g)
                    dve.wait_ge(a0_done, g + 1)
                    dve.tensor_copy(hW[:, bs, :], got).then_inc(a0_used, 1)
                dve.wait_ge(a0_used, TG)
                dve.wait_ge(a0_in, 48)
                link(dve, dve.tensor_tensor(tmp, hW, per_feature(attn_bc[:]), ALU.mult))
                link(dve, dve.tensor_reduce(scal[:, 0, :], tmp, AX.X, ALU.add))
                dve.scalar_tensor_tensor(out=tab[:, :, D], in0=scal[:, 0, :], scalar=0.01, in1=scal[:, 0, :],
                                         op0=ALU.mult, op1=ALU.max).then_inc(a0_scored, 1)

            @block.scalar
            def _(act):
                act.wait_ge(a0_in, 48)
                keep_blocks(act, hT, a0_turned, a0_kept, scale=mask_col)

            @block.tensor
            def _(pe):
                pe.wait_ge(a0_in, 48)
                pe.transpose(ps[:, 4, 0:P], wnat[:, 0:P], ident[:]).then_inc(a0_wt, 1)
                turn_blocks(pe, hs, None, a0_turned, a0_kept)
                pe.wait_ge(a0_wk, 1)
                wide_products(pe, hT, wT, a0_kept, a0_done, a0_used)

        to_steps(0, 5)
        acc = row_pass(0, D + 5)

        loop_score = sb("loop_score", [P, H1, NB])
        f0_ready, f0_done, f0_blocks = sem("f0_ready"), sem("f0_done"), sem("f0_blocks")
        with nc.Block() as block:
            @block.vector
            def _(dve):
                den, rec = small[:, 0, :], small[:, 1, :]
                dve.tensor_copy(deg[:], acc[:, :, D + 4])
                link(dve, dve.tensor_scalar(den, acc[:, :, D], 0.5, None, ALU.max))
                link(dve, dve.reciprocal(rec, den))
                link(dve, dve.tensor_tensor(hs[:], acc[:, :, 0:D], per_node(rec), ALU.mult))
                link(dve, dve.scalar_tensor_tensor(out=xs[:], in0=hs[:], scalar=0.0, in1=xs[:], op0=ALU.max, op1=ALU.add))
                link(dve, dve.tensor_scalar(den, deg[:], 1.0, None, ALU.max))
                link(dve, dve.reciprocal(rec, den))
                for k in range(H1):
                    dve.tensor_tensor(loop_score[:, k, :], acc[:, :, D + 1 + k], rec, ALU.mult)
                dve.wait_ge(f0_done, 1)
                totals, upto, node_no, first = small[:, 2, :], small[:, 3, :], small[:, 4, :], small[:, 5, :]
                link(dve, dve.tensor_copy(totals, ps[:, 1, 0:NB]))
                link(dve, dve.tensor_tensor_scan(upto, ones[:, 0:NB], totals, 0.0, ALU.mult, ALU.add))
                link(dve, dve.tensor_tensor(upto, upto, totals, ALU.subtract))
                link(dve, dve.tensor_tensor(first, upto, ps[:, 0, 0:NB], ALU.add))
                link(dve, dve.tensor_scalar(node_no, iota_hi[:], float(P), iota_p[:, 0:1], ALU.mult, ALU.add))
                link(dve, dve.tensor_scalar(node_no, node_no, float(EP), None, ALU.add))
                link(dve, dve.tensor_tensor(node_no, node_no, first, ALU.subtract))
                link(dve, dve.tensor_scalar(den, deg[:], 0.0, None, ALU.is_equal))
                link(dve, dve.tensor_tensor(node_no, node_no, den, ALU.mult))
                link(dve, dve.tensor_tensor(seed_idx[:], node_no, first, ALU.add))

            @block.tensor
            def _(pe):
                pe.matmul(ps[:, 0, 0:NB], tri[:], acc[:, :, D + 4], start=True, stop=True)
                pe.matmul(ps[:, 1, 0:NB], ones[:], acc[:, :, D + 4], start=True, stop=True).then_inc(f0_done, 1)

        def scatter_seeds(pool, done):
            for b in range(NB):
                pool.indirect_dma_start(seeds, bass.IndirectOffsetOnAxis(ap=seed_idx[:, b:b + 1], axis=0),
                                        seed_vals[:, b, :], None).then_inc(done, 16)
            pool.wait_ge(done, 16 * NB)

        end_layer()
        open_rows(1)

        U = wbuf[:, 1152 - 2 * H1:1152]
        att_bc = A2[:, 1024:1024 + 2 * 384]
        u_prods = A2[:, 2048:2048 + 768]
        a1_in, a1_root, a1_rooted, a1_norm = sem("a1_in"), sem("a1_root"), sem("a1_rooted"), sem("a1_norm")
        a1_turned, a1_kept, a1_done = sem("a1_turned"), sem("a1_kept"), sem("a1_done")
        a1_u, a1_seed, a1_seeded, a1_table = sem("a1_u"), sem("a1_seed"), sem("a1_seeded"), sem("a1_table")
        with nc.Block() as block:
            @block.sync
            def _(sp):
                sp.dma_start(wnat[:], L1_W).then_inc(a1_in, 16)
                sp.dma_start(att_bc[:, 0:384], L1_as.rearrange("h c -> (h c)").unsqueeze(0).broadcast_to([P, 384])).then_inc(a1_in, 16)
                sp.dma_start(att_bc[:, 384:768], L1_ad.rearrange("h c -> (h c)").unsqueeze(0).broadcast_to([P, 384])).then_inc(a1_in, 16)
                write_table(sp, 1, tab[:, :, 0:D + H1], (a1_seed, 1), a1_table)

            @block.gpsimd
            def _(pool):
                pool.wait_ge(a1_seed, 1)
                scatter_seeds(pool, a1_seeded)

            @block.vector
            def _(dve):
                dve.memset(A2[:, 0:NB * KW], 0.0)
                node_stats(dve, xs)
                standardise(dve, (a1_root, a1_rooted), xs, relu_done=a1_norm)
                dve.wait_ge(a1_norm, TG)
                dve.tensor_copy(tab[:, :, 0:D], hs[:])
                dve.wait_ge(a1_in, 48)
                for k in range(2):
                    u_prod = u_prods[:, k * 384:(k + 1) * 384]
                    link(dve, dve.tensor_tensor(u_prod, wnat[:], att_bc[:, k * 384:(k + 1) * 384], ALU.mult))
                    last = dve.tensor_reduce(U[:, k * H1:(k + 1) * H1], u_prod.rearrange("p (h c) -> p h c", c=D), AX.X, ALU.add)
                last.then_inc(a1_u, 1)
                dve.wait_ge(a1_done, 1)
                got = ps[:, 2, 0:NB * 2 * H1].rearrange("p (b k) -> p k b", k=2 * H1)
                link(dve, dve.tensor_copy(scal[:, 0:2 * H1, :], got))
                dve.tensor_copy(tab[:, :, D:D + H1].rearrange("p b k -> p k b"), scal[:, 0:H1, :])
                dve.tensor_copy(seed_vals[:, :, 0:H1].rearrange("p b k -> p k b"), scal[:, H1:2 * H1, :])
                link(dve, dve.tensor_tensor(loop_score[:], loop_score[:], scal[:, 0:H1, :], ALU.add))
                link(dve, dve.tensor_tensor(loop_score[:], loop_score[:], scal[:, H1:2 * H1, :], ALU.add))
                dve.scalar_tensor_tensor(out=seed_vals[:, :, H1:2 * H1].rearrange("p b k -> p k b"), in0=loop_score[:], scalar=0.2,
                                         in1=loop_score[:], op0=ALU.mult, op1=ALU.max).then_inc(a1_seed, 1)

            @block.scalar
            def _(act):
                std_root(act, a1_root, a1_rooted)
                keep_blocks(act, hT, a1_turned, a1_kept)

            @block.tensor
            def _(pe):
                turn_blocks(pe, hs, a1_norm, a1_turned, a1_kept)
                pe.wait_ge(a1_kept, TG)
                node_products(pe, hT, U, 2 * H1, (a1_u, 1), a1_done, per_bank=NB)

        db1_in = sem("db1_in")
        with nc.Block() as block:
            @block.gpsimd
            def _(pool):
                first_rows(pool, 1, 0, AHEAD[1][0])

            @block.sync
            def _(sp):
                sp.dma_start(A3[:, 0:EC * KW], seeds_edges.rearrange("(p c) k -> p (c k)", p=P)).then_inc(db1_in, 16)
                sp.wait_ge(db1_in, 16)
        copy_down(1, 2 * H1)
        with nc.Block() as block:
            @block.gpsimd
            def _(pool):
                first_rows(pool, 1, AHEAD[1][1], AHEAD[1][2])

            @block.vector
            def _(dve):
                dve.tensor_tensor(SE[:, :, 0:H1], DB[:, :, 0:H1], a_edge[:], ALU.add)
                dve.tensor_copy(SE[:, :, H1:2 * H1], DB[:, :, H1:2 * H1])
                dve.tensor_scalar(SE[:, :, 2 * H1], keep_f[:], -BIG, None, ALU.mult)
                dve.memset(SE[:, :, 2 * H1 + 1:KW], 0.0)

        to_steps(1, 2 * H1 + 1)
        acc = row_pass(1, H1 * D + 2 * H1)

        whT = A2[:, 0:384]
        lin = A2[:, 384:768]
        V = A2[:, 768:1152]
        gb_col = A2[:, 1152:1155]
        gb_wide = A2[:, 1280:1664]
        aggT = A2[:, 2048:2048 + 2 * 384]
        g_bc, b_bc, lb_bc = wnat[:, 0:D], wnat[:, D:2 * D], wnat[:, 2 * D:3 * D]
        f1_in, f1_late, f1_wt, f1_wk, f1_v, f1_vk = sem("f1_in"), sem("f1_late"), sem("f1_wt"), sem("f1_wk"), sem("f1_v"), sem("f1_vk")
        f1_mean, f1_turned, f1_kept, f1_y, f1_used = sem("f1_mean"), sem("f1_turned"), sem("f1_kept"), sem("f1_y"), sem("f1_used")
        f1_root, f1_rooted, f1_rec, f1_scaled = sem("f1_root"), sem("f1_rooted"), sem("f1_rec"), sem("f1_scaled")
        with nc.Block() as block:
            @block.sync
            def _(sp):
                sp.dma_start(lin.rearrange("p (h o) -> p h o", h=H1), L1_lW.rearrange("(h c) o -> c h o", h=H1)).then_inc(f1_in, 16)
                with nc.allow_non_contiguous_dma("three columns"):
                    sp.dma_start(gb_col.unsqueeze(2), L1_gb.rearrange("(h c) -> c h", h=H1).unsqueeze(2)).then_inc(f1_in, 16)
                sp.wait_ge(f1_wt, 1)
                for row, v in ((g_bc, L1_g), (b_bc, L1_b), (lb_bc, L1_lb)):
                    sp.dma_start(row, v.unsqueeze(0).broadcast_to([P, D])).then_inc(f1_late, 16)
                sp.wait_ge(f1_late, 48)

            @block.vector
            def _(dve):
                none, den = small[:, 0, :], small[:, 1, :]
                link(dve, dve.tensor_scalar(none, deg[:], 0.0, None, ALU.is_equal))
                for k in range(H1):
                    wl, rec = small[:, 3 + k, :], small[:, 9 + k, :]
                    link(dve, dve.tensor_tensor(wl, acc[:, :, H1 * D + H1 + k], none, ALU.add))
                    link(dve, dve.tensor_tensor(den, acc[:, :, H1 * D + k], wl, ALU.add))
                    link(dve, dve.reciprocal(rec, den))
                    dve.tensor_tensor(wl, wl, rec, ALU.mult).then_inc(f1_rec, 1)
                dve.wait_ge(f1_wt, 1)
                dve.tensor_copy(whT, ps[:, 7, 0:384])
                dve.wait_ge(f1_in, 32)
                dve.tensor_copy(gb_wide.rearrange("p (h m) -> p h m", h=H1), gb_col.unsqueeze(2).broadcast_to([P, H1, P])).then_inc(f1_wk, 1)
                dve.wait_ge(f1_v, 1)
                dve.tensor_copy(V, ps[:, 6, 0:384])
                dve.wait_ge(f1_late, 48)
                dve.tensor_tensor(bias_row[:], lb_bc, ps[:, 5, 0:D], ALU.add).then_inc(f1_vk, 1)
                dve.wait_ge(f1_vk, 1)
                dve.wait_ge(f1_rec, H1)

                def add_product(b):
                    dve.wait_ge(f1_y, b + 1)
                    dve.wait_ge(f1_mean, b + 1)
                    dve.tensor_tensor(hs[:, b, :], hs[:, b, :], ps[:, 2 + b % 2, 0:D], ALU.add).then_inc(f1_used, 1)

                LAG = 3
                for b in range(NB):
                    dve.wait_ge(f1_scaled, b + 1)
                    for k in range(H1):
                        mean = acc[:, b, k * D:(k + 1) * D]
                        dve.scalar_tensor_tensor(out=mean, in0=hs[:, b, :], scalar=small[:, 3 + k, b:b + 1], in1=mean,
                                                 op0=ALU.mult, op1=ALU.add)
                    dve.tensor_tensor(hs[:, b, :], hs[:, b, :], bias_row[:], ALU.add).then_inc(f1_mean, 1)
                    if b >= LAG:
                        add_product(b - LAG)
                for b in range(NB - LAG, NB):
                    add_product(b)
                dve.wait_ge(f1_used, NB)
                node_stats(dve, hs)
                standardise(dve, (f1_root, f1_rooted), hs)
                link(dve, dve.tensor_tensor(hs[:], hs[:], per_feature(g_bc), ALU.mult))
                link(dve, dve.tensor_tensor(hs[:], hs[:], per_feature(b_bc), ALU.add))
                dve.tensor_tensor(xs[:], xs[:], hs[:], ALU.add)

            @block.scalar
            def _(act):
                def keep(b):
                    act.wait_ge(f1_turned, b + 1)
                    if b >= 2:
                        act.wait_ge(f1_y, b - 1)
                    act.copy(aggT[:, (b % 2) * 384:(b % 2 + 1) * 384], ps[:, b % 2, 0:384]).then_inc(f1_kept, 1)

                LEAD = 4
                act.wait_ge(f1_rec, H1)
                for b in range(NB):
                    for k in range(H1):
                        mean = acc[:, b, k * D:(k + 1) * D]
                        last = act.activation(mean, mean, ACT.Copy, scale=small[:, 9 + k, b:b + 1])
                    last.then_inc(f1_scaled, 1)
                    if b >= LEAD:
                        keep(b - LEAD)
                for b in range(NB - LEAD, NB):
                    keep(b)
                std_root(act, f1_root, f1_rooted)

            @block.tensor
            def _(pe):
                for k in range(H1):
                    mm = pe.transpose(ps[:, 7, k * P:(k + 1) * P], wnat[:, k * P:(k + 1) * P], ident[:])
                mm.then_inc(f1_wt, 1)
                pe.wait_ge(f1_wk, 1)
                for k in range(H1):
                    pe.matmul(ps[:, 6, k * P:(k + 1) * P], whT[:, k * P:(k + 1) * P], lin[:, k * P:(k + 1) * P], start=True, stop=True)
                for k in range(H1):
                    mm = pe.matmul(ps[:, 5, 0:P], gb_wide[:, k * P:(k + 1) * P], lin[:, k * P:(k + 1) * P], start=(k == 0), stop=(k == H1 - 1))
                mm.then_inc(f1_v, 1)
                pe.wait_ge(f1_vk, 1)

                def turn(b):
                    pe.wait_ge(f1_mean, b + 1)
                    if b >= 2:
                        pe.wait_ge(f1_kept, b - 1)
                    for k in range(H1):
                        mm = pe.transpose(ps[:, b % 2, k * P:(k + 1) * P], acc[:, b, k * P:(k + 1) * P], ident[:])
                    mm.then_inc(f1_turned, 1)

                turn(0)
                for b in range(NB):
                    if b + 1 < NB:
                        turn(b + 1)
                    pe.wait_ge(f1_kept, b + 1)
                    if b >= 2:
                        pe.wait_ge(f1_used, b - 1)
                    for k in range(H1):
                        mm = pe.matmul(ps[:, 2 + b % 2, 0:P], aggT[:, (b % 2) * 384 + k * P:(b % 2) * 384 + (k + 1) * P], V[:, k * P:(k + 1) * P],
                                       start=(k == 0), stop=(k == H1 - 1))
                    mm.then_inc(f1_y, 1)

        end_layer()
        open_rows(2)

        Wd = wbuf[:, 1144:1152]
        bd_bc = bias_row[:, 0:K2]
        coef2 = scal[:, :, :].rearrange("p k b -> p (k b)")[:, 0:NB * K2].rearrange("p (b k) -> p b k", k=K2)
        dis = small[:, 8, :]
        a2_in, a2_root, a2_rooted, a2_norm = sem("a2_in"), sem("a2_root"), sem("a2_rooted"), sem("a2_norm")
        a2_turned, a2_kept, a2_done, a2_table = sem("a2_turned"), sem("a2_kept"), sem("a2_done"), sem("a2_table")
        a2_shift, a2_exp, a2_scaled = sem("a2_shift"), sem("a2_exp"), sem("a2_scaled")
        with nc.Block() as block:
            @block.sync
            def _(sp):
                sp.dma_start(Wd, L2_Wd).then_inc(a2_in, 16)
                sp.dma_start(bd_bc, L2_bd.unsqueeze(0).broadcast_to([P, K2])).then_inc(a2_in, 16)
                write_table(sp, 2, hs[:], (a2_scaled, 1), a2_table)

            @block.vector
            def _(dve):
                node_stats(dve, xs)
                standardise(dve, (a2_root, a2_rooted), xs, relu_done=a2_norm)
                dve.tensor_scalar(dis, deg[:], 1.0, None, ALU.add)
                dve.wait_ge(a2_in, 32)
                dve.wait_ge(a2_done, 1)
                got = ps[:, 2, 0:NB * K2].rearrange("p (b k) -> p b k", k=K2)
                link(dve, dve.tensor_tensor(coef2, got, bd_bc.unsqueeze(1).broadcast_to([P, NB, K2]), ALU.add))
                link(dve, dve.tensor_reduce(small[:, 3, :], coef2, AX.X, ALU.max))
                link(dve, dve.tensor_tensor(coef2, coef2, small[:, 3, :].unsqueeze(2).broadcast_to([P, NB, K2]), ALU.subtract))
                dve.sem_inc(a2_shift, 1)
                dve.wait_ge(a2_exp, 2)
                link(dve, dve.tensor_reduce(small[:, 4, :], coef2, AX.X, ALU.add))
                link(dve, dve.reciprocal(small[:, 5, :], small[:, 4, :]))
                link(dve, dve.reciprocal(dis, dis))
                dve.tensor_tensor(coef2, coef2, small[:, 5, :].unsqueeze(2).broadcast_to([P, NB, K2]), ALU.mult)
                dve.tensor_tensor(hs[:], hs[:], per_node(dis), ALU.mult).then_inc(a2_scaled, 1)

            @block.scalar
            def _(act):
                std_root(act, a2_root, a2_rooted)
                keep_blocks(act, hT, a2_turned, a2_kept)
                act.wait_ge(a2_shift, 1)
                act.activation(dis, dis, ACT.Sqrt).then_inc(a2_exp, 1)
                act.activation(coef2, coef2, ACT.Exp).then_inc(a2_exp, 1)

            @block.tensor
            def _(pe):
                pe.wait_ge(a2_in, 32)
                turn_blocks(pe, hs, a2_norm, a2_turned, a2_kept)
                node_products(pe, hT, Wd, K2, (a2_kept, TG), a2_done, per_bank=NB)

        acc = row_pass(2, D)

        W2 = wbuf[:, 0:K2 * D]
        b2_bc = A3[:, 0:K2 * D]
        SLOTS2 = 3
        biased = A3[:, K2 * D:(1 + SLOTS2) * K2 * D].rearrange("p (i z) -> p i z", i=SLOTS2)
        scaled = gath_flat[:, 0:SLOTS2 * K2 * D].rearrange("p (i z) -> p i z", i=SLOTS2)
        aT = A2[:, 0:NP].rearrange("p (b f) -> p b f", f=D)
        f2_in, f2_agg, f2_turned, f2_kept = sem("f2_in"), sem("f2_agg"), sem("f2_turned"), sem("f2_kept")
        f2_mul, f2_biased, f2_scaled, f2_sum = sem("f2_mul"), sem("f2_biased"), sem("f2_scaled"), sem("f2_sum")
        with nc.Block() as block:
            @block.sync
            def _(sp):
                sp.dma_start(W2.rearrange("p (k o) -> p k o", k=K2), L2_W.rearrange("k i o -> i k o")).then_inc(f2_in, 16)
                sp.dma_start(b2_bc, L2_b.rearrange("k o -> (k o)").unsqueeze(0).broadcast_to([P, K2 * D])).then_inc(f2_in, 16)
                sp.wait_ge(f2_in, 32)

            @block.vector
            def _(dve):
                for g in range(TG + 1):
                    if g < TG:
                        bs = slice(4 * g, min(4 * g + 4, NB))
                        dve_count[0] += 1
                        dve.tensor_tensor(acc[:, bs, :], acc[:, bs, :], hs[:, bs, :], ALU.add).then_inc(dve_chain, 1)
                    if g:
                        bs = slice(4 * g - 4, min(4 * g, NB))
                        dve.wait_ge(dve_chain, dve_count[0] - (1 if g < TG else 0))
                        dve.tensor_tensor(acc[:, bs, :], acc[:, bs, :], dis[:, bs].unsqueeze(2).broadcast_to([P, bs.stop - bs.start, D]),
                                          ALU.mult).then_inc(f2_agg, 1)
                dve.wait_ge(f2_in, 32)

                def reduce(b):
                    dve.wait_ge(f2_scaled, b + 1)
                    link(dve, dve.tensor_reduce(hs[:, b, :], scaled[:, b % SLOTS2, :].rearrange("p (k o) -> p o k", k=K2), AX.X, ALU.add))
                    dve.tensor_tensor(xs[:, b, :], xs[:, b, :], hs[:, b, :], ALU.add).then_inc(f2_sum, 1)

                for b in range(NB):
                    dve.wait_ge(f2_mul, b + 1)
                    if b >= SLOTS2:
                        dve.wait_ge(f2_scaled, b + 1 - SLOTS2)
                    dve.tensor_tensor(biased[:, b % SLOTS2, :].rearrange("p (i z) -> p i z", i=2), ps[:, 2 + 2 * (b % SLOTS2):4 + 2 * (b % SLOTS2), :],
                                      b2_bc.rearrange("p (i z) -> p i z", i=2), ALU.add).then_inc(f2_biased, 1)
                    if b >= 2:
                        reduce(b - 2)
                reduce(NB - 2)
                reduce(NB - 1)

            @block.scalar
            def _(act):
                keep_blocks(act, aT, f2_turned, f2_kept)
                for b in range(NB):
                    act.wait_ge(f2_biased, b + 1)
                    if b >= SLOTS2:
                        act.wait_ge(f2_sum, b + 1 - SLOTS2)
                    for k in range(K2):
                        last = act.activation(scaled[:, b % SLOTS2, k * D:(k + 1) * D], biased[:, b % SLOTS2, k * D:(k + 1) * D], ACT.Relu,
                                              scale=coef2[:, b, k:k + 1])
                    last.then_inc(f2_scaled, 1)

            @block.tensor
            def _(pe):
                turn_blocks(pe, acc, f2_agg, f2_turned, f2_kept)
                pe.wait_ge(f2_in, 32)
                for b in range(NB):
                    pe.wait_ge(f2_kept, b // 4 + 1)
                    if b >= SLOTS2:
                        pe.wait_ge(f2_biased, b + 1 - SLOTS2)
                    for i in range(2):
                        mm = pe.matmul(ps[:, 2 + 2 * (b % SLOTS2) + i, :], aT[:, b, :], W2[:, i * 512:(i + 1) * 512], start=True, stop=True)
                    mm.then_inc(f2_mul, 1)

        end_layer()
        open_rows(3)

        att3 = wnat[:, 0:2 * D]
        Wp, Wsk = wbuf[:, 0:D], wbuf[:, D:2 * D]
        a3_in, a3_root, a3_rooted, a3_norm = sem("a3_in"), sem("a3_root"), sem("a3_rooted"), sem("a3_norm")
        a3_turned, a3_kept, a3_done, a3_used = sem("a3_turned"), sem("a3_kept"), sem("a3_done"), sem("a3_used")
        a3_seed, a3_seeded, a3_table = sem("a3_seed"), sem("a3_seeded"), sem("a3_table")
        with nc.Block() as block:
            @block.sync
            def _(sp):
                sp.dma_start(Wp, L3_Wp).then_inc(a3_in, 16)
                sp.dma_start(Wsk, L3_Ws).then_inc(a3_in, 16)
                sp.dma_start(att3[:, 0:D], L3_as.rearrange("o h c -> o (h c)").broadcast_to([P, D])).then_inc(a3_in, 16)
                sp.dma_start(att3[:, D:2 * D], L3_at.rearrange("o h c -> o (h c)").broadcast_to([P, D])).then_inc(a3_in, 16)
                write_table(sp, 3, tab, (a3_seed, 1), a3_table)

            @block.gpsimd
            def _(pool):
                pool.wait_ge(a3_seed, 1)
                scatter_seeds(pool, a3_seeded)

            @block.vector
            def _(dve):
                node_stats(dve, xs)
                standardise(dve, (a3_root, a3_rooted), xs, relu_done=a3_norm)
                for g in range(TG):
                    bs, got = bank_squares(g)
                    dve.wait_ge(a3_done, g + 1)
                    dve.tensor_copy(hW[:, bs, :], got).then_inc(a3_used, 1)
                dve.wait_ge(a3_used, TG)
                dve.wait_ge(a3_in, 64)
                by_head = tmp.rearrange("p b (k c) -> p b k c", c=C3)
                link(dve, dve.tensor_tensor(tmp, hW, per_feature(att3[:, 0:D]), ALU.mult))
                link(dve, dve.tensor_reduce(tab[:, :, D:D + H3], by_head, AX.X, ALU.add))
                link(dve, dve.tensor_tensor(tmp, hW, per_feature(att3[:, D:2 * D]), ALU.mult))
                dve.tensor_reduce(seed_vals, by_head, AX.X, ALU.add).then_inc(a3_seed, 1)

            @block.scalar
            def _(act):
                std_root(act, a3_root, a3_rooted)
                keep_blocks(act, hT, a3_turned, a3_kept)

            @block.tensor
            def _(pe):
                turn_blocks(pe, hs, a3_norm, a3_turned, a3_kept)
                pe.wait_ge(a3_in, 64)
                wide_products(pe, hT, Wp, a3_kept, a3_done, a3_used)

        db3_in = sem("db3_in")
        with nc.Block() as block:
            @block.gpsimd
            def _(pool):
                first_rows(pool, 3, 0, AHEAD[3][0])

            @block.sync
            def _(sp):
                sp.dma_start(A3[:, 0:EC * KW], seeds_edges.rearrange("(p c) k -> p (c k)", p=P)).then_inc(db3_in, 16)
                sp.wait_ge(db3_in, 16)
        copy_down(3, H3)
        edge_no = A1[:, 0:EC]
        w3_iota = sem("w3_iota")
        with nc.Block() as block:
            @block.gpsimd
            def _(pool):
                pool.iota(edge_no, [[1, EC]], base=0, channel_multiplier=EC, allow_small_or_imprecise_dtypes=True).then_inc(w3_iota, 1)
                first_rows(pool, 3, AHEAD[3][1], AHEAD[3][2])

            @block.vector
            def _(dve):
                dve.wait_ge(w3_iota, 1)
                link(dve, dve.tensor_scalar(scan_tmp[:], edge_no, float(E), -BIG, ALU.is_ge, ALU.mult))
                dve.tensor_tensor(SE, DB, scan_tmp[:].unsqueeze(2).broadcast_to([P, EC, KW]), ALU.add)

        to_steps(3, H3)
        acc = row_pass(3, D + H3)

        hT3 = A2[:, 0:NP].rearrange("p (b f) -> p b f", f=D)
        z = A3[:, 0:NP].rearrange("p (b f) -> p b f", f=D)
        f3_start, f3_turned, f3_kept, f3_done, f3_used = sem("f3_start"), sem("f3_turned"), sem("f3_kept"), sem("f3_done"), sem("f3_used")
        f3_low, f3_exp, f3_x, f3_out = sem("f3_low"), sem("f3_exp"), sem("f3_x"), sem("f3_out")
        with nc.Block() as block:
            @block.vector
            def _(dve):
                den = scal[:, 0:H3, :].rearrange("p k b -> p (k b)").rearrange("p (b k) -> p b k", k=H3)
                rec = scal[:, H3:2 * H3, :].rearrange("p k b -> p (k b)").rearrange("p (b k) -> p b k", k=H3)
                dve.memset(small[:, 0, 0:1], 0.0).then_inc(f3_start, 1)
                link(dve, dve.tensor_scalar(den, acc[:, :, D:D + H3], 1e-16, None, ALU.add))
                link(dve, dve.reciprocal(rec, den))
                link(dve, dve.tensor_tensor(z.rearrange("p b (k c) -> p b k c", c=C3), acc[:, :, 0:D].rearrange("p b (k c) -> p b k c", c=C3),
                                            rec.unsqueeze(3).broadcast_to([P, NB, H3, C3]), ALU.mult))
                for g in range(TG):
                    bs, got = bank_squares(g)
                    dve.wait_ge(f3_done, g + 1)
                    dve.tensor_tensor(z[:, bs, :], z[:, bs, :], got, ALU.add).then_inc(f3_used, 1)
                dve.wait_ge(f3_used, TG)
                dve.tensor_scalar(tmp, z, 0.0, None, ALU.min).then_inc(f3_low, 1)
                link(dve, dve.scalar_tensor_tensor(out=xs[:], in0=z, scalar=0.0, in1=xs[:], op0=ALU.max, op1=ALU.add))
                dve.wait_ge(f3_exp, 1)
                dve.scalar_tensor_tensor(out=xs[:], in0=tmp, scalar=-1.0, in1=xs[:], op0=ALU.add, op1=ALU.add).then_inc(f3_x, 1)

            @block.scalar
            def _(act):
                keep_blocks(act, hT3, f3_turned, f3_kept)
                act.wait_ge(f3_low, 1)
                act.activation(tmp, tmp, ACT.Exp).then_inc(f3_exp, 1)

            @block.tensor
            def _(pe):
                turn_blocks(pe, hs, f3_start, f3_turned, f3_kept, whole=True)
                wide_products(pe, hT3, Wsk, f3_kept, f3_done, f3_used)

            @block.sync
            def _(sp):
                sp.wait_ge(f3_x, 1)
                sp.dma_start(out[0:(NB - 1) * P, :].rearrange("(b p) f -> p b f", p=P), xs[:, 0:NB - 1, :]).then_inc(f3_out, 16)
                sp.dma_start(out[(NB - 1) * P:N, :], xs[0:TAIL, NB - 1, :]).then_inc(f3_out, 16)
                sp.wait_ge(f3_out, 32)


_INS = ['x', 'src', 'dst', 'edge_attr_16', 'L0_gnn_biclique_mask', 'L0_gnn_W', 'L0_gnn_attn', 'L1_gnn_W', 'L1_gnn_W_edge',
        'L1_gnn_att_src', 'L1_gnn_att_dst', 'L1_gnn_att_edge', 'L1_gnn_gat_bias', 'L1_gnn_lin_W', 'L1_gnn_lin_b', 'L1_gnn_ln_g',
        'L1_gnn_ln_b', 'L2_gnn_W', 'L2_gnn_b', 'L2_gnn_W_dict', 'L2_gnn_b_dict', 'L3_gnn_W_proj', 'L3_gnn_W_skip', 'L3_gnn_a_src',
        'L3_gnn_a_tgt']
_OUTS = [((N, D), 'float32')]


def kernel(**inputs):
    import numpy as _np
    import concourse.bacc as _bacc
    from concourse import mybir as _mybir
    from concourse.bass_utils import run_bass_kernel_spmd as _run

    nc = _bacc.Bacc("TRN2", target_bir_lowering=False, num_devices=1)
    arrays, args = {}, []
    for name in _INS:
        a = _np.ascontiguousarray(inputs[name])
        arrays[f"in_{name}_dram"] = a
        args.append(nc.dram_tensor(f"in_{name}_dram", a.shape, _mybir.dt.from_np(a.dtype), kind="ExternalInput").ap())
    for i, (shape, dtype) in enumerate(_OUTS):
        dt = _mybir.dt.from_np(_np.dtype(dtype))
        args.append(nc.dram_tensor(f"out_{i}_dram", shape, dt, kind="ExternalOutput").ap())
    build_gnn(nc, *args)
    r = _run(nc, [arrays], core_ids=[0])
    got = tuple(r.results[0][f"out_{i}_dram"] for i in range(len(_OUTS)))
    return got[0]
```
